# Optimizing a Trainium2 kernel written in Bass

```python
import numpy as np
import jax
import jax.numpy as jnp

def _softmax(x, axis=-1):
    return jax.nn.softmax(x, axis=axis)

def _gelu(x):
    return jax.nn.gelu(x, approximate=True)

def _silu(x):
    return jax.nn.silu(x)

def _sigmoid(x):
    return jax.nn.sigmoid(x)

def _layernorm(x, axis=-1, eps=1e-05):
    m = jnp.mean(x, axis=axis, keepdims=True)
    v = jnp.var(x, axis=axis, keepdims=True)
    return (x - m) / jnp.sqrt(v + eps)

def _scatter_add(tgt, idx, src, axis=0):
    return tgt.at[idx].add(src)

def _segment_sum(src, seg, n):
    return jax.ops.segment_sum(src, seg, n)
kernel_name = 'mk_seq_preln_d2_jaxref_r8_13ab1d'

def setup_inputs(seed: int=0):
    np.random.seed(seed)
    _w = jnp.asarray

    def _L0_attn_setup():
        import jax, jax.numpy as jnp
        import numpy as np
        B, S, EMB = (2, 256, 512)
        NHEADS, KVHEADS, HEAD_D = (32, 8, 128)
        SPLITS = (NHEADS * HEAD_D, KVHEADS * HEAD_D, KVHEADS * HEAD_D)
        key = jax.random.key(seed)
        k1, k2, k3 = jax.random.split(key, 3)
        q = jax.random.normal(k1, (B, S, EMB), dtype=jnp.float32)
        w_qkv = jax.random.normal(k2, (sum(SPLITS), EMB), dtype=jnp.float32) * 0.02
        w_dense = jax.random.normal(k3, (EMB, NHEADS * HEAD_D), dtype=jnp.float32) * 0.02
        return {'q': q, 'w_qkv': w_qkv, 'w_dense': w_dense}
    _L0_attn_in = _L0_attn_setup()

    def _L0_ffn_setup():
        import jax, jax.numpy as jnp
        import numpy as np
        BATCH, SEQ, D = (2, 256, 512)
        K, TOPK, RANK = (64, 16, 16)
        ALPHA = 32.0
        SCALING = ALPHA / RANK
        key = jax.random.key(seed)
        k1, k2, k3, k4 = jax.random.split(key, 4)
        x = jax.random.normal(k1, (BATCH, SEQ, D), dtype=jnp.float32)
        A = jax.random.normal(k2, (K, RANK, D), dtype=jnp.float32) * 0.02
        B = jax.random.normal(k3, (K, D, RANK), dtype=jnp.float32) * 0.02
        Wr = jax.random.normal(k4, (K, D), dtype=jnp.float32) * 0.02
        return {'x': x, 'A': A, 'B': B, 'Wr': Wr}
    _L0_ffn_in = _L0_ffn_setup()

    def _L1_attn_setup():
        import jax, jax.numpy as jnp
        import numpy as np
        import math
        B, S, DM = (1, 256, 512)
        H, HKV, HD = (32, 8, 128)
        EPS = 1e-06
        NEG_INF = -1e+30

        def _alibi_slopes(n_heads: int) -> np.ndarray:
            start = 2 ** (-2 ** (-(math.log2(n_heads) - 3)))
            return np.array([start * start ** i for i in range(n_heads)], dtype=np.float32)

        def _rmsnorm(t, w):
            tf = t.astype(jnp.float32)
            inv = jax.lax.rsqrt(jnp.mean(tf * tf, axis=-1, keepdims=True) + EPS)
            return (tf * inv * w).astype(t.dtype)
        key = jax.random.key(seed)
        ks = jax.random.split(key, 5)
        std = 0.02
        return {'x': jax.random.normal(ks[0], (B, S, DM), dtype=jnp.float32), 'Wq': jax.random.normal(ks[1], (H * HD, DM), dtype=jnp.float32) * std, 'Wk': jax.random.normal(ks[2], (HKV * HD, DM), dtype=jnp.float32) * std, 'Wv': jax.random.normal(ks[3], (HKV * HD, DM), dtype=jnp.float32) * std, 'Wo': jax.random.normal(ks[4], (H * HD, DM), dtype=jnp.float32).T * (std / math.sqrt(2 * 32)), 'q_norm_w': jnp.ones((HD,), dtype=jnp.float32), 'k_norm_w': jnp.ones((HD,), dtype=jnp.float32)}
    _L1_attn_in = _L1_attn_setup()

    def _L1_ffn_setup():
        import jax, jax.numpy as jnp
        import numpy as np
        BLOCK = 64
        NF4_CODE = jnp.array([-1.0, -0.6961928009986877, -0.5250730514526367, -0.39491748809814453, -0.28444138169288635, -0.18477343022823334, -0.09105003625154495, 0.0, 0.07958029955625534, 0.16093020141124725, 0.24611230194568634, 0.33791524171829224, 0.44070982933044434, 0.5626170039176941, 0.7229568362236023, 1.0], dtype=jnp.float32)

        def dequant_nf4(q, absmax, shape):
            w = NF4_CODE[q.reshape(-1)]
            w = w.reshape(-1, BLOCK) * absmax[:, None]
            return w.reshape(shape)
        key = jax.random.key(seed)
        ks = jax.random.split(key, 7)
        HD, M = (512, 1792)
        nblk = HD * M // BLOCK
        x = jax.random.normal(ks[0], (2, 256, HD), dtype=jnp.float32)
        gate_q = jax.random.randint(ks[1], (M, HD), 0, 16, dtype=jnp.int32)
        up_q = jax.random.randint(ks[2], (M, HD), 0, 16, dtype=jnp.int32)
        down_q = jax.random.randint(ks[3], (HD, M), 0, 16, dtype=jnp.int32)
        gate_absmax = jax.random.uniform(ks[4], (nblk,), dtype=jnp.float32) * 0.05
        up_absmax = jax.random.uniform(ks[5], (nblk,), dtype=jnp.float32) * 0.05
        down_absmax = jax.random.uniform(ks[6], (nblk,), dtype=jnp.float32) * 0.05
        return {'x': x, 'gate_q': gate_q, 'gate_absmax': gate_absmax, 'up_q': up_q, 'up_absmax': up_absmax, 'down_q': down_q, 'down_absmax': down_absmax}
    _L1_ffn_in = _L1_ffn_setup()
    _d = {'L0_attn_q': _L0_attn_in['q'], 'L0_attn_w_qkv': _L0_attn_in['w_qkv'], 'L0_attn_w_dense': _L0_attn_in['w_dense'], 'L0_ffn_A': _L0_ffn_in['A'], 'L0_ffn_B': _L0_ffn_in['B'], 'L0_ffn_Wr': _L0_ffn_in['Wr'], 'L1_attn_Wq': _L1_attn_in['Wq'], 'L1_attn_Wk': _L1_attn_in['Wk'], 'L1_attn_Wv': _L1_attn_in['Wv'], 'L1_attn_Wo': _L1_attn_in['Wo'], 'L1_attn_q_norm_w': _L1_attn_in['q_norm_w'], 'L1_attn_k_norm_w': _L1_attn_in['k_norm_w'], 'L1_ffn_gate_q': _L1_ffn_in['gate_q'], 'L1_ffn_gate_absmax': _L1_ffn_in['gate_absmax'], 'L1_ffn_up_q': _L1_ffn_in['up_q'], 'L1_ffn_up_absmax': _L1_ffn_in['up_absmax'], 'L1_ffn_down_q': _L1_ffn_in['down_q'], 'L1_ffn_down_absmax': _L1_ffn_in['down_absmax']}
    _x0 = _d['L0_attn_q']
    _d['L0_attn_q'] = jax.random.normal(jax.random.fold_in(jax.random.key(seed), 1), (4, 256, 512), dtype=_x0.dtype)
    del _x0
    return _d

def reference(L0_attn_q, L0_attn_w_qkv, L0_attn_w_dense, L0_ffn_A, L0_ffn_B, L0_ffn_Wr, L1_attn_Wq, L1_attn_Wk, L1_attn_Wv, L1_attn_Wo, L1_attn_q_norm_w, L1_attn_k_norm_w, L1_ffn_gate_q, L1_ffn_gate_absmax, L1_ffn_up_q, L1_ffn_up_absmax, L1_ffn_down_q, L1_ffn_down_absmax):

    def _L0_attn_ref(q, w_qkv, w_dense):
        import jax, jax.numpy as jnp
        import numpy as np
        B, S, EMB = (2, 256, 512)
        NHEADS, KVHEADS, HEAD_D = (32, 8, 128)
        SPLITS = (NHEADS * HEAD_D, KVHEADS * HEAD_D, KVHEADS * HEAD_D)
        Bq, Sq, _ = q.shape
        qkv = q @ w_qkv.T
        qs, ks, vs = jnp.split(qkv, np.cumsum(SPLITS)[:-1], axis=-1)
        G = NHEADS // KVHEADS
        qh = qs.reshape(Bq, Sq, KVHEADS, G, HEAD_D)
        kh = ks.reshape(Bq, Sq, KVHEADS, HEAD_D)
        vh = vs.reshape(Bq, Sq, KVHEADS, HEAD_D)
        scale = 1.0 / jnp.sqrt(jnp.float32(HEAD_D))
        scores = jnp.einsum('bskgd,btkd->bkgst', qh, kh) * scale
        causal = jnp.tril(jnp.ones((Sq, Sq), dtype=bool))
        scores = jnp.where(causal, scores, jnp.finfo(scores.dtype).min)
        probs = jax.nn.softmax(scores, axis=-1)
        attn = jnp.einsum('bkgst,btkd->bskgd', probs, vh)
        attn = attn.reshape(Bq, Sq, NHEADS * HEAD_D)
        return attn @ w_dense.T

    def _L0_ffn_ref(x, A, B, Wr):
        import jax, jax.numpy as jnp
        import numpy as np
        BATCH, SEQ, D = (2, 256, 512)
        K, TOPK, RANK = (64, 16, 16)
        ALPHA = 32.0
        SCALING = ALPHA / RANK
        prefix = x.shape[:-1]
        xf = x.reshape(-1, x.shape[-1])
        N = xf.shape[0]
        scores = xf @ Wr.T
        top_vals, top_idx = jax.lax.top_k(scores, TOPK)
        gates = jax.nn.softmax(top_vals, axis=-1)
        G = jnp.zeros((N, K), xf.dtype).at[jnp.arange(N)[:, None], top_idx].set(gates)
        h = jnp.einsum('nd,krd->nkr', xf, A)
        out = jnp.einsum('nkr,kdr->nd', h * G[:, :, None], B)
        return (out * SCALING).reshape(*prefix, -1)

    def _L1_attn_ref(x, Wq, Wk, Wv, Wo, q_norm_w, k_norm_w):
        import jax, jax.numpy as jnp
        import numpy as np
        import math
        B, S, DM = (1, 256, 512)
        H, HKV, HD = (32, 8, 128)
        EPS = 1e-06
        NEG_INF = -1e+30

        def _alibi_slopes(n_heads: int) -> np.ndarray:
            start = 2 ** (-2 ** (-(math.log2(n_heads) - 3)))
            return np.array([start * start ** i for i in range(n_heads)], dtype=np.float32)

        def _rmsnorm(t, w):
            tf = t.astype(jnp.float32)
            inv = jax.lax.rsqrt(jnp.mean(tf * tf, axis=-1, keepdims=True) + EPS)
            return (tf * inv * w).astype(t.dtype)
        b, s, _ = x.shape
        G = H // HKV
        q = (x @ Wq.T).reshape(b, s, H, HD).transpose(0, 2, 1, 3)
        k = (x @ Wk.T).reshape(b, s, HKV, HD).transpose(0, 2, 1, 3)
        v = (x @ Wv.T).reshape(b, s, HKV, HD).transpose(0, 2, 1, 3)
        q = _rmsnorm(q, q_norm_w)
        k = _rmsnorm(k, k_norm_w)
        qg = q.reshape(b, HKV, G, s, HD)
        scores = jnp.einsum('bkgqd,bksd->bkgqs', qg, k) / math.sqrt(HD)
        slopes = jnp.asarray(_alibi_slopes(H)).reshape(HKV, G)
        pos = jnp.arange(s, dtype=jnp.float32)
        rel = pos[None, :] - pos[:, None]
        bias = jnp.where(rel > 0, NEG_INF, slopes[:, :, None, None] * rel)
        attn = jax.nn.softmax(scores + bias[None], axis=-1)
        out = jnp.einsum('bkgqs,bksd->bkgqd', attn, v)
        out = out.reshape(b, H, s, HD).transpose(0, 2, 1, 3).reshape(b, s, H * HD)
        return out @ Wo.T

    def _L1_ffn_ref(x, gate_q, gate_absmax, up_q, up_absmax, down_q, down_absmax):
        import jax, jax.numpy as jnp
        import numpy as np
        BLOCK = 64
        NF4_CODE = jnp.array([-1.0, -0.6961928009986877, -0.5250730514526367, -0.39491748809814453, -0.28444138169288635, -0.18477343022823334, -0.09105003625154495, 0.0, 0.07958029955625534, 0.16093020141124725, 0.24611230194568634, 0.33791524171829224, 0.44070982933044434, 0.5626170039176941, 0.7229568362236023, 1.0], dtype=jnp.float32)

        def dequant_nf4(q, absmax, shape):
            w = NF4_CODE[q.reshape(-1)]
            w = w.reshape(-1, BLOCK) * absmax[:, None]
            return w.reshape(shape)
        HD = x.shape[-1]
        M = gate_q.shape[0]
        Wg = dequant_nf4(gate_q, gate_absmax, (M, HD))
        Wu = dequant_nf4(up_q, up_absmax, (M, HD))
        Wd = dequant_nf4(down_q, down_absmax, (HD, M))
        g = jnp.einsum('bsh,mh->bsm', x, Wg)
        u = jnp.einsum('bsh,mh->bsm', x, Wu)
        h = jax.nn.silu(g) * u
        return jnp.einsum('bsm,hm->bsh', h, Wd)
    x = L0_attn_q
    x = x + _L0_attn_ref(_layernorm(x, axis=-1), L0_attn_w_qkv, L0_attn_w_dense)
    x = x + _L0_ffn_ref(_layernorm(x, axis=-1), L0_ffn_A, L0_ffn_B, L0_ffn_Wr)
    x = x + _L1_attn_ref(_layernorm(x, axis=-1), L1_attn_Wq, L1_attn_Wk, L1_attn_Wv, L1_attn_Wo, L1_attn_q_norm_w, L1_attn_k_norm_w)
    x = x + _L1_ffn_ref(_layernorm(x, axis=-1), L1_ffn_gate_q, L1_ffn_gate_absmax, L1_ffn_up_q, L1_ffn_up_absmax, L1_ffn_down_q, L1_ffn_down_absmax)
    return x

_drawn_inputs = setup_inputs


def setup_inputs(seed=0):
    import zlib

    import numpy as np

    out = dict(_drawn_inputs(seed))
    spreads = {'L1_attn_q_norm_w': (1.0, 0.6), 'L1_attn_k_norm_w': (1.0, 0.6)}
    factors = {'L0_ffn_A': 2.712,
     'L0_ffn_Wr': 2.861,
     'L1_attn_Wq': 3.043,
     'L1_attn_Wk': 3.046,
     'L1_ffn_gate_absmax': 3.015,
     'L1_ffn_up_absmax': 3.034,
     'L1_ffn_down_absmax': 3.04}
    for name, (base, spread) in spreads.items():
        noise = np.random.default_rng([zlib.crc32(name.encode()), seed]).standard_normal(out[name].shape)
        drawn = base * np.exp(spread * noise) if base else spread * noise
        out[name] = jnp.asarray(drawn.astype(out[name].dtype))
    for name, factor in factors.items():
        out[name] = (out[name] * factor).astype(out[name].dtype)
    return out
```

```python
import numpy as np

import concourse.bass as bass
from concourse import mybir
from contextlib import ExitStack

F32 = mybir.dt.float32
F32R = mybir.dt.float32r
I32 = mybir.dt.int32
ALU = mybir.AluOpType
ACT = mybir.ActivationFunctionType
AX = mybir.AxisListType

P = 128
BATCH, SEQ, D = 4, 256, 512
TOK = BATCH * SEQ
NT = TOK // P
DC = D // P
HALF = 512
GROUPS, HEADS = 8, 4
HD = 128
EXPERTS, RANK, TOPK = 64, 16, 16
ER = EXPERTS * RANK
EC = ER // P
FF = 1792
MT = FF // P
BLOCK = 64
LN_EPS, RMS_EPS = 1e-5, 1e-6
MASKED = -1e30
TAKEN = -3e38
SCALE = float(np.float32(1.0) / np.sqrt(np.float32(HD)))
LORA_SCALE = 32.0 / RANK
K, Q0, Q1, Q2, Q3, V = range(6)
WT = 6

NF4 = np.array([-1.0, -0.6961928009986877, -0.5250730514526367, -0.39491748809814453,
                -0.28444138169288635, -0.18477343022823334, -0.09105003625154495, 0.0,
                0.07958029955625534, 0.16093020141124725, 0.24611230194568634, 0.33791524171829224,
                0.44070982933044434, 0.5626170039176941, 0.7229568362236023, 1.0], dtype=np.float32)


def nf4_steps():
    steps = []
    for j in range(8):
        low, high = NF4[2 * j], NF4[2 * j + 1]
        step = np.float32(high - low)
        for way in (np.float32(np.inf), np.float32(-np.inf)):
            s = step
            for _ in range(8):
                if np.float32(low + s) == high:
                    break
                s = np.nextafter(s, way)
            if np.float32(low + s) == high:
                break
        assert np.float32(low + s) == high
        steps.append((float(low), float(s)))
    return steps


def alibi_slopes():
    start = 2 ** (-2 ** (-(np.log2(GROUPS * HEADS) - 3)))
    return [float(np.float32(start * start ** i)) for i in range(GROUPS * HEADS)]


def slot_steps(b, rms, projects, first=False):
    half = 0 if b in (1, 2) else 1
    ahead = 0 if b == 0 else 1
    tiles = [K, Q0, Q1] if b in (1, 3) else [Q2, Q3, V]
    if not projects:
        tiles = []
    t = [("tile", x, half, ahead) for x in tiles]
    s = [] if first else [("pt_split",)]
    s += [("scores",), ("stats",), ("exp",)] + t[0:1] + [("normalise",)] + t[1:2]
    if rms and tiles and tiles[0] == K:
        s += [("k_rms", half)]
    s += ([] if first else [("pv",)]) + t[2:3]
    s += [] if first else [("out", 0)]
    if tiles and tiles[-1] == V:
        s += [("v_turn", half)]
    if rms and b in (1, 3) and (projects or b == 1):
        s += [("q_rms_turn", 1 if b == 1 else 0)]
    s += [] if first else [("out", 1)]
    if rms and tiles:
        s += [("q_rms", half, 0 if tiles[0] == K else 1)]
    return s + [("transpose",)]


def lead_steps(rms):
    s = [("tile", x, 0, 0) for x in (K, Q0)] + ([("k_rms", 0)] if rms else [])
    s += [("tile", Q1, 0, 0)] + ([("q_rms", 0, 0)] if rms else [])
    s += [("tile", x, 0, 0) for x in (Q2, Q3, V)] + [("v_turn", 0)]
    s += ([("q_rms", 0, 1), ("q_rms_turn", 0)] if rms else [])
    s += [("tile", x, 1, 0) for x in (K, Q0)] + ([("k_rms", 1)] if rms else [])
    s += [("tile", Q1, 1, 0)] + ([("q_rms", 1, 0)] if rms else [])
    return s


def tail_steps():
    return [("pt_split",), ("pv",), ("out", 0), ("out", 1)]


RING_STEPS = ("tile", "k_rms", "v_turn", "q_rms", "q_rms_turn", "out")


class Tally:

    def __init__(self):
        self.turns, self.n = 0, 0

    def up(self, by=1):
        self.n += by

    def value(self):
        return self.turns + self.n


def turn_loop(eng, count, grows, body):
    with eng.Fori(0, count) as i:
        starts = [t.n for t, _ in grows]
        for t, by in grows:
            t.turns = i * by
        body(i)
    for (t, by), n in zip(grows, starts):
        assert t.n == n + by, (t.n - n, by)
        t.turns, t.n = 0, n + by * count


def build(nc, x_in, w_attn, w_dense, lora_a, lora_wr, lora_b, norm_w, codes, absmax, out):
    with ExitStack() as ctx:
        def sem(name):
            return ctx.enter_context(nc.semaphore(name))

        def sb(name, shape, dt=F32, scope=ctx):
            return scope.enter_context(nc.sbuf_tensor(name, shape, dt))

        def psum(name, shape):
            return ctx.enter_context(nc.psum_tensor(name, shape, F32))

        x = sb("x", [P, NT, D])
        xt_hi = sb("xt_hi", [P, DC, TOK], F32R)
        xt_lo = sb("xt_lo", [P, DC, TOK], F32R)
        ident = sb("ident", [P, P])
        xn = sb("xn", [P, 2, D])
        bn = sb("bn", [P, NT, 6])
        mv = sb("mv", [P, NT, 2])
        var_eps = sb("var_eps", [P, NT])
        rstd = sb("rstd", [P, NT])
        scores1 = psum("scores1", [P, HEADS, SEQ])
        scores0 = psum("scores0", [P, HEADS, P])
        turned = psum("turned", [P, 3, HEADS, P])
        ring = psum("ring", [P, 2, 512])

        s_x = [sem(f"s_x_loaded{t}") for t in range(NT)]
        s_ident = sem("s_ident")
        s_const = sem("s_const")
        s_norm_w = sem("s_norm_w")
        s_ring_full = sem("s_ring_full")
        s_ring_hi = sem("s_ring_hi")
        s_ring_free = sem("s_ring_free")
        s_stat = sem("s_stat")
        s_root = sem("s_root")
        s_xn = sem("s_xn")
        s_scores = sem("s_scores")
        s_max = sem("s_max")
        s_exp = sem("s_exp")
        s_prob = sem("s_prob")
        s_turned = sem("s_turned")
        s_pt_hi = sem("s_pt_hi")
        s_pt_lo = sem("s_pt_lo")
        s_pv = sem("s_pv")
        s_ot_hi = sem("s_ot_hi")
        s_ot_lo = sem("s_ot_lo")
        s_w_raw = [sem(f"s_w_raw{r}") for r in range(3)]
        s_wd_raw = [sem(f"s_wd_raw{r}") for r in range(2)]
        s_w = sem("s_w")
        s_wd = sem("s_wd")
        s_pool = sem("s_pool")
        s_dve = sem("s_dve")
        s_act = sem("s_act")
        s_sq = sem("s_sq")
        s_sq_split = sem("s_sq_split")
        s_root_k = sem("s_root_k")
        s_kn = sem("s_kn")
        s_k_ready = sem("s_k_ready")
        s_root_q = sem("s_root_q")
        s_out = sem("s_out_stored")

        def mm3(o, l_hi, l_lo, r_hi, r_lo, start=True, stop=True):
            nc.tensor.matmul(o, l_lo, r_hi, start=start, stop=False)
            nc.tensor.matmul(o, l_hi, r_lo, start=False, stop=False)
            return nc.tensor.matmul(o, l_hi, r_hi, start=False, stop=stop)

        def as_f32(ap):
            return ap.bitcast(F32)

        pe_ring, act_ring, dve_ring, pool_ring = Tally(), Tally(), Tally(), Tally()
        act_hi, dve_hi, act_chain, dve_chain, pool_chain = Tally(), Tally(), Tally(), Tally(), Tally()
        act_sq, dve_sq, pool_sq, pe_sq = Tally(), Tally(), Tally(), Tally()
        pool_w, sp_w = Tally(), Tally()

        def hold(eng):
            eng.nop(nofuse=True)

        def dve_link(ins):
            ins.then_inc(s_dve, 1)
            dve_chain.up()
            nc.vector.wait_ge(s_dve, dve_chain.value())

        def act_link(ins):
            ins.then_inc(s_act, 1)
            act_chain.up()
            nc.scalar.wait_ge(s_act, act_chain.value())

        def pool_link(ins):
            ins.then_inc(s_pool, 1)
            pool_chain.up()
            nc.gpsimd.wait_ge(s_pool, pool_chain.value())

        def polish_root(y, v, scale=1.0):
            dve_link(nc.vector.tensor_tensor(v, v, y, ALU.mult))
            dve_link(nc.vector.tensor_tensor(v, v, y, ALU.mult))
            dve_link(nc.vector.tensor_scalar(v, v, -0.5 * scale, 1.5 * scale, ALU.mult, ALU.add))
            dve_link(nc.vector.tensor_tensor(y, y, v, ALU.mult))

        def pe_ring_bank(pe):
            bank = pe_ring.n % 2
            if not (isinstance(pe_ring.turns, int) and pe_ring.n < 2):
                pe.wait_ge(s_ring_free, pe_ring.value() - 1)
            return ring[:, bank, :]

        def pe_ring_done(ins):
            ins.then_inc(s_ring_full, 1)
            pe_ring.up()

        def act_ring_tile(act):
            bank = act_ring.n % 2
            act_ring.up()
            act.wait_ge(s_ring_full, act_ring.value())
            return ring[:, bank, :]

        def act_ring_hi(ins):
            ins.then_inc(s_ring_hi, 1)
            act_hi.up()

        def dve_ring_tile(dve, after_hi=False):
            bank = dve_ring.n % 2
            dve_ring.up()
            if after_hi:
                dve_hi.up()
                dve.wait_ge(s_ring_hi, dve_hi.value())
            else:
                dve.wait_ge(s_ring_full, dve_ring.value())
            return ring[:, bank, :]

        def dve_ring_free(ins):
            ins.then_inc(s_ring_free, 1)

        norms = [0, 0]

        def dve_norm(dve, wait_x):
            norms[1] += 1
            for t in range(NT):
                wait_x(t)
                st = nc.vector.bn_stats(bn[:, t, :], x[:, t, :])
            dve_link(st)
            for t in range(NT):
                st = nc.vector.bn_aggr(mv[:, t, :], bn[:, t, :])
            dve_link(st)
            nc.vector.tensor_scalar(var_eps[:, :], mv[:, :, 1], LN_EPS, None, ALU.add).then_inc(s_stat, 1)
            dve.wait_ge(s_stat, norms[1])
            dve.wait_ge(s_root, norms[1])
            polish_root(rstd[:, :], var_eps[:, :])

            def normed(t):
                nc.vector.tensor_scalar(xn[:, t % 2, :], x[:, t, :], mv[:, t, 0:1], rstd[:, t:t + 1],
                                        ALU.subtract, ALU.mult).then_inc(s_xn, 1)

            normed(0)
            normed(1)
            for t in range(NT):
                tile = dve_ring_tile(dve, after_hi=True)
                at = slice(t * P, (t + 1) * P)
                dve_ring_free(nc.vector.tensor_tensor(
                    xt_lo[:, :, at], tile.rearrange("p (c q) -> p c q", c=DC), as_f32(xt_hi[:, :, at]),
                    ALU.subtract))
                if t + 2 < NT:
                    normed(t + 2)

        def act_norm(act):
            norms[0] += 1
            act.wait_ge(s_stat, norms[0])
            act_link(nc.scalar.activation(rstd[:, :], var_eps[:, :], ACT.Ln))
            nc.scalar.activation(rstd[:, :], rstd[:, :], ACT.Exp, scale=-0.5).then_inc(s_root, 1)
            for t in range(NT):
                tile = act_ring_tile(act)
                act_ring_hi(nc.scalar.copy(xt_hi[:, :, t * P:(t + 1) * P],
                                           tile.rearrange("p (c q) -> p c q", c=DC)))

        def pe_turn_normed(pe, t_xn, buf):
            tile = pe_ring_bank(pe)
            pe.wait_ge(s_xn, t_xn)
            for c in range(DC):
                ins = nc.tensor.transpose(tile[:, c * P:(c + 1) * P], buf[:, c * P:(c + 1) * P], ident[:, :])
            pe_ring_done(ins)

        def pe_norm(pe, before):
            for t in range(NT):
                pe_turn_normed(pe, before + t + 1, xn[:, t % 2, :])

        w_raw = sb("w_raw", [P, 3, DC * P])
        w_hi = sb("w_hi", [P, WT, DC, P], F32R)
        w_lo = sb("w_lo", [P, WT, DC, P], F32R)
        wd_raw = sb("wd_raw", [P, 2, D])
        wd_hi = sb("wd_hi", [P, HEADS, D], F32R)
        wd_lo = sb("wd_lo", [P, HEADS, D], F32R)
        tri = sb("tri", [P, P])
        ones_r = sb("ones_r", [P, P], F32R)
        pick = sb("pick", [P, 2 * P], F32R)
        rel = sb("rel", [P, SEQ + P])
        slopes = sb("slopes", [P, GROUPS * HEADS])
        norm_cols = sb("norm_cols", [P, 3])
        RING_TURN = [2 * WT + 2 + 2 * BATCH, 2 * WT + 2 + 2 * BATCH + 2 + 4 + 2]

        def split_steps(pool, dst_hi, dst_lo, src, sem_done):
            hold(nc.gpsimd)
            pool_link(nc.gpsimd.tensor_scalar(dst_hi, src, 1.0, 0.0, ALU.mult, ALU.add))
            nc.gpsimd.tensor_tensor(dst_lo, src, as_f32(dst_hi), ALU.subtract).then_inc(sem_done, 1)

        wd_done = Tally()

        def attention(layer, scope):
            rms = layer == 1
            ring_turn = RING_TURN[layer]
            S0 = 32 * layer

            qt_hi = sb(f"qt_hi{layer}", [P, HEADS, TOK], F32R, scope)
            qt_lo = sb(f"qt_lo{layer}", [P, HEADS, TOK], F32R, scope)
            qt_f = sb(f"qt_f{layer}", [P, HEADS, BATCH, P], F32, scope)
            kt_hi = sb(f"kt_hi{layer}", [P, TOK], F32R, scope)
            kt_lo = sb(f"kt_lo{layer}", [P, TOK], F32R, scope)
            kt_f = sb(f"kt_f{layer}", [P, BATCH, P], F32, scope)
            v_hi = sb(f"v_hi{layer}", [P, NT, HD], F32R, scope)
            v_lo = sb(f"v_lo{layer}", [P, NT, HD], F32R, scope)
            vt = sb(f"vt{layer}", [P, HALF], F32, scope)
            p0 = sb(f"p0{layer}", [P, HEADS, P], F32, scope)
            p1 = sb(f"p1{layer}", [P, HEADS, SEQ], F32, scope)
            pt_hi = sb(f"pt_hi{layer}", [P, 3, HEADS, P], F32R, scope)
            pt_lo = sb(f"pt_lo{layer}", [P, 3, HEADS, P], F32R, scope)
            ot_hi = sb(f"ot_hi{layer}", [P, 2, HEADS, P], F32R, scope)
            ot_lo = sb(f"ot_lo{layer}", [P, 2, HEADS, P], F32R, scope)
            negmax = sb(f"negmax{layer}", [P, 2, HEADS], F32, scope)
            bias = sb(f"bias{layer}", [P, 2, HEADS], F32, scope)
            sums = sb(f"sums{layer}", [P, 2, HEADS], F32, scope)
            rsum = sb(f"rsum{layer}", [P, 2, HEADS], F32, scope)
            if rms:
                sq = sb("sq", [P, HALF], F32, scope)
                sq_hi = sb("sq_hi", [P, 2, HALF], F32R, scope)
                sq_lo = sb("sq_lo", [P, 2, HALF], F32R, scope)
                k_raw = sb("k_raw", [P, HALF], F32, scope)
                k_root = sb("k_root", [P, HALF], F32, scope)
                k_ms = xn[:, 0, :]
                qss = xn[:, 1, :]
                q_ms = sb("q_ms", [P, HALF // P * HEADS], F32, scope)
                q_slope = sb("q_slope", [P, 2, HALF // P * HEADS], F32, scope)
                q_root = sb("q_root", [P, 2, HALF // P * HEADS], F32, scope)
            p1v = p1[:, :, :]

            def q_slot(b, k):
                return slice(b * SEQ + k * P, b * SEQ + (k + 1) * P)

            v_at = [0]

            def pe_steps(pe, steps, g, b):
                n = None if b is None else S0 + 4 * g + b
                for step in steps:
                    if step[0] == "tile":
                        _, X, half, ahead = step
                        tile = pe_ring_bank(pe)
                        if half == 0:
                            pe.wait_ge(s_w, WT * (GROUPS * layer + g + ahead) + X + 1)
                        cols = slice(half * HALF, (half + 1) * HALF)
                        for c in range(DC):
                            ins = mm3(tile, w_hi[:, X, c, :], w_lo[:, X, c, :], xt_hi[:, c, cols],
                                      xt_lo[:, c, cols], start=c == 0, stop=c == DC - 1)
                        pe_ring_done(ins)
                        if X == V:
                            v_at[0] = pe_ring.n
                    elif step[0] == "scores":
                        if not isinstance(n, int) or n > S0:
                            pe.wait_ge(s_exp, 2 * n)
                        if b % 2 == 0 and rms:
                            pe.wait_ge(s_k_ready, 2 * g + b // 2 + 1)
                        for h in range(HEADS):
                            ins = nc.tensor.matmul(scores0[:, h, :], qt_f[:, h, b, :], kt_f[:, b, :],
                                                   start=True, stop=True)
                        keys = slice(b * SEQ, (b + 1) * SEQ)
                        for h in range(HEADS):
                            ins = mm3(scores1[:, h, :], qt_hi[:, h, q_slot(b, 1)], qt_lo[:, h, q_slot(b, 1)],
                                      kt_hi[:, keys], kt_lo[:, keys])
                        ins.then_inc(s_scores, 1)
                    elif step[0] == "pv":
                        pb = (b - 1) % 4
                        pe.wait_ge(s_pt_lo, 3 * n)
                        v0, v1 = 2 * pb, 2 * pb + 1
                        mm3(turned[:, 0, :, :], v_hi[:, v0, :], v_lo[:, v0, :], pt_hi[:, 0, :, :],
                            pt_lo[:, 0, :, :]).then_inc(s_pv, 1)
                        mm3(turned[:, 1, :, :], v_hi[:, v0, :], v_lo[:, v0, :], pt_hi[:, 1, :, :],
                            pt_lo[:, 1, :, :], stop=False)
                        mm3(turned[:, 1, :, :], v_hi[:, v1, :], v_lo[:, v1, :], pt_hi[:, 2, :, :],
                            pt_lo[:, 2, :, :], start=False).then_inc(s_pv, 1)
                    elif step[0] == "out":
                        k = step[1]
                        tile = pe_ring_bank(pe)
                        pe.wait_ge(s_ot_lo, 2 * (n - 1) + k + 1)
                        if k == 0 and b == 1:
                            pe.wait_ge(s_wd, HEADS * (GROUPS * layer + g + 1))
                        for h in range(HEADS):
                            ins = mm3(tile, ot_hi[:, k, h, :], ot_lo[:, k, h, :], wd_hi[:, h, :],
                                      wd_lo[:, h, :], start=h == 0, stop=h == HEADS - 1)
                        pe_ring_done(ins)
                    elif step[0] == "v_turn":
                        tile = pe_ring_bank(pe)
                        pe.wait_ge(s_ring_free, pe_ring.turns + v_at[0])
                        for q in range(HALF // P):
                            ins = nc.tensor.transpose(tile[:, q * P:(q + 1) * P], vt[:, q * P:(q + 1) * P],
                                                      ident[:, :])
                        pe_ring_done(ins)
                    elif step[0] == "k_rms":
                        tile = pe_ring_bank(pe)
                        pe.wait_ge(s_sq_split, pe_sq.value() + 1)
                        nc.tensor.matmul(tile, ones_r[:, :], sq_lo[:, step[1], :], start=True, stop=False)
                        pe_ring_done(nc.tensor.matmul(tile, ones_r[:, :], sq_hi[:, step[1], :],
                                                      start=False, stop=True))
                    elif step[0] == "q_rms":
                        _, half, pair = step
                        tile = pe_ring_bank(pe)
                        pe_sq.up(3 if pair == 0 else 2)
                        pe.wait_ge(s_sq_split, pe_sq.value())
                        for j in range(2):
                            h = 2 * pair + j
                            part = (half + 1 + h) % 2
                            row = pick[:, P - h:2 * P - h]
                            nc.tensor.matmul(tile, row, sq_lo[:, part, :], start=j == 0, stop=False)
                            ins = nc.tensor.matmul(tile, row, sq_hi[:, part, :], start=False, stop=j == 1)
                        pe_ring_done(ins)
                    elif step[0] == "q_rms_turn":
                        tile = pe_ring_bank(pe)
                        half = step[1]
                        if b is None:
                            pe.wait_ge(s_ring_free, pe_ring.value())
                        hold(nc.tensor)
                        for q in range(HALF // P):
                            ins = nc.tensor.transpose(tile[:, q * HEADS:(q + 1) * HEADS],
                                                      qss[0:HEADS, q * P:(q + 1) * P], ident[0:HEADS, 0:HEADS])
                        pe_ring_done(ins)
                    elif step[0] == "transpose":
                        pe.wait_ge(s_prob, 2 * n + 1)
                        for h in range(HEADS):
                            ins = nc.tensor.transpose(turned[:, 0, h, :], p0[:, h, :], ident[:, :])
                        ins.then_inc(s_turned, 1)
                        pe.wait_ge(s_prob, 2 * n + 2)
                        for k in range(2):
                            for h in range(HEADS):
                                ins = nc.tensor.transpose(turned[:, 1 + k, h, :],
                                                          p1v[:, h, k * P:(k + 1) * P], ident[:, :])
                            ins.then_inc(s_turned, 1)

            def act_steps(act, steps, g, b):
                n = None if b is None else S0 + 4 * g + b
                for step in steps:
                    if step[0] == "pt_split":
                        for j in range(3):
                            act.wait_ge(s_turned, 3 * (n - 1) + j + 1)
                            nc.scalar.copy(pt_hi[:, j, :, :], turned[:, j, :, :]).then_inc(s_pt_hi, 1)
                    elif step[0] == "exp":
                        for k, (sc, pr) in enumerate(((scores0, p0), (scores1, p1))):
                            act.wait_ge(s_max, 2 * n + k + 1)
                            for h in range(HEADS):
                                at = (2 * (b % 2) + k) * HEADS + h
                                scale = q_root[:, b // 2, at:at + 1] if rms else SCALE
                                ins = nc.scalar.activation(pr[:, h, :], sc[:, h, :], ACT.Exp,
                                                           bias=bias[:, k, h:h + 1], scale=scale,
                                                           accum_out=sums[:, k, h:h + 1])
                            ins.then_inc(s_exp, 1)
                    elif step[0] == "pv":
                        for k in range(2):
                            act.wait_ge(s_pv, 2 * (n - 1) + k + 1)
                            nc.scalar.copy(ot_hi[:, k, :, :], turned[:, k, :, :]).then_inc(s_ot_hi, 1)
                    elif step[0] == "tile":
                        _, X, half, ahead = step
                        tile = act_ring_tile(act)
                        tile_b = tile.rearrange("p (b s) -> p b s", b=2)
                        cols = slice(half * HALF, (half + 1) * HALF)
                        if X == V:
                            continue
                        if rms:
                            if not isinstance(act_sq.value(), int) or act_sq.value() > 0:
                                act.wait_ge(s_sq_split, act_sq.value())
                            nc.scalar.activation(sq[:, :], tile, ACT.Square).then_inc(s_sq, 1)
                            act_sq.up()
                        if X == K:
                            if rms:
                                continue
                            nc.scalar.copy(kt_f[:, 2 * half:2 * half + 2, :], tile_b[:, :, 0:P])
                            act_ring_hi(nc.scalar.copy(kt_hi[:, cols], tile))
                        else:
                            h = X - Q0
                            nc.scalar.copy(qt_f[:, h, 2 * half:2 * half + 2, :], tile_b[:, :, 0:P])
                            act_ring_hi(nc.scalar.copy(qt_hi[:, h, cols], tile))
                    elif step[0] == "v_turn":
                        tile = act_ring_tile(act)
                        act_ring_hi(nc.scalar.copy(v_hi[:, 4 * step[1]:4 * step[1] + 4, :],
                                                   tile.rearrange("p (t d) -> p t d", d=HD)))
                    elif step[0] == "k_rms":
                        act_ring.up()
                        act.wait_ge(s_ring_free, act_ring.value())
                        act_link(nc.scalar.activation(k_root[:, :], k_ms[:, :], ACT.Ln))
                        nc.scalar.activation(k_root[:, :], k_root[:, :], ACT.Exp, scale=-0.5).then_inc(s_root_k, 1)
                    elif step[0] in ("q_rms", "out"):
                        act_ring.up()
                    elif step[0] == "q_rms_turn":
                        act_ring.up()
                        act.wait_ge(s_ring_free, act_ring.value())
                        root = q_root[:, step[1], :]
                        act_link(nc.scalar.activation(root, q_ms[:, :], ACT.Ln))
                        nc.scalar.activation(root, root, ACT.Exp, scale=-0.5).then_inc(s_root_q, 1)

            dve_kr, dve_qr, pool_kr = Tally(), Tally(), Tally()

            def dve_steps(dve, steps, g, b):
                n = None if b is None else S0 + 4 * g + b
                for step in steps:
                    if step[0] == "pt_split":
                        for j in range(3):
                            dve.wait_ge(s_pt_hi, 3 * (n - 1) + j + 1)
                            nc.vector.tensor_tensor(pt_lo[:, j, :, :], turned[:, j, :, :],
                                                    as_f32(pt_hi[:, j, :, :]), ALU.subtract).then_inc(s_pt_lo, 1)
                    elif step[0] == "stats":
                        dve.wait_ge(s_scores, n + 1)
                        if rms:
                            half, t = b // 2, 2 * (b % 2)
                            for h in range(HEADS):
                                nc.vector.scalar_tensor_tensor(
                                    scores0[:, h, :], rel[:, 0:P], q_slope[:, half, t * HEADS + h:t * HEADS + h + 1],
                                    scores0[:, h, :], ALU.mult, ALU.add)
                            for h in range(HEADS):
                                at = (t + 1) * HEADS + h
                                ins = nc.vector.scalar_tensor_tensor(
                                    scores1[:, h, :], rel[:, P:P + SEQ], q_slope[:, half, at:at + 1],
                                    scores1[:, h, :], ALU.mult, ALU.add)
                        else:
                            see = tri[:, :].unsqueeze(1).to_broadcast([P, HEADS, P])
                            nc.vector.tensor_tensor(scores0[:, :, :], scores0[:, :, :], see, ALU.add)
                            ins = nc.vector.tensor_tensor(scores1[:, :, P:SEQ], scores1[:, :, P:SEQ], see, ALU.add)
                        dve_link(ins)
                        for k, sc in enumerate((scores0, scores1)):
                            dve_link(nc.vector.tensor_reduce(negmax[:, k, :], sc[:, :, :], AX.X, ALU.max, negate=True))
                            if rms:
                                at = (t + k) * HEADS
                                ins = nc.vector.tensor_tensor(bias[:, k, :], negmax[:, k, :],
                                                              q_root[:, half, at:at + HEADS], ALU.mult)
                            else:
                                ins = nc.vector.tensor_scalar(bias[:, k, :], negmax[:, k, :], SCALE, None, ALU.mult)
                            ins.then_inc(s_max, 1)
                    elif step[0] == "normalise":
                        for k, (pr, width) in enumerate(((p0, P), (p1, SEQ))):
                            dve.wait_ge(s_exp, 2 * n + k + 1)
                            dve_link(nc.vector.reciprocal(rsum[:, k, :], sums[:, k, :]))
                            nc.vector.tensor_tensor(pr[:, :, :], pr[:, :, :],
                                                    rsum[:, k, :].unsqueeze(2).to_broadcast([P, HEADS, width]),
                                                    ALU.mult).then_inc(s_prob, 1)
                    elif step[0] == "pv":
                        for k in range(2):
                            dve.wait_ge(s_ot_hi, 2 * (n - 1) + k + 1)
                            nc.vector.tensor_tensor(ot_lo[:, k, :, :], turned[:, k, :, :],
                                                    as_f32(ot_hi[:, k, :, :]), ALU.subtract).then_inc(s_ot_lo, 1)
                    elif step[0] == "out":
                        tile = dve_ring_tile(dve)
                        t = 2 * ((b - 1) % 4) + step[1]
                        dve_ring_free(nc.vector.tensor_tensor(x[:, t, :], x[:, t, :], tile, ALU.add))
                    elif step[0] == "tile":
                        _, X, half, ahead = step
                        cols = slice(half * HALF, (half + 1) * HALF)
                        if X == V:
                            tile = dve_ring_tile(dve)
                            dve_ring_free(nc.vector.tensor_copy(vt[:, :], tile))
                        elif X == K and rms:
                            tile = dve_ring_tile(dve)
                            dve_sq.up()
                            dve.wait_ge(s_sq, dve_sq.value())
                            dve_ring_free(nc.vector.tensor_scalar(k_raw[:, :], tile, norm_cols[:, 2:3], None,
                                                                  ALU.mult))
                        else:
                            if rms:
                                dve_sq.up()
                            tile = dve_ring_tile(dve, after_hi=True)
                            hi, lo = (kt_hi[:, cols], kt_lo[:, cols]) if X == K else \
                                (qt_hi[:, X - Q0, cols], qt_lo[:, X - Q0, cols])
                            dve_ring_free(nc.vector.tensor_tensor(lo, tile, as_f32(hi), ALU.subtract))
                    elif step[0] == "v_turn":
                        tile = dve_ring_tile(dve, after_hi=True)
                        at = slice(4 * step[1], 4 * step[1] + 4)
                        dve_ring_free(nc.vector.tensor_tensor(
                            v_lo[:, at, :], tile.rearrange("p (t d) -> p t d", d=HD), as_f32(v_hi[:, at, :]),
                            ALU.subtract))
                    elif step[0] == "k_rms":
                        tile = dve_ring_tile(dve)
                        dve_kr.up()
                        dve_ring_free(nc.vector.tensor_scalar(k_ms[:, :], tile, 1.0 / HD, RMS_EPS, ALU.mult,
                                                              ALU.add))
                        dve.wait_ge(s_root_k, dve_kr.value())
                        polish_root(k_root[:, :], k_ms[:, :])
                        nc.vector.tensor_tensor(k_raw[:, :], k_raw[:, :], k_root[:, :], ALU.mult).then_inc(s_kn, 1)
                    elif step[0] == "q_rms":
                        tile = dve_ring_tile(dve)
                        if step[2] == 0:
                            ins = nc.vector.tensor_copy(qss[0:HEADS, :], tile[0:HEADS, :])
                        else:
                            ins = nc.vector.tensor_tensor(qss[0:HEADS, :], qss[0:HEADS, :], tile[0:HEADS, :], ALU.add)
                        dve_ring_free(ins)
                    elif step[0] == "q_rms_turn":
                        tile = dve_ring_tile(dve)
                        dve_qr.up()
                        dve_ring_free(nc.vector.tensor_scalar(
                            q_ms[:, :], tile[:, 0:HALF // P * HEADS], 1.0 / HD, RMS_EPS, ALU.mult, ALU.add))
                        dve.wait_ge(s_root_q, dve_qr.value())
                        half = step[1]
                        root = q_root[:, half, :]
                        polish_root(root, q_ms[:, :], SCALE)
                        dve_link(nc.vector.reciprocal(q_ms[:, :], root))
                        group = 0 if b is None else g if half == 1 else g + 1
                        of_group = slopes[:, bass.ds(HEADS * group, HEADS)] if not isinstance(group, int) else \
                            slopes[:, HEADS * group:HEADS * group + HEADS]
                        dve_link(nc.vector.tensor_tensor(
                            q_slope[:, half, :].rearrange("p (t h) -> p t h", h=HEADS),
                            q_ms[:, :].rearrange("p (t h) -> p t h", h=HEADS),
                            of_group.unsqueeze(1).to_broadcast([P, HALF // P, HEADS]), ALU.mult))

            squares_used = [0]

            def pool_steps(pool, steps, g, b, refill=True):
                if b is not None:
                    squares_used[0] = pool_ring.n
                for step in steps:
                    before = pool_ring.n
                    if step[0] in RING_STEPS:
                        pool_ring.up()
                    if step[0] in ("k_rms", "q_rms"):
                        squares_used[0] = pool_ring.n
                    if step[0] == "tile":
                        _, X, half, ahead = step
                        if rms and X != V:
                            pool_sq.up()
                            part = half if X == K else (half + 1 + X - Q0) % 2
                            pool.wait_ge(s_sq, pool_sq.value())
                            if squares_used[0]:
                                pool.wait_ge(s_ring_full, pool_ring.turns + squares_used[0])
                            split_steps(pool, sq_hi[:, part, :], sq_lo[:, part, :], sq[:, :], s_sq_split)
                        if half == 1 and refill:
                            pool.wait_ge(s_ring_full, pool_ring.value())
                            pool_split_w(pool, X)
                    elif step[0] == "k_rms":
                        pool_kr.up()
                        cols = slice(step[1] * HALF, (step[1] + 1) * HALF)
                        pool.wait_ge(s_kn, pool_kr.value())
                        hold(nc.gpsimd)
                        nc.gpsimd.tensor_scalar(kt_f[:, 2 * step[1]:2 * step[1] + 2, :],
                                                k_raw[:, :].rearrange("p (b s) -> p b s", b=2)[:, :, 0:P],
                                                1.0, 0.0, ALU.mult, ALU.add)
                        split_steps(pool, kt_hi[:, cols], kt_lo[:, cols], k_raw[:, :], s_k_ready)
                    elif step == ("out", 1) and b == 0 and g is not GROUPS:
                        pool.wait_ge(s_ring_full, pool_ring.value())
                        pool_split_wd(pool)

            def sp_steps(sp, steps, g, b, refill=True):
                for step in steps:
                    if step[0] == "tile" and step[2] == 1 and refill:
                        sp_load_w(sp, step[1], GROUPS * layer + g + step[3] + 1)
                    elif step == ("out", 1) and b == 0 and g is not GROUPS:
                        sp_load_wd(sp, GROUPS * layer + g)

            def walk(eng, do, grows, pool_like=False):
                do(eng, lead_steps(rms), 0, None)
                do(eng, slot_steps(0, rms, True, first=True), 0, 0)
                last = GROUPS - 1

                def turn(g, **more):
                    for b in (1, 2, 3):
                        do(eng, slot_steps(b, rms, True), g, b, **more)
                    do(eng, slot_steps(0, rms, True), g + 1, 0, **more)

                if pool_like and layer == 1:
                    turn_loop(eng, last - 1, grows, turn)
                    turn(last - 1, refill=False)
                else:
                    turn_loop(eng, last, grows, turn)
                for b in (1, 2, 3):
                    do(eng, slot_steps(b, rms, False), last, b)
                do(eng, tail_steps(), GROUPS, 0)

            def pe(eng):
                walk(eng, pe_steps, [(pe_ring, ring_turn), (pe_sq, 10 * rms)])

            def act(eng):
                walk(eng, act_steps, [(act_ring, ring_turn), (act_hi, 12 - 2 - 2 * rms + 2),
                                      (act_chain, 4 * rms), (act_sq, 10 * rms)])

            def dve(eng):
                walk(eng, dve_steps, [(dve_ring, ring_turn), (dve_hi, 12 - 2 - 2 * rms + 2),
                                      (dve_chain, 4 * (3 + 2) + 20 * rms),
                                      (dve_sq, 10 * rms), (dve_kr, 2 * rms), (dve_qr, 2 * rms)])

            def pool(eng):
                if layer == 0:
                    for X in range(WT):
                        pool_split_w(eng, X)
                pool_split_wd(eng)
                walk(eng, pool_steps, [(pool_ring, ring_turn), (pool_chain, WT + HEADS + 12 * rms),
                                       (pool_sq, 10 * rms), (pool_kr, 2 * rms), (pool_w, 2), (pool_wd, 2)], True)

            def sp(eng):
                if layer == 0:
                    for X in range(WT):
                        sp_load_w(eng, X, 0)
                sp_load_wd(eng, GROUPS * layer)
                walk(eng, sp_steps, [(sp_w, WT), (sp_wd, HEADS)], True)

            return pe, act, dve, pool, sp

        pool_wd, sp_wd = Tally(), Tally()

        def pool_split_w(pool, X):
            if X % 3 == 0:
                pool_w.up()
            pool.wait_ge(s_w_raw[X % 3], 16 * pool_w.value())
            split_steps(pool, w_hi[:, X, :, :], w_lo[:, X, :, :],
                        w_raw[:, X % 3, :].rearrange("p (c d) -> p c d", c=DC), s_w)

        def pool_split_wd(pool):
            for h in range(HEADS):
                if h % 2 == 0:
                    pool_wd.up()
                pool.wait_ge(s_wd_raw[h % 2], 16 * pool_wd.value())
                split_steps(pool, wd_hi[:, h, :], wd_lo[:, h, :], wd_raw[:, h % 2, :], s_wd)

        def sp_load_w(sp, X, group):
            if not (isinstance(sp_w.turns, int) and sp_w.n < 3):
                sp.wait_ge(s_w, sp_w.value() - 2)
            sp_w.up()
            sp.dma_start(w_raw[:, X % 3, :], w_attn[group, X, :, :]).then_inc(s_w_raw[X % 3], 16)

        def sp_load_wd(sp, group):
            for h in range(HEADS):
                if not (isinstance(sp_wd.turns, int) and sp_wd.n < 2):
                    sp.wait_ge(s_wd, sp_wd.value() - 1)
                sp_wd.up()
                sp.dma_start(wd_raw[:, h % 2, :], w_dense[group, h, :, :]).then_inc(s_wd_raw[h % 2], 16)

        s_load0 = [sem(f"s_lora_raw{i}") for i in range(2)]
        s_a = sem("s_a")
        s_ab = sem("s_ab")
        s_tok = sem("s_tok")
        s_tok_root = sem("s_tok_root")
        s_down = sem("s_down")
        s_score = sem("s_score")
        s_gate_exp = sem("s_gate_exp")
        s_gated = sem("s_gated")
        s_gt = sem("s_gt")
        s_gt_hi = sem("s_gt_hi")
        s_gt_lo = sem("s_gt_lo")

        AW = EXPERTS + ER
        CUTS = [0, 320, 704, 1088]

        def experts(scope):
            a_hi = sb("a_hi", [P, DC, AW], F32R, scope)
            a_lo = sb("a_lo", [P, DC, AW], F32R, scope)
            b_hi = sb("b_hi", [P, EC, D], F32R, scope)
            b_lo = sb("b_lo", [P, EC, D], F32R, scope)
            hg = sb("hg", [P, ER], F32, scope)
            gt_hi = sb("gt_hi", [P, EC, P], F32R, scope)
            gt_lo = sb("gt_lo", [P, EC, P], F32R, scope)
            a_raw = sb("a_raw", [P, DC, AW], F32, scope)
            b_raw = a_raw[:, :, :].rearrange("p c e -> p (c e)")[:, 0:EC * D].rearrange("p (c d) -> p c d", d=D)
            score = sb("score", [P, EXPERTS], F32, scope)
            rest = sb("rest", [P, 2, EXPERTS], F32, scope)
            top = sb("top", [P, 2, 8], F32, scope)
            top_neg = sb("top_neg", [P, 1], F32, scope)
            gate = sb("gate", [P, EXPERTS], F32, scope)
            gsum = sb("gsum", [P, 2], F32, scope)
            banks = [scores1[:, 0:2, :], scores1[:, 2:4, :], scores0[:, :, :]]
            down = [v.rearrange("p a b -> p (a b)")[:, 0:CUTS[i + 1] - CUTS[i]] for i, v in enumerate(banks)]

            def sp(eng):
                eng.wait_ge(s_ring_free, attention_tiles[0])
                eng.dma_start(a_raw[:, :, 0:EXPERTS], lora_wr).then_inc(s_load0[0], 16)
                eng.dma_start(a_raw[:, :, EXPERTS:AW], lora_a).then_inc(s_load0[0], 16)
                eng.wait_ge(s_ab, DC)
                eng.dma_start(b_raw[:, :, :], lora_b).then_inc(s_load0[1], 16)

            def chunks():
                for c in range(DC):
                    yield a_raw[:, c, :], a_hi[:, c, :], a_lo[:, c, :], s_load0[0], 32
                for c in range(0, EC, 2):
                    yield (b_raw[:, c:c + 2, :], b_hi[:, c:c + 2, :], b_lo[:, c:c + 2, :], s_load0[1], 16)

            def act(eng):
                tok_root(eng, 0)
                for raw, hi, _, landed, count in chunks():
                    eng.wait_ge(landed, count)
                    nc.scalar.copy(hi, raw).then_inc(s_a, 1)
                turned_hi(eng, 0)

                def pair(i, first=False, last=False):
                    for par in range(2):
                        t, more = 2 * i + par, not (last and par == 1)
                        if more:
                            tok_root(eng, t + 1)
                        eng.wait_ge(s_score, t + 1)
                        nc.scalar.activation(gate[:, :], score[:, :], ACT.Exp,
                                             bias=top_neg[:, :]).then_inc(s_gate_exp, 1)
                        for k in range(2):
                            eng.wait_ge(s_gt, 2 * t + k + 1)
                            nc.scalar.copy(gt_hi[:, 4 * k:4 * k + 4, :], turned[:, k, :, :]).then_inc(s_gt_hi, 1)
                        if not (first and par == 0):
                            act_ring.up()
                        if more:
                            turned_hi(eng, par + 1)
                pair(0, first=True)
                turn_loop(eng, NT // 2 - 2, [(act_ring, 4), (act_hi, 2), (act_chain, 2)], lambda i: pair(i + 1))
                pair(NT // 2 - 1, last=True)
                act_ring.up()

            def tok_root(eng, t):
                eng.wait_ge(s_tok, t + 1)
                act_link(nc.scalar.activation(rstd[:, 0:1], var_eps[:, 0:1], ACT.Ln))
                nc.scalar.activation(rstd[:, 0:1], rstd[:, 0:1], ACT.Exp, scale=-0.5).then_inc(s_tok_root, 1)

            def turned_hi(eng, par):
                tile = act_ring_tile(eng)
                at = slice((par % 2) * P, (par % 2 + 1) * P)
                act_ring_hi(nc.scalar.copy(xt_hi[:, :, at], tile.rearrange("p (c q) -> p c q", c=DC)))

            def dve_tok(eng, t, par):
                xs = x[:, bass.ds(t, 1), :].rearrange("p a d -> p (a d)") if not isinstance(t, int) else x[:, t, :]
                hold(nc.vector)
                dve_link(nc.vector.bn_stats(bn[:, 0, :], xs))
                hold(nc.vector)
                dve_link(nc.vector.bn_aggr(mv[:, 0, :], bn[:, 0, :]))
                nc.vector.tensor_scalar(var_eps[:, 0:1], mv[:, 0, 1:2], LN_EPS, None, ALU.add).then_inc(s_tok, 1)
                eng.wait_ge(s_tok, t + 1)
                eng.wait_ge(s_tok_root, t + 1)
                polish_root(rstd[:, 0:1], var_eps[:, 0:1])
                nc.vector.tensor_scalar(xn[:, par, :], xs, mv[:, 0, 0:1], rstd[:, 0:1],
                                        ALU.subtract, ALU.mult).then_inc(s_xn, 1)

            def dve_turned_lo(eng, par):
                tile = dve_ring_tile(eng, after_hi=True)
                at = slice(par * P, (par + 1) * P)
                dve_ring_free(nc.vector.tensor_tensor(xt_lo[:, :, at], tile.rearrange("p (c q) -> p c q", c=DC),
                                                      as_f32(xt_hi[:, :, at]), ALU.subtract))

            def dve(eng):
                dve_tok(eng, 0, 0)
                for n, (raw, hi, lo, _, _) in enumerate(chunks()):
                    eng.wait_ge(s_a, n + 1)
                    nc.vector.tensor_tensor(lo, raw, as_f32(hi), ALU.subtract).then_inc(s_ab, 1)
                dve_turned_lo(eng, 0)

                def pair(i, first=False, last=False):
                    for par in range(2):
                        t, more = 2 * i + par, not (last and par == 1)
                        lead = first and par == 0
                        if more:
                            dve_tok(eng, t + 1, 1 - par)
                        eng.wait_ge(s_down, 3 * t + 1)
                        dve_link(nc.vector.tensor_copy(score[:, :], down[0][:, 0:EXPERTS]))
                        hold(nc.vector)
                        dve_link(nc.vector.max(top[:, 0, :], score[:, :]))
                        nc.vector.tensor_scalar(top_neg[:, :], top[:, 0, 0:1], -1.0, None,
                                                ALU.mult).then_inc(s_score, 1)
                        dve_link(nc.vector.match_replace(rest[:, 0, :], top[:, 0, :], score[:, :], TAKEN))
                        hold(nc.vector)
                        dve_link(nc.vector.max(top[:, 1, :], rest[:, 0, :]))
                        hold(nc.vector)
                        dve_link(nc.vector.match_replace(rest[:, 1, :], top[:, 1, :], rest[:, 0, :], TAKEN))
                        dve_link(nc.vector.tensor_scalar(rest[:, 0, :], rest[:, 1, :], TAKEN, None, ALU.is_equal))
                        eng.wait_ge(s_gate_exp, t + 1)
                        dve_link(nc.vector.tensor_tensor(gate[:, :], gate[:, :], rest[:, 0, :], ALU.mult))
                        dve_link(nc.vector.tensor_reduce(gsum[:, 0:1], gate[:, :], AX.X, ALU.add))
                        dve_link(nc.vector.reciprocal(gsum[:, 1:2], gsum[:, 0:1]))
                        dve_link(nc.vector.tensor_scalar(gate[:, :], gate[:, :], gsum[:, 1:2], LORA_SCALE,
                                                         ALU.mult, ALU.mult))
                        for k in range(3):
                            eng.wait_ge(s_down, 3 * t + k + 1)
                            skip = EXPERTS if k == 0 else 0
                            lo_col, hi_col = CUTS[k] - EXPERTS + skip, CUTS[k + 1] - EXPERTS
                            experts_of = slice(lo_col // RANK, hi_col // RANK)
                            count = (hi_col - lo_col) // RANK
                            nc.vector.tensor_tensor(
                                hg[:, lo_col:hi_col].rearrange("p (e r) -> p e r", r=RANK),
                                down[k][:, skip:].rearrange("p (e r) -> p e r", r=RANK),
                                gate[:, experts_of].unsqueeze(2).to_broadcast([P, count, RANK]),
                                ALU.mult).then_inc(s_gated, 1)
                        if not lead:
                            dve_add_out(eng, t - 1)
                        for k in range(2):
                            eng.wait_ge(s_gt_hi, 2 * t + k + 1)
                            nc.vector.tensor_tensor(gt_lo[:, 4 * k:4 * k + 4, :], turned[:, k, :, :],
                                                    as_f32(gt_hi[:, 4 * k:4 * k + 4, :]),
                                                    ALU.subtract).then_inc(s_gt_lo, 1)
                        if more:
                            dve_turned_lo(eng, 1 - par)
                pair(0, first=True)
                turn_loop(eng, NT // 2 - 2, [(dve_ring, 4), (dve_hi, 2), (dve_chain, 32)],
                          lambda i: pair(i + 1))
                pair(NT // 2 - 1, last=True)
                dve_add_out(eng, NT - 1)

            def dve_add_out(eng, t):
                tile = dve_ring_tile(eng)
                xs = x[:, bass.ds(t, 1), :].rearrange("p a d -> p (a d)") if not isinstance(t, int) else x[:, t, :]
                dve_ring_free(nc.vector.tensor_tensor(xs, xs, tile, ALU.add))

            def pe(eng, normed):
                pe_turn_normed(eng, normed + 1, xn[:, 0, :])

                def pair(i, first=False, last=False):
                    for par in range(2):
                        t, more = 2 * i + par, not (last and par == 1)
                        lead = first and par == 0
                        at = slice(par * P, (par + 1) * P)
                        if lead:
                            eng.wait_ge(s_ab, DC)
                            eng.wait_ge(s_ring_free, pe_ring.value())
                        else:
                            eng.wait_ge(s_gated, 3 * t)
                            eng.wait_ge(s_ring_free, pe_ring.value())
                        for k in range(3):
                            for c in range(DC):
                                ins = mm3(down[k], xt_hi[:, c, at], xt_lo[:, c, at],
                                          a_hi[:, c, CUTS[k]:CUTS[k + 1]], a_lo[:, c, CUTS[k]:CUTS[k + 1]],
                                          start=c == 0, stop=c == DC - 1)
                            ins.then_inc(s_down, 1)
                        if not lead:
                            pe_out(eng, t - 1)
                        for k in range(2):
                            eng.wait_ge(s_gated, 3 * t + (2 if k == 0 else 3))
                            for c in range(4):
                                ins = nc.tensor.transpose(turned[:, k, c, :],
                                                          hg[:, (4 * k + c) * P:(4 * k + c + 1) * P], ident[:, :])
                            ins.then_inc(s_gt, 1)
                        if more:
                            pe_turn_normed(eng, normed + t + 2, xn[:, 1 - par, :])
                pair(0, first=True)
                turn_loop(eng, NT // 2 - 2, [(pe_ring, 4)], lambda i: pair(i + 1))
                pair(NT // 2 - 1, last=True)
                pe_out(eng, NT - 1)

            def pe_out(eng, t):
                tile = pe_ring_bank(eng)
                if isinstance(t, int) and t == 0:
                    eng.wait_ge(s_ab, DC + EC // 2)
                eng.wait_ge(s_gt_lo, 2 * (t + 1))
                for c in range(EC):
                    ins = mm3(tile, gt_hi[:, c, :], gt_lo[:, c, :], b_hi[:, c, :], b_lo[:, c, :],
                              start=c == 0, stop=c == EC - 1)
                pe_ring_done(ins)

            return pe, act, dve, sp

        TILES = 6
        s_code = [sem(f"s_codes{i}") for i in range(2)]
        s_bits = sem("s_bits")
        s_lv_act = sem("s_levels_act")
        s_lv_pool = sem("s_levels_pool")
        s_deq = sem("s_dequantised")
        s_wq_hi = sem("s_wq_hi")
        s_wq = sem("s_wq")
        s_gu = sem("s_gate_up")
        s_silu = sem("s_silu")
        s_h = sem("s_h")
        s_h_hi = sem("s_h_hi")
        s_h_lo = sem("s_h_lo")
        s_dn = sem("s_dn")
        s_added = sem("s_added")

        def nf4(scope):
            raw = sb("code_raw", [P, 2, D], I32, scope)
            am = sb("absmax_rows", [P, 2, D], F32, scope)
            bits = sb("bits", [P, 2, 4, D], I32, scope)
            lv = sb("lv", [P, 2, 8, D], F32, scope)
            deq = sb("deq", [P, TILES, D], F32, scope)
            wq_hi = w_hi[:, :, :, :].rearrange("p t c d -> p t (c d)")
            wq_lo = w_lo[:, :, :, :].rearrange("p t c d -> p t (c d)")
            sg = sb("sg", [P, 2, HALF], F32, scope)
            hf = sb("hf", [P, 2, HALF], F32, scope)
            h_hi = sb("h_hi", [P, 2, TOK], F32R, scope)
            h_lo = sb("h_lo", [P, 2, TOK], F32R, scope)
            steps_of = nf4_steps()
            gu = [(ring[:, 0, :], ring[:, 1, :]),
                  tuple(turned[:, k, :, :].rearrange("p a b -> p (a b)") for k in range(2))]
            dn = [scores1[:, 0:2, :].rearrange("p a b -> p (a b)"), scores1[:, 2:4, :].rearrange("p a b -> p (a b)"),
                  scores0[:, :, :].rearrange("p a b -> p (a b)"), turned[:, 2, :, :].rearrange("p a b -> p (a b)")]
            LAST = MT // 2 - 1

            def plan(i):
                more = not (isinstance(i, int) and i == LAST)
                s = [("unit", 0), ("deq", 0), ("split", 5, 0), ("unit", 1)]
                if more:
                    s += [("deq", 1), ("unit", 2), ("deq", 2), ("split", 0, 1), ("unit", 3), ("deq", 3),
                          ("split", 1, 1), ("split", 2, 1), ("down", 0), ("deq", 4), ("split", 3, 1),
                          ("down", 1), ("deq", 5), ("split", 4, 1)]
                else:
                    s += [("unit", 2), ("unit", 3), ("down", 0), ("down", 1)]
                return s

            lead = [("deq", 0), ("deq", 1), ("split", 0, 1), ("deq", 2), ("split", 1, 1), ("deq", 3),
                    ("split", 2, 1), ("deq", 4), ("split", 3, 1), ("deq", 5), ("split", 4, 1)]

            def walk(eng, do):
                do(eng, lead, -1)
                do(eng, plan(0), 0)
                with eng.Fori(1, LAST) as i:
                    do(eng, plan(i), i)
                do(eng, plan(LAST), LAST)

            def above(eng, s, v, low=1):
                if not isinstance(v, int) or v >= low:
                    eng.wait_ge(s, v)

            def exists(i, k):
                return not (isinstance(i, int) and i == LAST)

            def sp(eng):
                def load(eng, steps, i):
                    for step in steps:
                        if step[0] == "deq" and exists(i, step[1]):
                            k = step[1]
                            j = TILES * (i + 1) + k
                            m = 2 * (i + 1) + (k // 2 if k < 4 else k - 4)
                            kind = k % 2 if k < 4 else 2
                            above(eng, s_deq, j - 1)
                            eng.dma_start(raw[:, k % 2, :], codes[m, kind, :, :]).then_inc(s_code[k % 2], 16)
                            for side in range(2):
                                eng.dma_start(am[64 * side:64 * side + 64, k % 2, :],
                                              absmax[m, kind, side, :].partition_broadcast(64)).then_inc(s_code[k % 2], 16)
                eng.wait_ge(s_ring_free, attention_tiles[1])
                walk(eng, load)
                for t in range(NT):
                    eng.wait_ge(s_added, NT * LAST + t + 1)
                    eng.dma_start(out[t * P:(t + 1) * P, :], x[:, t, :]).then_inc(s_out, 16)
                eng.wait_ge(s_out, 16 * NT)

            def act(eng):
                def do(eng, steps, i):
                    for step in steps:
                        if step[0] == "unit":
                            u = 4 * i + step[1]
                            g_bank = gu[step[1] % 2][0]
                            eng.wait_ge(s_gu, 2 * u + 1)
                            above(eng, s_h, u - 1)
                            nc.scalar.activation(sg[:, step[1] % 2, :], g_bank, ACT.Silu).then_inc(s_silu, 1)
                            eng.wait_ge(s_h, u + 1)
                            mm, half = step[1] % 2, step[1] // 2
                            nc.scalar.copy(h_hi[:, mm, half * HALF:(half + 1) * HALF],
                                           hf[:, step[1] % 2, :]).then_inc(s_h_hi, 1)
                        elif step[0] == "deq" and exists(i, step[1]):
                            k = step[1]
                            j = TILES * (i + 1) + k
                            eng.wait_ge(s_bits, j + 1)
                            above(eng, s_deq, j - 1)
                            for q in range(4):
                                low, dist = steps_of[q]
                                ins = nc.scalar.activation(lv[:, k % 2, q, :], bits[:, k % 2, 0, :], ACT.Copy,
                                                           bias=low, scale=dist)
                            ins.then_inc(s_lv_act, 1)
                        elif step[0] == "split":
                            k, j = step[1], TILES * (i + step[2]) + step[1]
                            eng.wait_ge(s_deq, j + 1)
                            slot_used(eng, i, k, step[2])
                            nc.scalar.copy(wq_hi[:, k, :], deq[:, k, :]).then_inc(s_wq_hi, 1)
                walk(eng, do)

            def slot_used(eng, i, k, ahead):
                if k in (0, 1):
                    above(eng, s_gu, 2 * (4 * i + 2) + 2)
                elif k in (2, 3):
                    above(eng, s_gu, 2 * (4 * i + 3) + 2)
                else:
                    above(eng, s_dn, NT * (i + ahead))

            def pool(eng):
                def do(eng, steps, i):
                    for step in steps:
                        if step[0] == "unit":
                            u = 4 * i + step[1]
                            mm, half = step[1] % 2, step[1] // 2
                            cols = slice(half * HALF, (half + 1) * HALF)
                            eng.wait_ge(s_h_hi, u + 1)
                            nc.gpsimd.tensor_tensor(h_lo[:, mm, cols], hf[:, step[1] % 2, :],
                                                    as_f32(h_hi[:, mm, cols]), ALU.subtract).then_inc(s_h_lo, 1)
                        elif step[0] == "deq" and exists(i, step[1]):
                            k = step[1]
                            j = TILES * (i + 1) + k
                            eng.wait_ge(s_bits, j + 1)
                            above(eng, s_deq, j - 1)
                            hold(nc.gpsimd)
                            for q in range(4, 8):
                                low, dist = steps_of[q]
                                ins = nc.gpsimd.tensor_scalar(lv[:, k % 2, q, :], bits[:, k % 2, 0, :], dist, low,
                                                              ALU.mult, ALU.add)
                            ins.then_inc(s_lv_pool, 1)
                        elif step[0] == "split":
                            k, j = step[1], TILES * (i + step[2]) + step[1]
                            eng.wait_ge(s_wq_hi, j + 1)
                            nc.gpsimd.tensor_tensor(wq_lo[:, k, :], deq[:, k, :], as_f32(wq_hi[:, k, :]),
                                                    ALU.subtract).then_inc(s_wq, 1)
                walk(eng, do)

            def dve(eng):
                chain = Tally()
                chain.n = dve_chain.n

                def do(eng, steps, i):
                    for step in steps:
                        if step[0] == "unit":
                            u = 4 * i + step[1]
                            eng.wait_ge(s_silu, u + 1)
                            eng.wait_ge(s_gu, 2 * u + 2)
                            above(eng, s_h_lo, u - 1)
                            nc.vector.tensor_tensor(hf[:, step[1] % 2, :], sg[:, step[1] % 2, :],
                                                    gu[step[1] % 2][1], ALU.mult).then_inc(s_h, 1)
                        elif step[0] == "deq":
                            k = step[1]
                            j = TILES * (i + 1) + k
                            if exists(i, k):
                                eng.wait_ge(s_code[k % 2], 48 * (3 * (i + 1) + k // 2 + 1))
                                for b in range(4):
                                    ins = nc.vector.tensor_scalar(bits[:, k % 2, b, :], raw[:, k % 2, :], 1 << b, None,
                                                                  ALU.bitwise_and)
                                ins.then_inc(s_bits, 1)
                            if not (isinstance(j, int) and j == 0):
                                select(eng, j - 1, (k - 1) % 2, (k - 1) % TILES)
                        elif step[0] == "down":
                            for t in range(4 * step[1], 4 * step[1] + 4):
                                eng.wait_ge(s_dn, NT * i + t + 1)
                                nc.vector.tensor_tensor(x[:, t, :], x[:, t, :], dn[t % 4], ALU.add).then_inc(s_added, 1)

                def select(eng, j, par, slot):
                    eng.wait_ge(s_lv_act, j + 1)
                    eng.wait_ge(s_lv_pool, j + 1)
                    eng.wait_ge(s_bits, j + 1)
                    hold(nc.vector)
                    link(nc.vector.copy_predicated(
                        lv[:, par, 0::2, :], bits[:, par, 1, :].unsqueeze(1).to_broadcast([P, 4, D]), lv[:, par, 1::2, :]))
                    hold(nc.vector)
                    link(nc.vector.copy_predicated(
                        lv[:, par, 0::4, :], bits[:, par, 2, :].unsqueeze(1).to_broadcast([P, 2, D]), lv[:, par, 2::4, :]))
                    hold(nc.vector)
                    link(nc.vector.copy_predicated(lv[:, par, 0, :], bits[:, par, 3, :], lv[:, par, 4, :]))
                    above(eng, s_wq, j - TILES + 1)
                    nc.vector.tensor_tensor(deq[:, slot, :], lv[:, par, 0, :], am[:, par, :], ALU.mult).then_inc(s_deq, 1)

                link = dve_link
                do(eng, lead, -1)
                do(eng, plan(0), 0)
                turn_loop(eng, LAST - 1, [(dve_chain, 3 * TILES)], lambda i: do(eng, plan(i + 1), i + 1))
                do(eng, plan(LAST), LAST)

            def pe(eng):
                eng.wait_ge(s_ring_free, pe_ring.value())

                def do(eng, steps, i):
                    for step in steps:
                        if step[0] == "unit":
                            k = step[1]
                            u, mm, half = 4 * i + k, k % 2, k // 2
                            cols = slice(half * HALF, (half + 1) * HALF)
                            above(eng, s_h, u - 1)
                            for kind in range(2):
                                w = 2 * mm + kind
                                if half == 0:
                                    eng.wait_ge(s_wq, TILES * i + w + 1)
                                for c in range(DC):
                                    at = slice(c * P, (c + 1) * P)
                                    ins = mm3(gu[k % 2][kind], wq_hi[:, w, at], wq_lo[:, w, at], xt_hi[:, c, cols],
                                              xt_lo[:, c, cols], start=c == 0, stop=c == DC - 1)
                                ins.then_inc(s_gu, 1)
                        elif step[0] == "down":
                            eng.wait_ge(s_h_lo, 4 * i + 2 * step[1] + 2)
                            if step[1] == 0:
                                eng.wait_ge(s_wq, TILES * i + TILES)
                            for t in range(4 * step[1], 4 * step[1] + 4):
                                above(eng, s_added, NT * i + t - 3)
                                for mm in range(2):
                                    at = slice(t * P, (t + 1) * P)
                                    ins = mm3(dn[t % 4], h_hi[:, mm, at], h_lo[:, mm, at], wq_hi[:, 4 + mm, :],
                                              wq_lo[:, 4 + mm, :], start=mm == 0, stop=mm == 1)
                                ins.then_inc(s_dn, 1)
                do(eng, plan(0), 0)
                with eng.Fori(1, LAST) as i:
                    do(eng, plan(i), i)
                do(eng, plan(LAST), LAST)

            return pe, act, dve, pool, sp

        attention_tiles = [0, 0]
        a_scope, b_scope, c_scope, d_scope = ExitStack(), ExitStack(), ExitStack(), ExitStack()
        with a_scope:
            pe_a, act_a, dve_a, pool_a, sp_a = attention(0, a_scope)
        with b_scope:
            pe_b, act_b, dve_b, sp_b = experts(b_scope)
        with c_scope:
            pe_c, act_c, dve_c, pool_c, sp_c = attention(1, c_scope)
        with d_scope:
            pe_d, act_d, dve_d, pool_d, sp_d = nf4(d_scope)

        block = ctx.enter_context(nc.Block())

        @block.tensor
        def _(pe):
            pe.wait_ge(s_ident, 2)
            pe_norm(pe, 0)
            pe_a(pe)
            attention_tiles[0] = pe_ring.n
            pe_b(pe, NT)
            pe_norm(pe, 2 * NT)
            pe.wait_ge(s_const, 2)
            pe_c(pe)
            attention_tiles[1] = pe_ring.n
            pe_norm(pe, 3 * NT)
            pe_d(pe)

        @block.scalar
        def _(act):
            act_norm(act)
            act_a(act)
            act_b(act)
            act_norm(act)
            act_c(act)
            act_norm(act)
            act_d(act)

        @block.vector
        def _(dve):
            def x_added(t):
                if t == 0:
                    dve.wait_ge(s_ring_free, dve_ring.value())

            dve_norm(dve, lambda t: dve.wait_ge(s_x[t], 16))
            dve.wait_ge(s_ident, 2)
            dve_a(dve)
            dve_b(dve)
            dve_norm(dve, x_added)
            dve.wait_ge(s_norm_w, 32)
            dve_link(nc.vector.tensor_tensor(norm_cols[:, 2:3], norm_cols[:, 0:1], norm_cols[:, 1:2], ALU.mult))
            dve.wait_ge(s_const, 3)
            dve_c(dve)
            dve_norm(dve, x_added)
            dve_d(dve)

        @block.gpsimd
        def _(pool):
            pool_link(nc.gpsimd.memset(ident[:, :], 0.0))
            pool_link(nc.gpsimd.memset(tri[:, :], 0.0))
            nc.gpsimd.affine_select(out=ident[:, :], in_=ident[:, :], compare_op=ALU.not_equal, fill=1.0,
                                    base=0, pattern=[[-1, P]], channel_multiplier=1).then_inc(s_ident, 1)
            nc.gpsimd.affine_select(out=tri[:, :], in_=tri[:, :], compare_op=ALU.is_ge, fill=MASKED,
                                    base=0, pattern=[[-1, P]], channel_multiplier=1).then_inc(s_ident, 1)
            pool_ring.up(NT)
            pool_a(pool)
            pool_ring.up(2 * NT + NT)
            for n, (col, value) in enumerate(((0, 0.0), (1, 1.0))):
                dst = (pick[:, :], ones_r[:, :])[n]
                pool_link(nc.gpsimd.memset(rel[:, 0:dst.shape[1]], value))
                pool_link(nc.gpsimd.tensor_scalar(dst, rel[:, 0:dst.shape[1]], 1.0, 0.0, ALU.mult, ALU.add))
            nc.gpsimd.tensor_scalar(pick[:, P:P + 1], rel[:, 0:1], 1.0, 0.0, ALU.mult, ALU.add).then_inc(s_const, 1)
            nc.gpsimd.tensor_scalar(ones_r[:, 0:1], rel[:, 0:1], 1.0, 0.0, ALU.mult, ALU.add).then_inc(s_const, 1)
            for i, slope in enumerate(alibi_slopes()):
                nc.gpsimd.memset(slopes[:, i:i + 1], slope)
            pool.wait_ge(s_const, 2)
            for base, cols in ((0, slice(0, P)), (-P, slice(P, P + SEQ))):
                part = rel[:, cols]
                width = cols.stop - cols.start
                pool_link(nc.gpsimd.iota(part, pattern=[[1, width]], base=base, channel_multiplier=-1,
                                         allow_small_or_imprecise_dtypes=True))
                last = nc.gpsimd.affine_select(out=part, in_=part, compare_op=ALU.is_ge, fill=MASKED,
                                               base=-base, pattern=[[-1, width]], channel_multiplier=1)
                if base == 0:
                    pool_link(last)
            last.then_inc(s_const, 1)
            pool_c(pool)
            pool_d(pool)

        @block.sync
        def _(sp):
            for t in range(NT):
                sp.dma_start(x[:, t, :], x_in[t * P:(t + 1) * P, :]).then_inc(s_x[t], 16)
            for i in range(2):
                sp.dma_start(norm_cols[:, i:i + 1], norm_w[i, :].rearrange("(p a) -> p a", a=1)).then_inc(s_norm_w, 16)
            sp_a(sp)
            sp_b(sp)
            sp_c(sp)
            sp_d(sp)


def kernel(L0_attn_q, L0_attn_w_qkv, L0_attn_w_dense, L0_ffn_A, L0_ffn_B, L0_ffn_Wr, L1_attn_Wq, L1_attn_Wk,
           L1_attn_Wv, L1_attn_Wo, L1_attn_q_norm_w, L1_attn_k_norm_w, L1_ffn_gate_q, L1_ffn_gate_absmax,
           L1_ffn_up_q, L1_ffn_up_absmax, L1_ffn_down_q, L1_ffn_down_absmax):
    import concourse.bacc as bacc
    from concourse.bass_utils import run_bass_kernel_spmd

    def attn_tiles(wq, wk, wv):
        q = np.asarray(wq).reshape(GROUPS, HEADS, HD, DC, P)
        k = np.asarray(wk).reshape(GROUPS, 1, HD, DC, P)
        v = np.asarray(wv).reshape(GROUPS, 1, HD, DC, P)
        tiles = np.concatenate([k, q, v], axis=1)
        return tiles.transpose(0, 1, 4, 3, 2).reshape(GROUPS, WT, P, DC * HD)

    def by_chunk(w):
        return np.asarray(w).T.reshape(DC, P, -1).transpose(1, 0, 2)

    def hidden_in(q):
        return np.asarray(q).reshape(MT, P, DC, P).transpose(0, 3, 2, 1).reshape(MT, P, D)

    def hidden_in_absmax(a):
        return np.asarray(a).reshape(MT, P, DC, 2).transpose(0, 3, 2, 1).reshape(MT, 2, D)

    qkv, nq, nk = np.asarray(L0_attn_w_qkv), GROUPS * HEADS * HD, GROUPS * HD
    arrays = {
        "x_in": np.asarray(L0_attn_q).reshape(TOK, D),
        "w_attn": np.concatenate([attn_tiles(qkv[:nq], qkv[nq:nq + nk], qkv[nq + nk:]),
                                  attn_tiles(L1_attn_Wq, L1_attn_Wk, L1_attn_Wv)]),
        "w_dense": np.concatenate([np.asarray(w).T.reshape(GROUPS, HEADS, HD, D)
                                   for w in (L0_attn_w_dense, L1_attn_Wo)]),
        "lora_a": by_chunk(np.asarray(L0_ffn_A).reshape(ER, D)),
        "lora_wr": by_chunk(L0_ffn_Wr),
        "lora_b": np.asarray(L0_ffn_B).transpose(0, 2, 1).reshape(EC, P, D).transpose(1, 0, 2),
        "norm_w": np.stack([np.asarray(L1_attn_q_norm_w), np.asarray(L1_attn_k_norm_w)]),
        "codes": np.stack([hidden_in(L1_ffn_gate_q), hidden_in(L1_ffn_up_q),
                           np.asarray(L1_ffn_down_q).T.reshape(MT, P, D)], axis=1),
        "absmax": np.stack([hidden_in_absmax(L1_ffn_gate_absmax), hidden_in_absmax(L1_ffn_up_absmax),
                            np.asarray(L1_ffn_down_absmax).reshape(D, MT, 2).transpose(1, 2, 0)], axis=1),
    }
    nc = bacc.Bacc("TRN2", target_bir_lowering=False, num_devices=1)
    arrays = {f"{n}_dram": np.ascontiguousarray(a) for n, a in arrays.items()}
    args = {n[:-5]: nc.dram_tensor(n, a.shape, mybir.dt.from_np(a.dtype), kind="ExternalInput").ap()
            for n, a in arrays.items()}
    out = nc.dram_tensor("out_dram", (TOK, D), F32, kind="ExternalOutput").ap()
    build(nc, out=out, **args)
    r = run_bass_kernel_spmd(nc, [arrays], core_ids=[0])
    return r.results[0]["out_dram"].reshape(BATCH, SEQ, D)
```

```python
import numpy as np

import concourse.bass as bass
from concourse import mybir
from contextlib import ExitStack

F32 = mybir.dt.float32
F32R = mybir.dt.float32r
I32 = mybir.dt.int32
ALU = mybir.AluOpType
ACT = mybir.ActivationFunctionType
AX = mybir.AxisListType

P = 128
BATCH, SEQ, D = 4, 256, 512
TOK = BATCH * SEQ
NT = TOK // P
DC = D // P
HALF = 512
GROUPS, HEADS = 8, 4
HD = 128
EXPERTS, RANK, TOPK = 64, 16, 16
ER = EXPERTS * RANK
EC = ER // P
FF = 1792
MT = FF // P
BLOCK = 64
LN_EPS, RMS_EPS = 1e-5, 1e-6
MASKED = -1e30
TAKEN = -3e38
SCALE = float(np.float32(1.0) / np.sqrt(np.float32(HD)))
LORA_SCALE = 32.0 / RANK
K, Q0, Q1, Q2, Q3, V = range(6)
WT = 6

NF4 = np.array([-1.0, -0.6961928009986877, -0.5250730514526367, -0.39491748809814453,
                -0.28444138169288635, -0.18477343022823334, -0.09105003625154495, 0.0,
                0.07958029955625534, 0.16093020141124725, 0.24611230194568634, 0.33791524171829224,
                0.44070982933044434, 0.5626170039176941, 0.7229568362236023, 1.0], dtype=np.float32)


def nf4_steps():
    steps = []
    for j in range(8):
        low, high = NF4[2 * j], NF4[2 * j + 1]
        step = np.float32(high - low)
        for way in (np.float32(np.inf), np.float32(-np.inf)):
            s = step
            for _ in range(8):
                if np.float32(low + s) == high:
                    break
                s = np.nextafter(s, way)
            if np.float32(low + s) == high:
                break
        assert np.float32(low + s) == high
        steps.append((float(low), float(s)))
    return steps


def alibi_slopes():
    start = 2 ** (-2 ** (-(np.log2(GROUPS * HEADS) - 3)))
    return [float(np.float32(start * start ** i)) for i in range(GROUPS * HEADS)]


def slot_steps(b, rms, projects, first=False):
    half = 0 if b in (1, 2) else 1
    ahead = 0 if b == 0 else 1
    tiles = [K, Q0, Q1] if b in (1, 3) else [Q2, Q3, V]
    if not projects:
        tiles = []
    t = [("tile", x, half, ahead) for x in tiles]
    s = [] if first else [("pt_split",)]
    s += [("scores",), ("mask",), ("max", 0)] + t[0:1] + [("max", 1), ("exp", 0), ("normalise", 0)]
    s += t[1:2] + [("exp", 1)]
    roots = rms and b in (1, 3) and (projects or b == 1)
    if roots:
        s += [("q_rms_turn", 1 if b == 1 else 0)]
    s += [] if first else [("pv",)]
    if rms and tiles and tiles[0] == K:
        s += [("k_rms", half)]
    s += t[2:3] + [("normalise", 1)]
    s += [] if first else [("out", 0)]
    if tiles and tiles[-1] == V:
        s += [("v_turn", half)]
    if roots:
        s += [("k_norm", 1 if b == 1 else 0)]
    s += [] if first else [("out", 1)]
    if rms and tiles:
        s += [("q_rms", half, 0 if tiles[0] == K else 1)]
    return s + [("transpose",)]


def lead_steps(rms):
    s = [("tile", x, 0, 0) for x in (K, Q0)] + ([("k_rms", 0)] if rms else [])
    s += [("tile", Q1, 0, 0)] + ([("q_rms", 0, 0)] if rms else [])
    s += [("tile", x, 0, 0) for x in (Q2, Q3, V)] + [("v_turn", 0)]
    s += ([("q_rms", 0, 1), ("q_rms_turn", 0), ("k_norm", 0)] if rms else [])
    s += [("tile", x, 1, 0) for x in (K, Q0)] + ([("k_rms", 1)] if rms else [])
    s += [("tile", Q1, 1, 0)] + ([("q_rms", 1, 0)] if rms else [])
    return s


def tail_steps():
    return [("pt_split",), ("pv",), ("out", 0), ("out", 1)]


RING_STEPS = ("tile", "k_rms", "v_turn", "q_rms", "q_rms_turn", "k_norm", "out")
SIDE = 2


class Tally:

    def __init__(self):
        self.turns, self.n = 0, 0

    def up(self, by=1):
        self.n += by

    def value(self):
        return self.turns + self.n


class Ring(Tally):

    def __init__(self):
        super().__init__()
        self.mains, self.last = 0, [0, 0, 0]

    def take(self, side=False):
        bank = SIDE if side else self.mains % 2
        before = self.last[bank]
        self.up()
        self.mains += not side
        self.last[bank] = self.n
        return bank, before


def turn_loop(eng, count, grows, body):
    with eng.Fori(0, count) as i:
        starts = [t.n for t, _ in grows]
        for t, by in grows:
            t.turns = i * by
        body(i)
    for (t, by), n in zip(grows, starts):
        assert t.n == n + by, (t.n - n, by)
        t.turns, t.n = 0, n + by * count
        if isinstance(t, Ring):
            t.last = [v + by * (count - 1) for v in t.last]


def build(nc, x_in, w_attn, w_dense, lora_a, lora_wr, lora_b, norm_w, codes, absmax, out):
    with ExitStack() as ctx:
        def sem(name):
            return ctx.enter_context(nc.semaphore(name))

        def sb(name, shape, dt=F32, scope=ctx):
            return scope.enter_context(nc.sbuf_tensor(name, shape, dt))

        def psum(name, shape):
            return ctx.enter_context(nc.psum_tensor(name, shape, F32))

        x = sb("x", [P, NT, D])
        xt_hi = sb("xt_hi", [P, DC, TOK], F32R)
        xt_lo = sb("xt_lo", [P, DC, TOK], F32R)
        ident = sb("ident", [P, P])
        xn = sb("xn", [P, 2, D])
        bn = sb("bn", [P, NT, 6])
        mv = sb("mv", [P, NT, 2])
        var_eps = sb("var_eps", [P, NT])
        rstd = sb("rstd", [P, NT])
        newton = sb("newton", [P, NT])
        scores1 = psum("scores1", [P, HEADS, SEQ])
        scores0 = psum("scores0", [P, HEADS, P])
        turned = psum("turned", [P, 3, HEADS, P])
        ring = psum("ring", [P, 2, 512])

        s_x = [sem(f"s_x_loaded{t}") for t in range(NT)]
        s_ident = sem("s_ident")
        s_const = sem("s_const")
        s_norm_w = sem("s_norm_w")
        s_ring_full = sem("s_ring_full")
        s_ring_hi = sem("s_ring_hi")
        s_ring_free = sem("s_ring_free")
        s_xn = sem("s_xn")
        s_scores = sem("s_scores")
        s_max = sem("s_max")
        s_exp = sem("s_exp")
        s_prob = sem("s_prob")
        s_turned = sem("s_turned")
        s_pt_hi = sem("s_pt_hi")
        s_pt_lo = sem("s_pt_lo")
        s_pv = sem("s_pv")
        s_ot_hi = sem("s_ot_hi")
        s_ot_lo = sem("s_ot_lo")
        s_w_raw = [sem(f"s_w_raw{r}") for r in range(3)]
        s_wd_raw = [sem(f"s_wd_raw{r}") for r in range(2)]
        s_w = sem("s_w")
        s_wd = sem("s_wd")
        s_pool = sem("s_pool")
        s_dve = sem("s_dve")
        s_act = sem("s_act")
        s_sq = sem("s_sq")
        s_sq_split = sem("s_sq_split")
        s_k_ready = sem("s_k_ready")
        s_roots = sem("s_roots")
        s_out = sem("s_out_stored")

        def mm3(o, l_hi, l_lo, r_hi, r_lo, start=True, stop=True):
            nc.tensor.matmul(o, l_lo, r_hi, start=start, stop=False)
            nc.tensor.matmul(o, l_hi, r_lo, start=False, stop=False)
            return nc.tensor.matmul(o, l_hi, r_hi, start=False, stop=stop)

        def as_f32(ap):
            return ap.bitcast(F32)

        pe_ring, act_ring, dve_ring, pool_ring = Ring(), Ring(), Ring(), Tally()
        ring_banks = [ring[:, 0, :], ring[:, 1, :], turned[:, 2, :, :].rearrange("p a b -> p (a b)")]
        act_hi, dve_hi, act_chain, dve_chain, pool_chain = Tally(), Tally(), Tally(), Tally(), Tally()
        act_sq, dve_sq, pool_sq, pe_sq = Tally(), Tally(), Tally(), Tally()
        pool_w, sp_w = Tally(), Tally()

        def hold(eng):
            eng.nop(nofuse=True)

        def dve_link(ins):
            ins.then_inc(s_dve, 1)
            dve_chain.up()
            nc.vector.wait_ge(s_dve, dve_chain.value())

        def act_link(ins):
            ins.then_inc(s_act, 1)
            act_chain.up()
            nc.scalar.wait_ge(s_act, act_chain.value())

        def pool_link(ins):
            ins.then_inc(s_pool, 1)
            pool_chain.up()
            nc.gpsimd.wait_ge(s_pool, pool_chain.value())

        def roots(y, v, tmp):
            y_bits = y.bitcast(I32)
            dve_link(nc.vector.tensor_scalar(y_bits, v.bitcast(I32), 1, None, ALU.logical_shift_right))
            dve_link(nc.vector.tensor_scalar(y_bits, y_bits, -1.0, float(0x5F3759DF), ALU.mult, ALU.add))
            for _ in range(3):
                dve_link(nc.vector.tensor_tensor(tmp, y, y, ALU.mult))
                dve_link(nc.vector.scalar_tensor_tensor(tmp, tmp, -0.5, v, ALU.mult, ALU.mult))
                dve_link(nc.vector.scalar_tensor_tensor(y, tmp, 1.5, y, ALU.add, ALU.mult))

        def pe_ring_bank(pe, side=False):
            bank, before = pe_ring.take(side)
            if not isinstance(pe_ring.turns, int) or before > 0:
                pe.wait_ge(s_ring_free, pe_ring.turns + before)
            return ring_banks[bank]

        def pe_ring_done(ins):
            ins.then_inc(s_ring_full, 1)

        def act_ring_tile(act, side=False):
            bank, _ = act_ring.take(side)
            act.wait_ge(s_ring_full, act_ring.value())
            return ring_banks[bank]

        def act_ring_hi(ins):
            ins.then_inc(s_ring_hi, 1)
            act_hi.up()

        def dve_ring_tile(dve, after_hi=False, side=False):
            bank, _ = dve_ring.take(side)
            if after_hi:
                dve_hi.up()
                dve.wait_ge(s_ring_hi, dve_hi.value())
            else:
                dve.wait_ge(s_ring_full, dve_ring.value())
            return ring_banks[bank]

        def dve_ring_free(ins):
            ins.then_inc(s_ring_free, 1)

        def dve_norm(dve, wait_x):
            for t in range(NT):
                wait_x(t)
                st = nc.vector.bn_stats(bn[:, t, :], x[:, t, :])
            dve_link(st)
            for t in range(NT):
                st = nc.vector.bn_aggr(mv[:, t, :], bn[:, t, :])
            dve_link(st)
            dve_link(nc.vector.tensor_scalar(var_eps[:, :], mv[:, :, 1], LN_EPS, None, ALU.add))
            roots(rstd[:, :], var_eps[:, :], newton[:, :])

            def normed(t):
                nc.vector.tensor_scalar(xn[:, t % 2, :], x[:, t, :], mv[:, t, 0:1], rstd[:, t:t + 1],
                                        ALU.subtract, ALU.mult).then_inc(s_xn, 1)

            normed(0)
            normed(1)
            for t in range(NT):
                tile = dve_ring_tile(dve, after_hi=True)
                at = slice(t * P, (t + 1) * P)
                dve_ring_free(nc.vector.tensor_tensor(
                    xt_lo[:, :, at], tile.rearrange("p (c q) -> p c q", c=DC), as_f32(xt_hi[:, :, at]),
                    ALU.subtract))
                if t + 2 < NT:
                    normed(t + 2)

        def act_norm(act):
            for t in range(NT):
                tile = act_ring_tile(act)
                act_ring_hi(nc.scalar.copy(xt_hi[:, :, t * P:(t + 1) * P],
                                           tile.rearrange("p (c q) -> p c q", c=DC)))

        def pe_turn_normed(pe, t_xn, buf):
            tile = pe_ring_bank(pe)
            pe.wait_ge(s_xn, t_xn)
            for c in range(DC):
                ins = nc.tensor.transpose(tile[:, c * P:(c + 1) * P], buf[:, c * P:(c + 1) * P], ident[:, :])
            pe_ring_done(ins)

        def pe_norm(pe, before):
            for t in range(NT):
                pe_turn_normed(pe, before + t + 1, xn[:, t % 2, :])

        w_raw = sb("w_raw", [P, 3, DC * P])
        w_hi = sb("w_hi", [P, WT, DC, P], F32R)
        w_lo = sb("w_lo", [P, WT, DC, P], F32R)
        wd_raw = sb("wd_raw", [P, 2, D])
        wd_hi = sb("wd_hi", [P, HEADS, D], F32R)
        wd_lo = sb("wd_lo", [P, HEADS, D], F32R)
        tri = sb("tri", [P, P])
        ones_r = sb("ones_r", [P, P], F32R)
        pick = sb("pick", [P, 2 * P], F32R)
        rel = sb("rel", [P, SEQ + P])
        slopes = sb("slopes", [P, GROUPS * HEADS])
        norm_cols = sb("norm_cols", [P, 3])
        RING_TURN = [2 * WT + 2 + 2 * BATCH, 2 * WT + 2 + 2 * BATCH + 2 + 4 + 2 + 2]

        def split_steps(pool, dst_hi, dst_lo, src, sem_done):
            hold(nc.gpsimd)
            pool_link(nc.gpsimd.tensor_scalar(dst_hi, src, 1.0, 0.0, ALU.mult, ALU.add))
            nc.gpsimd.tensor_tensor(dst_lo, src, as_f32(dst_hi), ALU.subtract).then_inc(sem_done, 1)

        ROWS = HEADS + 1

        def attention(layer, scope):
            rms = layer == 1
            ring_turn = RING_TURN[layer]
            S0 = 32 * layer

            qt_hi = sb(f"qt_hi{layer}", [P, HEADS, TOK], F32R, scope)
            qt_lo = sb(f"qt_lo{layer}", [P, HEADS, TOK], F32R, scope)
            qt_f = sb(f"qt_f{layer}", [P, HEADS, BATCH, P], F32, scope)
            kt_hi = sb(f"kt_hi{layer}", [P, TOK], F32R, scope)
            kt_lo = sb(f"kt_lo{layer}", [P, TOK], F32R, scope)
            kt_f = sb(f"kt_f{layer}", [P, BATCH, P], F32, scope)
            v_hi = sb(f"v_hi{layer}", [P, NT, HD], F32R, scope)
            v_lo = sb(f"v_lo{layer}", [P, NT, HD], F32R, scope)
            vt = sb(f"vt{layer}", [P, HALF], F32, scope)
            p0 = sb(f"p0{layer}", [P, HEADS, P], F32, scope)
            p1 = sb(f"p1{layer}", [P, HEADS, SEQ], F32, scope)
            pt_hi = sb(f"pt_hi{layer}", [P, 3, HEADS, P], F32R, scope)
            pt_lo = sb(f"pt_lo{layer}", [P, 3, HEADS, P], F32R, scope)
            ot_hi = sb(f"ot_hi{layer}", [P, 2, HEADS, P], F32R, scope)
            ot_lo = sb(f"ot_lo{layer}", [P, 2, HEADS, P], F32R, scope)
            negmax = sb(f"negmax{layer}", [P, 2, HEADS], F32, scope)
            bias = sb(f"bias{layer}", [P, 2, HEADS], F32, scope)
            sums = sb(f"sums{layer}", [P, 2, HEADS], F32, scope)
            rsum = sb(f"rsum{layer}", [P, 2, HEADS], F32, scope)
            if rms:
                sq = sb("sq", [P, HALF], F32, scope)
                sq_hi = sb("sq_hi", [P, 2, HALF], F32R, scope)
                sq_lo = sb("sq_lo", [P, 2, HALF], F32R, scope)
                k_raw = sb("k_raw", [P, 2, HALF], F32, scope)
                sumsq = xn
                ms = sb("ms", [P, HALF // P, ROWS], F32, scope)
                ms_tmp = sb("ms_tmp", [P, HALF // P, ROWS], F32, scope)
                root = sb("root", [P, 2, HALF // P, ROWS], F32, scope)
                q_slope = sb("q_slope", [P, 2, HALF // P, HEADS], F32, scope)
            p1v = p1[:, :, :]

            def q_slot(b, k):
                return slice(b * SEQ + k * P, b * SEQ + (k + 1) * P)

            pe_roots, dve_roots = Tally(), Tally()
            v_at = [0]

            def pe_steps(pe, steps, g, b):
                n = None if b is None else S0 + 4 * g + b
                pe_ring.last = [pe_ring.n] * 3
                for step in steps:
                    if step[0] == "tile":
                        _, X, half, ahead = step
                        tile = pe_ring_bank(pe)
                        if half == 0:
                            pe.wait_ge(s_w, WT * (GROUPS * layer + g + ahead) + X + 1)
                        cols = slice(half * HALF, (half + 1) * HALF)
                        for c in range(DC):
                            ins = mm3(tile, w_hi[:, X, c, :], w_lo[:, X, c, :], xt_hi[:, c, cols],
                                      xt_lo[:, c, cols], start=c == 0, stop=c == DC - 1)
                        pe_ring_done(ins)
                        if X == V:
                            v_at[0] = pe_ring.n
                    elif step[0] == "scores":
                        if not isinstance(n, int) or n > S0:
                            pe.wait_ge(s_exp, 2 * n)
                        if b % 2 == 0 and rms:
                            pe.wait_ge(s_k_ready, 2 * g + b // 2 + 1)
                        for h in range(HEADS):
                            ins = nc.tensor.matmul(scores0[:, h, :], qt_f[:, h, b, :], kt_f[:, b, :],
                                                   start=True, stop=True)
                        keys = slice(b * SEQ, (b + 1) * SEQ)
                        for h in range(HEADS):
                            ins = mm3(scores1[:, h, :], qt_hi[:, h, q_slot(b, 1)], qt_lo[:, h, q_slot(b, 1)],
                                      kt_hi[:, keys], kt_lo[:, keys])
                        ins.then_inc(s_scores, 1)
                    elif step[0] == "pv":
                        pb = (b - 1) % 4
                        pe.wait_ge(s_pt_lo, 3 * n)
                        v0, v1 = 2 * pb, 2 * pb + 1
                        mm3(turned[:, 0, :, :], v_hi[:, v0, :], v_lo[:, v0, :], pt_hi[:, 0, :, :],
                            pt_lo[:, 0, :, :]).then_inc(s_pv, 1)
                        mm3(turned[:, 1, :, :], v_hi[:, v0, :], v_lo[:, v0, :], pt_hi[:, 1, :, :],
                            pt_lo[:, 1, :, :], stop=False)
                        mm3(turned[:, 1, :, :], v_hi[:, v1, :], v_lo[:, v1, :], pt_hi[:, 2, :, :],
                            pt_lo[:, 2, :, :], start=False).then_inc(s_pv, 1)
                    elif step[0] == "out":
                        k = step[1]
                        tile = pe_ring_bank(pe)
                        pe.wait_ge(s_ot_lo, 2 * (n - 1) + k + 1)
                        if k == 0 and b == 1:
                            pe.wait_ge(s_wd, HEADS * (GROUPS * layer + g + 1))
                        for h in range(HEADS):
                            ins = mm3(tile, ot_hi[:, k, h, :], ot_lo[:, k, h, :], wd_hi[:, h, :],
                                      wd_lo[:, h, :], start=h == 0, stop=h == HEADS - 1)
                        pe_ring_done(ins)
                    elif step[0] == "v_turn":
                        tile = pe_ring_bank(pe, side=True)
                        pe.wait_ge(s_ring_free, pe_ring.turns + v_at[0])
                        for q in range(HALF // P):
                            ins = nc.tensor.transpose(tile[:, q * P:(q + 1) * P], vt[:, q * P:(q + 1) * P],
                                                      ident[:, :])
                        pe_ring_done(ins)
                    elif step[0] == "k_rms":
                        tile = pe_ring_bank(pe, side=True)
                        pe.wait_ge(s_sq_split, pe_sq.value() + 1)
                        row = pick[:, P - HEADS:2 * P - HEADS]
                        nc.tensor.matmul(tile, row, sq_lo[:, step[1], :], start=True, stop=False)
                        pe_ring_done(nc.tensor.matmul(tile, row, sq_hi[:, step[1], :], start=False, stop=True))
                    elif step[0] == "q_rms":
                        _, half, pair = step
                        tile = pe_ring_bank(pe, side=True)
                        pe_sq.up(3 if pair == 0 else 2)
                        pe.wait_ge(s_sq_split, pe_sq.value())
                        for j in range(2):
                            h = 2 * pair + j
                            part = (half + 1 + h) % 2
                            row = pick[:, P - h:2 * P - h]
                            nc.tensor.matmul(tile, row, sq_lo[:, part, :], start=j == 0, stop=False)
                            ins = nc.tensor.matmul(tile, row, sq_hi[:, part, :], start=False, stop=j == 1)
                        pe_ring_done(ins)
                    elif step[0] == "q_rms_turn":
                        tile = pe_ring_bank(pe, side=True)
                        half = step[1]
                        if b is not None:
                            pe.wait_ge(s_pt_lo, 3 * n)
                        else:
                            pe.wait_ge(s_ring_free, pe_ring.value() - 1)
                        hold(nc.tensor)
                        for q in range(HALF // P):
                            ins = nc.tensor.transpose(tile[:, q * ROWS:(q + 1) * ROWS],
                                                      sumsq[0:ROWS, half, q * P:(q + 1) * P],
                                                      ident[0:ROWS, 0:ROWS])
                        pe_ring_done(ins)
                    elif step[0] == "k_norm":
                        tile = pe_ring_bank(pe, side=True)
                        pe_roots.up()
                        pe.wait_ge(s_roots, pe_roots.value())
                        for q in range(HALF // P):
                            ins = nc.tensor.matmul(tile[:, q * P:(q + 1) * P],
                                                   root[:, step[1], q, HEADS:ROWS].to_broadcast([P, P]),
                                                   ident[:, :], start=True, stop=True)
                        pe_ring_done(ins)
                    elif step[0] == "transpose":
                        pe.wait_ge(s_prob, 2 * n + 1)
                        for h in range(HEADS):
                            ins = nc.tensor.transpose(turned[:, 0, h, :], p0[:, h, :], ident[:, :])
                        ins.then_inc(s_turned, 1)
                        pe.wait_ge(s_prob, 2 * n + 2)
                        for k in range(2):
                            if k == 1:
                                pe.wait_ge(s_ring_free, pe_ring.turns + pe_ring.last[SIDE])
                            for h in range(HEADS):
                                ins = nc.tensor.transpose(turned[:, 1 + k, h, :],
                                                          p1v[:, h, k * P:(k + 1) * P], ident[:, :])
                            ins.then_inc(s_turned, 1)

            def act_steps(act, steps, g, b):
                n = None if b is None else S0 + 4 * g + b
                for step in steps:
                    if step[0] == "pt_split":
                        for j in range(3):
                            act.wait_ge(s_turned, 3 * (n - 1) + j + 1)
                            nc.scalar.copy(pt_hi[:, j, :, :], turned[:, j, :, :]).then_inc(s_pt_hi, 1)
                    elif step[0] == "exp":
                        k = step[1]
                        sc, pr = ((scores0, p0), (scores1, p1))[k]
                        act.wait_ge(s_max, 2 * n + k + 1)
                        for h in range(HEADS):
                            scale = root[:, b // 2, 2 * (b % 2) + k, h:h + 1] if rms else SCALE
                            ins = nc.scalar.activation(pr[:, h, :], sc[:, h, :], ACT.Exp, bias=bias[:, k, h:h + 1],
                                                       scale=scale, accum_out=sums[:, k, h:h + 1])
                        ins.then_inc(s_exp, 1)
                    elif step[0] == "pv":
                        for k in range(2):
                            act.wait_ge(s_pv, 2 * (n - 1) + k + 1)
                            nc.scalar.copy(ot_hi[:, k, :, :], turned[:, k, :, :]).then_inc(s_ot_hi, 1)
                    elif step[0] == "tile":
                        _, X, half, ahead = step
                        tile = act_ring_tile(act)
                        tile_b = tile.rearrange("p (b s) -> p b s", b=2)
                        cols = slice(half * HALF, (half + 1) * HALF)
                        if X == V:
                            continue
                        if rms:
                            if not isinstance(act_sq.value(), int) or act_sq.value() > 0:
                                act.wait_ge(s_sq_split, act_sq.value())
                            nc.scalar.activation(sq[:, :], tile, ACT.Square).then_inc(s_sq, 1)
                            act_sq.up()
                        if X == K:
                            if rms:
                                continue
                            nc.scalar.copy(kt_f[:, 2 * half:2 * half + 2, :], tile_b[:, :, 0:P])
                            act_ring_hi(nc.scalar.copy(kt_hi[:, cols], tile))
                        else:
                            h = X - Q0
                            nc.scalar.copy(qt_f[:, h, 2 * half:2 * half + 2, :], tile_b[:, :, 0:P])
                            act_ring_hi(nc.scalar.copy(qt_hi[:, h, cols], tile))
                    elif step[0] == "v_turn":
                        tile = act_ring_tile(act, side=True)
                        act_ring_hi(nc.scalar.copy(v_hi[:, 4 * step[1]:4 * step[1] + 4, :],
                                                   tile.rearrange("p (t d) -> p t d", d=HD)))
                    elif step[0] in ("k_rms", "q_rms", "q_rms_turn", "k_norm", "out"):
                        act_ring.take(side=step[0] != "out")

            def dve_steps(dve, steps, g, b):
                n = None if b is None else S0 + 4 * g + b
                for step in steps:
                    if step[0] == "pt_split":
                        for j in range(3):
                            dve.wait_ge(s_pt_hi, 3 * (n - 1) + j + 1)
                            nc.vector.tensor_tensor(pt_lo[:, j, :, :], turned[:, j, :, :],
                                                    as_f32(pt_hi[:, j, :, :]), ALU.subtract).then_inc(s_pt_lo, 1)
                    elif step[0] == "mask":
                        dve.wait_ge(s_scores, n + 1)
                        if rms:
                            half, t = b // 2, 2 * (b % 2)
                            for h in range(HEADS):
                                nc.vector.scalar_tensor_tensor(
                                    scores0[:, h, :], rel[:, 0:P], q_slope[:, half, t, h:h + 1],
                                    scores0[:, h, :], ALU.mult, ALU.add)
                            for h in range(HEADS):
                                ins = nc.vector.scalar_tensor_tensor(
                                    scores1[:, h, :], rel[:, P:P + SEQ], q_slope[:, half, t + 1, h:h + 1],
                                    scores1[:, h, :], ALU.mult, ALU.add)
                        else:
                            see = tri[:, :].unsqueeze(1).to_broadcast([P, HEADS, P])
                            nc.vector.tensor_tensor(scores0[:, :, :], scores0[:, :, :], see, ALU.add)
                            ins = nc.vector.tensor_tensor(scores1[:, :, P:SEQ], scores1[:, :, P:SEQ], see, ALU.add)
                        dve_link(ins)
                    elif step[0] == "max":
                        k = step[1]
                        sc = (scores0, scores1)[k]
                        dve_link(nc.vector.tensor_reduce(negmax[:, k, :], sc[:, :, :], AX.X, ALU.max, negate=True))
                        if rms:
                            ins = nc.vector.tensor_tensor(bias[:, k, :], negmax[:, k, :],
                                                          root[:, b // 2, 2 * (b % 2) + k, 0:HEADS], ALU.mult)
                        else:
                            ins = nc.vector.tensor_scalar(bias[:, k, :], negmax[:, k, :], SCALE, None, ALU.mult)
                        ins.then_inc(s_max, 1)
                    elif step[0] == "normalise":
                        k = step[1]
                        pr, width = ((p0, P), (p1, SEQ))[k]
                        dve.wait_ge(s_exp, 2 * n + k + 1)
                        dve_link(nc.vector.reciprocal(rsum[:, k, :], sums[:, k, :]))
                        nc.vector.tensor_tensor(pr[:, :, :], pr[:, :, :],
                                                rsum[:, k, :].unsqueeze(2).to_broadcast([P, HEADS, width]),
                                                ALU.mult).then_inc(s_prob, 1)
                    elif step[0] == "pv":
                        for k in range(2):
                            dve.wait_ge(s_ot_hi, 2 * (n - 1) + k + 1)
                            nc.vector.tensor_tensor(ot_lo[:, k, :, :], turned[:, k, :, :],
                                                    as_f32(ot_hi[:, k, :, :]), ALU.subtract).then_inc(s_ot_lo, 1)
                    elif step[0] == "out":
                        tile = dve_ring_tile(dve)
                        t = 2 * ((b - 1) % 4) + step[1]
                        dve_ring_free(nc.vector.tensor_tensor(x[:, t, :], x[:, t, :], tile, ALU.add))
                    elif step[0] == "tile":
                        _, X, half, ahead = step
                        cols = slice(half * HALF, (half + 1) * HALF)
                        if X == V:
                            tile = dve_ring_tile(dve)
                            dve_ring_free(nc.vector.tensor_copy(vt[:, :], tile))
                        elif X == K and rms:
                            tile = dve_ring_tile(dve)
                            dve_sq.up()
                            dve.wait_ge(s_sq, dve_sq.value())
                            dve_ring_free(nc.vector.tensor_scalar(k_raw[:, half, :], tile, norm_cols[:, 2:3], None,
                                                                  ALU.mult))
                        else:
                            if rms:
                                dve_sq.up()
                            tile = dve_ring_tile(dve, after_hi=True)
                            hi, lo = (kt_hi[:, cols], kt_lo[:, cols]) if X == K else \
                                (qt_hi[:, X - Q0, cols], qt_lo[:, X - Q0, cols])
                            dve_ring_free(nc.vector.tensor_tensor(lo, tile, as_f32(hi), ALU.subtract))
                    elif step[0] == "v_turn":
                        tile = dve_ring_tile(dve, after_hi=True, side=True)
                        at = slice(4 * step[1], 4 * step[1] + 4)
                        dve_ring_free(nc.vector.tensor_tensor(
                            v_lo[:, at, :], tile.rearrange("p (t d) -> p t d", d=HD), as_f32(v_hi[:, at, :]),
                            ALU.subtract))
                    elif step[0] == "k_rms":
                        tile = dve_ring_tile(dve, side=True)
                        dve_ring_free(nc.vector.tensor_copy(sumsq[0:ROWS, step[1], :], tile[0:ROWS, :]))
                    elif step[0] == "q_rms":
                        tile = dve_ring_tile(dve, side=True)
                        rows = sumsq[0:ROWS, step[1], :]
                        dve_ring_free(nc.vector.tensor_tensor(rows, rows, tile[0:ROWS, :], ALU.add))
                    elif step[0] == "q_rms_turn":
                        tile, half = dve_ring_tile(dve, side=True), step[1]
                        dve_ring_free(nc.vector.tensor_scalar(
                            ms[:, :, :], tile[:, 0:HALF // P * ROWS].rearrange("p (t h) -> p t h", h=ROWS),
                            1.0 / HD, RMS_EPS, ALU.mult, ALU.add))
                        dve.wait_ge(s_ring_free, dve_ring.value())
                        roots(root[:, half, :, :], ms[:, :, :], ms_tmp[:, :, :])
                        dve_link(nc.vector.reciprocal(ms[:, :, :], root[:, half, :, :]))
                        group = 0 if b is None else g if half == 1 else g + 1
                        of_group = slopes[:, bass.ds(HEADS * group, HEADS)] if not isinstance(group, int) else \
                            slopes[:, HEADS * group:HEADS * group + HEADS]
                        dve_roots.up()
                        nc.vector.tensor_tensor(q_slope[:, half, :, :], ms[:, :, 0:HEADS],
                                                of_group.unsqueeze(1).to_broadcast([P, HALF // P, HEADS]),
                                                ALU.mult).then_inc(s_roots, 1)
                        dve.wait_ge(s_roots, dve_roots.value())
                    elif step[0] == "k_norm":
                        tile = dve_ring_tile(dve, side=True)
                        keys = k_raw[:, step[1], :]
                        dve_ring_free(nc.vector.tensor_tensor(keys, keys, tile, ALU.mult))

            squares_used = [0]

            def pool_steps(pool, steps, g, b, refill=True):
                if b is not None:
                    squares_used[0] = pool_ring.n
                for step in steps:
                    before = pool_ring.n
                    if step[0] in RING_STEPS:
                        pool_ring.up()
                    if step[0] in ("k_rms", "q_rms"):
                        squares_used[0] = pool_ring.n
                    if step[0] == "tile":
                        _, X, half, ahead = step
                        if rms and X != V:
                            pool_sq.up()
                            part = half if X == K else (half + 1 + X - Q0) % 2
                            pool.wait_ge(s_sq, pool_sq.value())
                            if squares_used[0]:
                                pool.wait_ge(s_ring_full, pool_ring.turns + squares_used[0])
                            split_steps(pool, sq_hi[:, part, :], sq_lo[:, part, :], sq[:, :], s_sq_split)
                        if half == 1 and refill:
                            pool.wait_ge(s_ring_full, pool_ring.value())
                            pool_split_w(pool, X)
                    elif step[0] == "k_norm":
                        cols = slice(step[1] * HALF, (step[1] + 1) * HALF)
                        keys = k_raw[:, step[1], :]
                        pool.wait_ge(s_ring_free, pool_ring.value())
                        hold(nc.gpsimd)
                        nc.gpsimd.tensor_scalar(kt_f[:, 2 * step[1]:2 * step[1] + 2, :],
                                                keys.rearrange("p (b s) -> p b s", b=2)[:, :, 0:P],
                                                1.0, 0.0, ALU.mult, ALU.add)
                        split_steps(pool, kt_hi[:, cols], kt_lo[:, cols], keys, s_k_ready)
                    elif step == ("out", 1) and b == 0 and g is not GROUPS:
                        pool.wait_ge(s_ring_full, pool_ring.value())
                        pool_split_wd(pool)

            def sp_steps(sp, steps, g, b, refill=True):
                for step in steps:
                    if step[0] == "tile" and step[2] == 1 and refill:
                        sp_load_w(sp, step[1], GROUPS * layer + g + step[3] + 1)
                    elif step == ("out", 1) and b == 0 and g is not GROUPS:
                        sp_load_wd(sp, GROUPS * layer + g)

            def walk(eng, do, grows, pool_like=False):
                do(eng, lead_steps(rms), 0, None)
                do(eng, slot_steps(0, rms, True, first=True), 0, 0)
                last = GROUPS - 1

                def turn(g, **more):
                    for b in (1, 2, 3):
                        do(eng, slot_steps(b, rms, True), g, b, **more)
                    do(eng, slot_steps(0, rms, True), g + 1, 0, **more)

                if pool_like and layer == 1:
                    turn_loop(eng, last - 1, grows, turn)
                    turn(last - 1, refill=False)
                else:
                    turn_loop(eng, last, grows, turn)
                for b in (1, 2, 3):
                    do(eng, slot_steps(b, rms, False), last, b)
                do(eng, tail_steps(), GROUPS, 0)

            def pe(eng):
                walk(eng, pe_steps, [(pe_ring, ring_turn), (pe_sq, 10 * rms), (pe_roots, 2 * rms)])

            def act(eng):
                walk(eng, act_steps, [(act_ring, ring_turn), (act_hi, 12 - 2 - 2 * rms + 2),
                                      (act_sq, 10 * rms)])

            def dve(eng):
                walk(eng, dve_steps, [(dve_ring, ring_turn), (dve_hi, 12 - 2 - 2 * rms + 2),
                                      (dve_chain, 4 * (3 + 2) + 24 * rms),
                                      (dve_sq, 10 * rms), (dve_roots, 2 * rms)])

            def pool(eng):
                if layer == 0:
                    for X in range(WT):
                        pool_split_w(eng, X)
                pool_split_wd(eng)
                walk(eng, pool_steps, [(pool_ring, ring_turn), (pool_chain, WT + HEADS + 12 * rms),
                                       (pool_sq, 10 * rms), (pool_w, 2), (pool_wd, 2)], True)

            def sp(eng):
                if layer == 0:
                    for X in range(WT):
                        sp_load_w(eng, X, 0)
                sp_load_wd(eng, GROUPS * layer)
                walk(eng, sp_steps, [(sp_w, WT), (sp_wd, HEADS)], True)

            return pe, act, dve, pool, sp

        pool_wd, sp_wd = Tally(), Tally()

        def pool_split_w(pool, X):
            if X % 3 == 0:
                pool_w.up()
            pool.wait_ge(s_w_raw[X % 3], 16 * pool_w.value())
            split_steps(pool, w_hi[:, X, :, :], w_lo[:, X, :, :],
                        w_raw[:, X % 3, :].rearrange("p (c d) -> p c d", c=DC), s_w)

        def pool_split_wd(pool):
            for h in range(HEADS):
                if h % 2 == 0:
                    pool_wd.up()
                pool.wait_ge(s_wd_raw[h % 2], 16 * pool_wd.value())
                split_steps(pool, wd_hi[:, h, :], wd_lo[:, h, :], wd_raw[:, h % 2, :], s_wd)

        def sp_load_w(sp, X, group):
            if not (isinstance(sp_w.turns, int) and sp_w.n < 3):
                sp.wait_ge(s_w, sp_w.value() - 2)
            sp_w.up()
            sp.dma_start(w_raw[:, X % 3, :], w_attn[group, X, :, :]).then_inc(s_w_raw[X % 3], 16)

        def sp_load_wd(sp, group):
            for h in range(HEADS):
                if not (isinstance(sp_wd.turns, int) and sp_wd.n < 2):
                    sp.wait_ge(s_wd, sp_wd.value() - 1)
                sp_wd.up()
                sp.dma_start(wd_raw[:, h % 2, :], w_dense[group, h, :, :]).then_inc(s_wd_raw[h % 2], 16)

        s_load0 = [sem(f"s_lora_raw{i}") for i in range(2)]
        s_a = sem("s_a")
        s_ab = sem("s_ab")
        s_down = sem("s_down")
        s_score = sem("s_score")
        s_gate_exp = sem("s_gate_exp")
        s_gated = sem("s_gated")
        s_gt = sem("s_gt")
        s_gt_hi = sem("s_gt_hi")
        s_gt_lo = sem("s_gt_lo")

        AW = EXPERTS + ER
        CUTS = [0, 320, 704, 1088]

        def experts(scope):
            a_hi = sb("a_hi", [P, DC, AW], F32R, scope)
            a_lo = sb("a_lo", [P, DC, AW], F32R, scope)
            b_hi = sb("b_hi", [P, EC, D], F32R, scope)
            b_lo = sb("b_lo", [P, EC, D], F32R, scope)
            hg = sb("hg", [P, ER], F32, scope)
            gt_hi = sb("gt_hi", [P, EC, P], F32R, scope)
            gt_lo = sb("gt_lo", [P, EC, P], F32R, scope)
            a_raw = sb("a_raw", [P, DC, AW], F32, scope)
            b_raw = a_raw[:, :, :].rearrange("p c e -> p (c e)")[:, 0:EC * D].rearrange("p (c d) -> p c d", d=D)
            score = sb("score", [P, EXPERTS], F32, scope)
            rest = sb("rest", [P, 2, EXPERTS], F32, scope)
            top = sb("top", [P, 2, 8], F32, scope)
            top_neg = sb("top_neg", [P, 1], F32, scope)
            gate = sb("gate", [P, EXPERTS], F32, scope)
            gsum = sb("gsum", [P, 2], F32, scope)
            banks = [scores1[:, 0:2, :], scores1[:, 2:4, :], scores0[:, :, :]]
            down = [v.rearrange("p a b -> p (a b)")[:, 0:CUTS[i + 1] - CUTS[i]] for i, v in enumerate(banks)]

            def sp(eng):
                eng.wait_ge(s_ring_free, attention_tiles[0])
                eng.dma_start(a_raw[:, :, 0:EXPERTS], lora_wr).then_inc(s_load0[0], 16)
                eng.dma_start(a_raw[:, :, EXPERTS:AW], lora_a).then_inc(s_load0[0], 16)
                eng.wait_ge(s_ab, DC)
                eng.dma_start(b_raw[:, :, :], lora_b).then_inc(s_load0[1], 16)

            def chunks():
                for c in range(DC):
                    yield a_raw[:, c, :], a_hi[:, c, :], a_lo[:, c, :], s_load0[0], 32
                for c in range(0, EC, 2):
                    yield (b_raw[:, c:c + 2, :], b_hi[:, c:c + 2, :], b_lo[:, c:c + 2, :], s_load0[1], 16)

            def act(eng):
                for raw, hi, _, landed, count in chunks():
                    eng.wait_ge(landed, count)
                    nc.scalar.copy(hi, raw).then_inc(s_a, 1)
                turned_hi(eng, 0)

                def pair(i, first=False, last=False):
                    for par in range(2):
                        t, more = 2 * i + par, not (last and par == 1)
                        eng.wait_ge(s_score, t + 1)
                        nc.scalar.activation(gate[:, :], score[:, :], ACT.Exp,
                                             bias=top_neg[:, :]).then_inc(s_gate_exp, 1)
                        for k in range(2):
                            eng.wait_ge(s_gt, 2 * t + k + 1)
                            nc.scalar.copy(gt_hi[:, 4 * k:4 * k + 4, :], turned[:, k, :, :]).then_inc(s_gt_hi, 1)
                        if not (first and par == 0):
                            act_ring.take()
                        if more:
                            turned_hi(eng, par + 1)
                pair(0, first=True)
                turn_loop(eng, NT // 2 - 2, [(act_ring, 4), (act_hi, 2)], lambda i: pair(i + 1))
                pair(NT // 2 - 1, last=True)
                act_ring.take()

            def turned_hi(eng, par):
                tile = act_ring_tile(eng)
                at = slice((par % 2) * P, (par % 2 + 1) * P)
                act_ring_hi(nc.scalar.copy(xt_hi[:, :, at], tile.rearrange("p (c q) -> p c q", c=DC)))

            def dve_tok(eng, t, par):
                xs = x[:, bass.ds(t, 1), :].rearrange("p a d -> p (a d)") if not isinstance(t, int) else x[:, t, :]
                hold(nc.vector)
                dve_link(nc.vector.bn_stats(bn[:, 0, :], xs))
                hold(nc.vector)
                dve_link(nc.vector.bn_aggr(mv[:, 0, :], bn[:, 0, :]))
                dve_link(nc.vector.tensor_scalar(var_eps[:, 0:1], mv[:, 0, 1:2], LN_EPS, None, ALU.add))
                roots(rstd[:, 0:1], var_eps[:, 0:1], newton[:, 0:1])
                nc.vector.tensor_scalar(xn[:, par, :], xs, mv[:, 0, 0:1], rstd[:, 0:1],
                                        ALU.subtract, ALU.mult).then_inc(s_xn, 1)

            def dve_turned_lo(eng, par):
                tile = dve_ring_tile(eng, after_hi=True)
                at = slice(par * P, (par + 1) * P)
                dve_ring_free(nc.vector.tensor_tensor(xt_lo[:, :, at], tile.rearrange("p (c q) -> p c q", c=DC),
                                                      as_f32(xt_hi[:, :, at]), ALU.subtract))

            def dve(eng):
                dve_tok(eng, 0, 0)
                for n, (raw, hi, lo, _, _) in enumerate(chunks()):
                    eng.wait_ge(s_a, n + 1)
                    nc.vector.tensor_tensor(lo, raw, as_f32(hi), ALU.subtract).then_inc(s_ab, 1)
                dve_turned_lo(eng, 0)

                def pair(i, first=False, last=False):
                    for par in range(2):
                        t, more = 2 * i + par, not (last and par == 1)
                        lead = first and par == 0
                        if more:
                            dve_tok(eng, t + 1, 1 - par)
                        eng.wait_ge(s_down, 3 * t + 1)
                        dve_link(nc.vector.tensor_copy(score[:, :], down[0][:, 0:EXPERTS]))
                        hold(nc.vector)
                        dve_link(nc.vector.max(top[:, 0, :], score[:, :]))
                        nc.vector.tensor_scalar(top_neg[:, :], top[:, 0, 0:1], -1.0, None,
                                                ALU.mult).then_inc(s_score, 1)
                        dve_link(nc.vector.match_replace(rest[:, 0, :], top[:, 0, :], score[:, :], TAKEN))
                        hold(nc.vector)
                        dve_link(nc.vector.max(top[:, 1, :], rest[:, 0, :]))
                        hold(nc.vector)
                        dve_link(nc.vector.match_replace(rest[:, 1, :], top[:, 1, :], rest[:, 0, :], TAKEN))
                        dve_link(nc.vector.tensor_scalar(rest[:, 0, :], rest[:, 1, :], TAKEN, None, ALU.is_equal))
                        eng.wait_ge(s_gate_exp, t + 1)
                        dve_link(nc.vector.tensor_tensor(gate[:, :], gate[:, :], rest[:, 0, :], ALU.mult))
                        dve_link(nc.vector.tensor_reduce(gsum[:, 0:1], gate[:, :], AX.X, ALU.add))
                        dve_link(nc.vector.reciprocal(gsum[:, 1:2], gsum[:, 0:1]))
                        dve_link(nc.vector.tensor_scalar(gate[:, :], gate[:, :], gsum[:, 1:2], LORA_SCALE,
                                                         ALU.mult, ALU.mult))
                        for k in range(3):
                            eng.wait_ge(s_down, 3 * t + k + 1)
                            skip = EXPERTS if k == 0 else 0
                            lo_col, hi_col = CUTS[k] - EXPERTS + skip, CUTS[k + 1] - EXPERTS
                            experts_of = slice(lo_col // RANK, hi_col // RANK)
                            count = (hi_col - lo_col) // RANK
                            nc.vector.tensor_tensor(
                                hg[:, lo_col:hi_col].rearrange("p (e r) -> p e r", r=RANK),
                                down[k][:, skip:].rearrange("p (e r) -> p e r", r=RANK),
                                gate[:, experts_of].unsqueeze(2).to_broadcast([P, count, RANK]),
                                ALU.mult).then_inc(s_gated, 1)
                        if not lead:
                            dve_add_out(eng, t - 1)
                        for k in range(2):
                            eng.wait_ge(s_gt_hi, 2 * t + k + 1)
                            nc.vector.tensor_tensor(gt_lo[:, 4 * k:4 * k + 4, :], turned[:, k, :, :],
                                                    as_f32(gt_hi[:, 4 * k:4 * k + 4, :]),
                                                    ALU.subtract).then_inc(s_gt_lo, 1)
                        if more:
                            dve_turned_lo(eng, 1 - par)
                pair(0, first=True)
                turn_loop(eng, NT // 2 - 2, [(dve_ring, 4), (dve_hi, 2), (dve_chain, 2 * 24)],
                          lambda i: pair(i + 1))
                pair(NT // 2 - 1, last=True)
                dve_add_out(eng, NT - 1)

            def dve_add_out(eng, t):
                tile = dve_ring_tile(eng)
                xs = x[:, bass.ds(t, 1), :].rearrange("p a d -> p (a d)") if not isinstance(t, int) else x[:, t, :]
                dve_ring_free(nc.vector.tensor_tensor(xs, xs, tile, ALU.add))

            def pe(eng, normed):
                pe_turn_normed(eng, normed + 1, xn[:, 0, :])

                def pair(i, first=False, last=False):
                    for par in range(2):
                        t, more = 2 * i + par, not (last and par == 1)
                        lead = first and par == 0
                        at = slice(par * P, (par + 1) * P)
                        if lead:
                            eng.wait_ge(s_ab, DC)
                            eng.wait_ge(s_ring_free, pe_ring.value())
                        else:
                            eng.wait_ge(s_gated, 3 * t)
                            eng.wait_ge(s_ring_free, pe_ring.value())
                        for k in range(3):
                            for c in range(DC):
                                ins = mm3(down[k], xt_hi[:, c, at], xt_lo[:, c, at],
                                          a_hi[:, c, CUTS[k]:CUTS[k + 1]], a_lo[:, c, CUTS[k]:CUTS[k + 1]],
                                          start=c == 0, stop=c == DC - 1)
                            ins.then_inc(s_down, 1)
                        if not lead:
                            pe_out(eng, t - 1)
                        for k in range(2):
                            eng.wait_ge(s_gated, 3 * t + (2 if k == 0 else 3))
                            for c in range(4):
                                ins = nc.tensor.transpose(turned[:, k, c, :],
                                                          hg[:, (4 * k + c) * P:(4 * k + c + 1) * P], ident[:, :])
                            ins.then_inc(s_gt, 1)
                        if more:
                            pe_turn_normed(eng, normed + t + 2, xn[:, 1 - par, :])
                pair(0, first=True)
                turn_loop(eng, NT // 2 - 2, [(pe_ring, 4)], lambda i: pair(i + 1))
                pair(NT // 2 - 1, last=True)
                pe_out(eng, NT - 1)

            def pe_out(eng, t):
                tile = pe_ring_bank(eng)
                if isinstance(t, int) and t == 0:
                    eng.wait_ge(s_ab, DC + EC // 2)
                eng.wait_ge(s_gt_lo, 2 * (t + 1))
                for c in range(EC):
                    ins = mm3(tile, gt_hi[:, c, :], gt_lo[:, c, :], b_hi[:, c, :], b_lo[:, c, :],
                              start=c == 0, stop=c == EC - 1)
                pe_ring_done(ins)

            return pe, act, dve, sp

        TILES = 6
        RAWS = 3
        LV_ACT = 6
        s_code = [sem(f"s_codes{i}") for i in range(RAWS)]
        s_bits = sem("s_bits")
        s_lv_act = sem("s_levels_act")
        s_lv_pool = sem("s_levels_pool")
        s_deq = sem("s_dequantised")
        s_wq_hi = sem("s_wq_hi")
        s_wq = sem("s_wq")
        s_gu = sem("s_gate_up")
        s_silu = sem("s_silu")
        s_h = sem("s_h")
        s_h_hi = sem("s_h_hi")
        s_h_lo = sem("s_h_lo")
        s_dn = sem("s_dn")
        s_added = sem("s_added")

        def nf4(scope):
            raw = sb("code_raw", [P, RAWS, D], I32, scope)
            am = sb("absmax_rows", [P, RAWS, D], F32, scope)
            bits = sb("bits", [P, 2, 4, D], I32, scope)
            lv = sb("lv", [P, 2, 8, D], F32, scope)
            deq = sb("deq", [P, TILES, D], F32, scope)
            wq_hi = w_hi[:, :, :, :].rearrange("p t c d -> p t (c d)")
            wq_lo = w_lo[:, :, :, :].rearrange("p t c d -> p t (c d)")
            sg = sb("sg", [P, 2, HALF], F32, scope)
            hf = sb("hf", [P, 2, HALF], F32, scope)
            h_hi = sb("h_hi", [P, 2, TOK], F32R, scope)
            h_lo = sb("h_lo", [P, 2, TOK], F32R, scope)
            steps_of = nf4_steps()
            gu = [(ring[:, 0, :], ring[:, 1, :]),
                  tuple(turned[:, k, :, :].rearrange("p a b -> p (a b)") for k in range(2))]
            dn = [scores1[:, 0:2, :].rearrange("p a b -> p (a b)"), scores1[:, 2:4, :].rearrange("p a b -> p (a b)"),
                  scores0[:, :, :].rearrange("p a b -> p (a b)"), turned[:, 2, :, :].rearrange("p a b -> p (a b)")]
            LAST = MT // 2 - 1

            def plan(i):
                more = not (isinstance(i, int) and i == LAST)
                s = [("unit", 0), ("deq", 0), ("split", 5, 0), ("unit", 1)]
                if more:
                    s += [("deq", 1), ("unit", 2), ("deq", 2), ("split", 0, 1), ("unit", 3), ("deq", 3),
                          ("split", 1, 1), ("split", 2, 1), ("down", 0), ("deq", 4), ("split", 3, 1),
                          ("down", 1), ("deq", 5), ("split", 4, 1)]
                else:
                    s += [("unit", 2), ("unit", 3), ("down", 0), ("down", 1)]
                return s

            lead = [("deq", 0), ("deq", 1), ("split", 0, 1), ("deq", 2), ("split", 1, 1), ("deq", 3),
                    ("split", 2, 1), ("deq", 4), ("split", 3, 1), ("deq", 5), ("split", 4, 1)]

            def walk(eng, do):
                do(eng, lead, -1)
                do(eng, plan(0), 0)
                with eng.Fori(1, LAST) as i:
                    do(eng, plan(i), i)
                do(eng, plan(LAST), LAST)

            def above(eng, s, v, low=1):
                if not isinstance(v, int) or v >= low:
                    eng.wait_ge(s, v)

            def exists(i, k):
                return not (isinstance(i, int) and i == LAST)

            def sp(eng):
                def load(eng, steps, i):
                    for step in steps:
                        if step[0] == "deq" and exists(i, step[1]):
                            k = step[1]
                            j = TILES * (i + 1) + k
                            m = 2 * (i + 1) + (k // 2 if k < 4 else k - 4)
                            kind = k % 2 if k < 4 else 2
                            above(eng, s_deq, j - RAWS + 1)
                            eng.dma_start(raw[:, k % RAWS, :], codes[m, kind, :, :]).then_inc(s_code[k % RAWS], 16)
                            for side in range(2):
                                eng.dma_start(am[64 * side:64 * side + 64, k % RAWS, :],
                                              absmax[m, kind, side, :].partition_broadcast(64)
                                              ).then_inc(s_code[k % RAWS], 16)
                eng.wait_ge(s_ring_free, attention_tiles[1])
                walk(eng, load)
                for t in range(NT):
                    eng.wait_ge(s_added, NT * LAST + t + 1)
                    eng.dma_start(out[t * P:(t + 1) * P, :], x[:, t, :]).then_inc(s_out, 16)
                eng.wait_ge(s_out, 16 * NT)

            def act(eng):
                def do(eng, steps, i):
                    for step in steps:
                        if step[0] == "unit":
                            u = 4 * i + step[1]
                            g_bank = gu[step[1] % 2][0]
                            eng.wait_ge(s_gu, 2 * u + 1)
                            above(eng, s_h, u - 1)
                            nc.scalar.activation(sg[:, step[1] % 2, :], g_bank, ACT.Silu).then_inc(s_silu, 1)
                            eng.wait_ge(s_h, u + 1)
                            mm, half = step[1] % 2, step[1] // 2
                            nc.scalar.copy(h_hi[:, mm, half * HALF:(half + 1) * HALF],
                                           hf[:, step[1] % 2, :]).then_inc(s_h_hi, 1)
                        elif step[0] == "deq" and exists(i, step[1]):
                            k = step[1]
                            j = TILES * (i + 1) + k
                            eng.wait_ge(s_bits, j + 1)
                            above(eng, s_deq, j - 1)
                            for q in range(LV_ACT):
                                low, dist = steps_of[q]
                                ins = nc.scalar.activation(lv[:, k % 2, q, :], bits[:, k % 2, 0, :], ACT.Copy,
                                                           bias=low, scale=dist)
                            ins.then_inc(s_lv_act, 1)
                        elif step[0] == "split":
                            k, j = step[1], TILES * (i + step[2]) + step[1]
                            eng.wait_ge(s_deq, j + 1)
                            slot_used(eng, i, k, step[2])
                            nc.scalar.copy(wq_hi[:, k, :], deq[:, k, :]).then_inc(s_wq_hi, 1)
                walk(eng, do)

            def slot_used(eng, i, k, ahead):
                if k in (0, 1):
                    above(eng, s_gu, 2 * (4 * i + 2) + 2)
                elif k in (2, 3):
                    above(eng, s_gu, 2 * (4 * i + 3) + 2)
                else:
                    above(eng, s_dn, NT * (i + ahead))

            def pool(eng):
                def do(eng, steps, i):
                    for step in steps:
                        if step[0] == "unit":
                            u = 4 * i + step[1]
                            mm, half = step[1] % 2, step[1] // 2
                            cols = slice(half * HALF, (half + 1) * HALF)
                            eng.wait_ge(s_h_hi, u + 1)
                            nc.gpsimd.tensor_tensor(h_lo[:, mm, cols], hf[:, step[1] % 2, :],
                                                    as_f32(h_hi[:, mm, cols]), ALU.subtract).then_inc(s_h_lo, 1)
                        elif step[0] == "deq" and exists(i, step[1]):
                            k = step[1]
                            j = TILES * (i + 1) + k
                            eng.wait_ge(s_bits, j + 1)
                            above(eng, s_deq, j - 1)
                            hold(nc.gpsimd)
                            nc.gpsimd.tensor_scalar(bits[:, k % 2, 3, :], raw[:, k % RAWS, :], -7.0, 0.0,
                                                    ALU.add, ALU.max)
                            for q in range(LV_ACT, 8):
                                low, dist = steps_of[q]
                                ins = nc.gpsimd.tensor_scalar(lv[:, k % 2, q, :], bits[:, k % 2, 0, :], dist, low,
                                                              ALU.mult, ALU.add)
                            ins.then_inc(s_lv_pool, 1)
                        elif step[0] == "split":
                            k, j = step[1], TILES * (i + step[2]) + step[1]
                            eng.wait_ge(s_wq_hi, j + 1)
                            nc.gpsimd.tensor_tensor(wq_lo[:, k, :], deq[:, k, :], as_f32(wq_hi[:, k, :]),
                                                    ALU.subtract).then_inc(s_wq, 1)
                walk(eng, do)

            def dve(eng):
                chain = dve_chain

                def do(eng, steps, i):
                    for step in steps:
                        if step[0] == "unit":
                            u = 4 * i + step[1]
                            eng.wait_ge(s_silu, u + 1)
                            eng.wait_ge(s_gu, 2 * u + 2)
                            above(eng, s_h_lo, u - 1)
                            nc.vector.tensor_tensor(hf[:, step[1] % 2, :], sg[:, step[1] % 2, :],
                                                    gu[step[1] % 2][1], ALU.mult).then_inc(s_h, 1)
                        elif step[0] == "deq":
                            k = step[1]
                            j = TILES * (i + 1) + k
                            def bit(b):
                                if exists(i, k):
                                    return nc.vector.tensor_scalar(bits[:, k % 2, b, :], raw[:, k % RAWS, :],
                                                                   1 << b, None, ALU.bitwise_and)
                            if exists(i, k):
                                eng.wait_ge(s_code[k % RAWS], 48 * (2 * (i + 1) + k // RAWS + 1))
                                bit(0).then_inc(s_bits, 1)
                            if isinstance(j, int) and j == 0:
                                bit(1)
                                dve_link(bit(2))
                            else:
                                select(eng, j - 1, k - 1, bit)
                        elif step[0] == "down":
                            for t in range(4 * step[1], 4 * step[1] + 4):
                                eng.wait_ge(s_dn, NT * i + t + 1)
                                nc.vector.tensor_tensor(x[:, t, :], x[:, t, :], dn[t % 4], ALU.add).then_inc(s_added, 1)

                def select(eng, j, k, bit):
                    par, slot = k % 2, k % TILES
                    above(eng, s_deq, j)
                    eng.wait_ge(s_lv_act, j + 1)
                    eng.wait_ge(s_lv_pool, j + 1)
                    hold(nc.vector)
                    for b, (into, other) in ((1, (lv[:, par, 0::2, :], lv[:, par, 1::2, :])),
                                             (2, (lv[:, par, 0::4, :], lv[:, par, 2::4, :])),
                                             (3, (lv[:, par, 0:1, :], lv[:, par, 4:5, :]))):
                        nc.vector.copy_predicated(
                            into, bits[:, par, b, :].unsqueeze(1).to_broadcast([P, 8 >> b, D]), other
                        ).then_inc(s_dve, 1)
                        chain.up()
                        if b < 3:
                            bit(b)
                        eng.wait_ge(s_dve, chain.value())
                        if b < 3:
                            hold(nc.vector)
                    above(eng, s_wq, j - TILES + 1)
                    nc.vector.tensor_tensor(deq[:, slot, :], lv[:, par, 0, :], am[:, k % RAWS, :],
                                            ALU.mult).then_inc(s_deq, 1)

                do(eng, lead, -1)
                do(eng, plan(0), 0)
                turn_loop(eng, LAST - 1, [(dve_chain, 3 * TILES)], lambda i: do(eng, plan(i + 1), i + 1))
                do(eng, plan(LAST), LAST)

            def pe(eng):
                eng.wait_ge(s_ring_free, pe_ring.value())

                def do(eng, steps, i):
                    for step in steps:
                        if step[0] == "unit":
                            k = step[1]
                            u, mm, half = 4 * i + k, k % 2, k // 2
                            cols = slice(half * HALF, (half + 1) * HALF)
                            above(eng, s_h, u - 1)
                            for kind in range(2):
                                w = 2 * mm + kind
                                if half == 0:
                                    eng.wait_ge(s_wq, TILES * i + w + 1)
                                for c in range(DC):
                                    at = slice(c * P, (c + 1) * P)
                                    ins = mm3(gu[k % 2][kind], wq_hi[:, w, at], wq_lo[:, w, at], xt_hi[:, c, cols],
                                              xt_lo[:, c, cols], start=c == 0, stop=c == DC - 1)
                                ins.then_inc(s_gu, 1)
                        elif step[0] == "down":
                            eng.wait_ge(s_h_lo, 4 * i + 2 * step[1] + 2)
                            if step[1] == 0:
                                eng.wait_ge(s_wq, TILES * i + TILES)
                            for t in range(4 * step[1], 4 * step[1] + 4):
                                above(eng, s_added, NT * i + t - 3)
                                for mm in range(2):
                                    at = slice(t * P, (t + 1) * P)
                                    ins = mm3(dn[t % 4], h_hi[:, mm, at], h_lo[:, mm, at], wq_hi[:, 4 + mm, :],
                                              wq_lo[:, 4 + mm, :], start=mm == 0, stop=mm == 1)
                                ins.then_inc(s_dn, 1)
                do(eng, plan(0), 0)
                with eng.Fori(1, LAST) as i:
                    do(eng, plan(i), i)
                do(eng, plan(LAST), LAST)

            return pe, act, dve, pool, sp

        attention_tiles = [0, 0]
        a_scope, b_scope, c_scope, d_scope = ExitStack(), ExitStack(), ExitStack(), ExitStack()
        with a_scope:
            pe_a, act_a, dve_a, pool_a, sp_a = attention(0, a_scope)
        with b_scope:
            pe_b, act_b, dve_b, sp_b = experts(b_scope)
        with c_scope:
            pe_c, act_c, dve_c, pool_c, sp_c = attention(1, c_scope)
        with d_scope:
            pe_d, act_d, dve_d, pool_d, sp_d = nf4(d_scope)

        block = ctx.enter_context(nc.Block())

        @block.tensor
        def _(pe):
            pe.wait_ge(s_ident, 2)
            pe_norm(pe, 0)
            pe_a(pe)
            attention_tiles[0] = pe_ring.n
            pe_b(pe, NT)
            pe_norm(pe, 2 * NT)
            pe.wait_ge(s_const, 2)
            pe_c(pe)
            attention_tiles[1] = pe_ring.n
            pe_norm(pe, 3 * NT)
            pe_d(pe)

        @block.scalar
        def _(act):
            act_norm(act)
            act_a(act)
            act_b(act)
            act_norm(act)
            act_c(act)
            act_norm(act)
            act_d(act)

        @block.vector
        def _(dve):
            def x_added(t):
                if t == 0:
                    dve.wait_ge(s_ring_free, dve_ring.value())

            dve_norm(dve, lambda t: dve.wait_ge(s_x[t], 16))
            dve.wait_ge(s_ident, 2)
            dve_a(dve)
            dve_b(dve)
            dve_norm(dve, x_added)
            dve.wait_ge(s_norm_w, 32)
            dve_link(nc.vector.tensor_scalar(norm_cols[:, 2:3], norm_cols[:, 0:1], norm_cols[:, 1:2], SCALE,
                                             ALU.mult, ALU.mult))
            dve.wait_ge(s_const, 3)
            dve_c(dve)
            dve_norm(dve, x_added)
            dve_d(dve)

        @block.gpsimd
        def _(pool):
            pool_link(nc.gpsimd.memset(ident[:, :], 0.0))
            pool_link(nc.gpsimd.memset(tri[:, :], 0.0))
            nc.gpsimd.affine_select(out=ident[:, :], in_=ident[:, :], compare_op=ALU.not_equal, fill=1.0,
                                    base=0, pattern=[[-1, P]], channel_multiplier=1).then_inc(s_ident, 1)
            nc.gpsimd.affine_select(out=tri[:, :], in_=tri[:, :], compare_op=ALU.is_ge, fill=MASKED,
                                    base=0, pattern=[[-1, P]], channel_multiplier=1).then_inc(s_ident, 1)
            pool_ring.up(NT)
            pool_a(pool)
            pool_ring.up(2 * NT + NT)
            for n, (col, value) in enumerate(((0, 0.0), (1, 1.0))):
                dst = (pick[:, :], ones_r[:, :])[n]
                pool_link(nc.gpsimd.memset(rel[:, 0:dst.shape[1]], value))
                pool_link(nc.gpsimd.tensor_scalar(dst, rel[:, 0:dst.shape[1]], 1.0, 0.0, ALU.mult, ALU.add))
            nc.gpsimd.tensor_scalar(pick[:, P:P + 1], rel[:, 0:1], 1.0, 0.0, ALU.mult, ALU.add).then_inc(s_const, 1)
            nc.gpsimd.tensor_scalar(ones_r[:, 0:1], rel[:, 0:1], 1.0, 0.0, ALU.mult, ALU.add).then_inc(s_const, 1)
            for i, slope in enumerate(alibi_slopes()):
                nc.gpsimd.memset(slopes[:, i:i + 1], slope)
            pool.wait_ge(s_const, 2)
            for base, cols in ((0, slice(0, P)), (-P, slice(P, P + SEQ))):
                part = rel[:, cols]
                width = cols.stop - cols.start
                pool_link(nc.gpsimd.iota(part, pattern=[[1, width]], base=base, channel_multiplier=-1,
                                         allow_small_or_imprecise_dtypes=True))
                last = nc.gpsimd.affine_select(out=part, in_=part, compare_op=ALU.is_ge, fill=MASKED,
                                               base=-base, pattern=[[-1, width]], channel_multiplier=1)
                if base == 0:
                    pool_link(last)
            last.then_inc(s_const, 1)
            pool_c(pool)
            pool_d(pool)

        @block.sync
        def _(sp):
            for t in range(NT):
                sp.dma_start(x[:, t, :], x_in[t * P:(t + 1) * P, :]).then_inc(s_x[t], 16)
            for i in range(2):
                sp.dma_start(norm_cols[:, i:i + 1], norm_w[i, :].rearrange("(p a) -> p a", a=1)).then_inc(s_norm_w, 16)
            sp_a(sp)
            sp_b(sp)
            sp_c(sp)
            sp_d(sp)


def kernel(L0_attn_q, L0_attn_w_qkv, L0_attn_w_dense, L0_ffn_A, L0_ffn_B, L0_ffn_Wr, L1_attn_Wq, L1_attn_Wk,
           L1_attn_Wv, L1_attn_Wo, L1_attn_q_norm_w, L1_attn_k_norm_w, L1_ffn_gate_q, L1_ffn_gate_absmax,
           L1_ffn_up_q, L1_ffn_up_absmax, L1_ffn_down_q, L1_ffn_down_absmax):
    import concourse.bacc as bacc
    from concourse.bass_utils import run_bass_kernel_spmd

    def attn_tiles(wq, wk, wv):
        q = np.asarray(wq).reshape(GROUPS, HEADS, HD, DC, P)
        k = np.asarray(wk).reshape(GROUPS, 1, HD, DC, P)
        v = np.asarray(wv).reshape(GROUPS, 1, HD, DC, P)
        tiles = np.concatenate([k, q, v], axis=1)
        return tiles.transpose(0, 1, 4, 3, 2).reshape(GROUPS, WT, P, DC * HD)

    def by_chunk(w):
        return np.asarray(w).T.reshape(DC, P, -1).transpose(1, 0, 2)

    def hidden_in(q):
        return np.asarray(q).reshape(MT, P, DC, P).transpose(0, 3, 2, 1).reshape(MT, P, D)

    def hidden_in_absmax(a):
        return np.asarray(a).reshape(MT, P, DC, 2).transpose(0, 3, 2, 1).reshape(MT, 2, D)

    qkv, nq, nk = np.asarray(L0_attn_w_qkv), GROUPS * HEADS * HD, GROUPS * HD
    arrays = {
        "x_in": np.asarray(L0_attn_q).reshape(TOK, D),
        "w_attn": np.concatenate([attn_tiles(qkv[:nq], qkv[nq:nq + nk], qkv[nq + nk:]),
                                  attn_tiles(L1_attn_Wq, L1_attn_Wk, L1_attn_Wv)]),
        "w_dense": np.concatenate([np.asarray(w).T.reshape(GROUPS, HEADS, HD, D)
                                   for w in (L0_attn_w_dense, L1_attn_Wo)]),
        "lora_a": by_chunk(np.asarray(L0_ffn_A).reshape(ER, D)),
        "lora_wr": by_chunk(L0_ffn_Wr),
        "lora_b": np.asarray(L0_ffn_B).transpose(0, 2, 1).reshape(EC, P, D).transpose(1, 0, 2),
        "norm_w": np.stack([np.asarray(L1_attn_q_norm_w), np.asarray(L1_attn_k_norm_w)]),
        "codes": np.stack([hidden_in(L1_ffn_gate_q), hidden_in(L1_ffn_up_q),
                           np.asarray(L1_ffn_down_q).T.reshape(MT, P, D)], axis=1),
        "absmax": np.stack([hidden_in_absmax(L1_ffn_gate_absmax), hidden_in_absmax(L1_ffn_up_absmax),
                            np.asarray(L1_ffn_down_absmax).reshape(D, MT, 2).transpose(1, 2, 0)], axis=1),
    }
    nc = bacc.Bacc("TRN2", target_bir_lowering=False, num_devices=1)
    arrays = {f"{n}_dram": np.ascontiguousarray(a) for n, a in arrays.items()}
    args = {n[:-5]: nc.dram_tensor(n, a.shape, mybir.dt.from_np(a.dtype), kind="ExternalInput").ap()
            for n, a in arrays.items()}
    out = nc.dram_tensor("out_dram", (TOK, D), F32, kind="ExternalOutput").ap()
    build(nc, out=out, **args)
    r = run_bass_kernel_spmd(nc, [arrays], core_ids=[0])
    return r.results[0]["out_dram"].reshape(BATCH, SEQ, D)
```

```python
import numpy as np

import concourse.bass as bass
from concourse import mybir
from contextlib import ExitStack

F32 = mybir.dt.float32
F32R = mybir.dt.float32r
I32 = mybir.dt.int32
ALU = mybir.AluOpType
ACT = mybir.ActivationFunctionType
AX = mybir.AxisListType

P = 128
BATCH, SEQ, D = 4, 256, 512
TOK = BATCH * SEQ
NT = TOK // P
DC = D // P
HALF = 512
GROUPS, HEADS = 8, 4
HD = 128
EXPERTS, RANK, TOPK = 64, 16, 16
ER = EXPERTS * RANK
EC = ER // P
FF = 1792
MT = FF // P
LN_EPS, RMS_EPS = 1e-5, 1e-6
MASKED = -1e30
TAKEN = -3e38
SCALE = float(np.float32(1.0) / np.sqrt(np.float32(HD)))
LORA_SCALE = 32.0 / RANK
K, Q0, Q1, Q2, Q3, V = range(6)
WT = 6

NF4 = np.array([-1.0, -0.6961928009986877, -0.5250730514526367, -0.39491748809814453,
                -0.28444138169288635, -0.18477343022823334, -0.09105003625154495, 0.0,
                0.07958029955625534, 0.16093020141124725, 0.24611230194568634, 0.33791524171829224,
                0.44070982933044434, 0.5626170039176941, 0.7229568362236023, 1.0], dtype=np.float32)


def nf4_steps():
    steps = []
    for j in range(8):
        low, high = NF4[2 * j], NF4[2 * j + 1]
        step = np.float32(high - low)
        for way in (np.float32(np.inf), np.float32(-np.inf)):
            s = step
            for _ in range(8):
                if np.float32(low + s) == high:
                    break
                s = np.nextafter(s, way)
            if np.float32(low + s) == high:
                break
        assert np.float32(low + s) == high
        steps.append((float(low), float(s)))
    return steps


def alibi_slopes():
    start = 2 ** (-2 ** (-(np.log2(GROUPS * HEADS) - 3)))
    return [float(np.float32(start * start ** i)) for i in range(GROUPS * HEADS)]


def slot_steps(b, rms, projects, first=False):
    half = 0 if b in (1, 2) else 1
    ahead = 0 if b == 0 else 1
    tiles = [K, Q0, Q1] if b in (1, 3) else [Q2, Q3, V]
    if not projects:
        tiles = []
    t = [("tile", x, half, ahead) for x in tiles]
    s = [] if first else [("pt_split",)]
    norms = [b - 2] if not projects and b >= 2 else []
    s += norm_begin(norms, "pool") if norms else []
    if projects or b == 1:
        s += [("scores", 0), ("mask", 0), ("max", 0, 0)] + t[0:1] + [("max", 1, 0)]
    s += [("exp", 0), ("normalise", 0)]
    s += t[1:2] + [("exp", 1)]
    roots = rms and b in (1, 3) and (projects or b == 1)
    if roots:
        s += [("q_rms_turn", 1 if b == 1 else 0)]
    s += [] if first else [("pv",)]
    if rms and tiles and tiles[0] == K:
        s += [("k_rms", half)]
    s += t[2:3] + [("normalise", 1)]
    ahead = not projects and b < 3
    if ahead and not roots:
        s += [("scores", 1)]
    s += [] if first else [("out", 0)]
    if ahead and not roots:
        s += [("mask", 1), ("max", 0, 1), ("max", 1, 1)]
    s += [("norm_write", batch, "act") for batch in norms]
    if tiles and tiles[-1] == V:
        s += [("v_turn", half)]
    if roots:
        s += [("k_norm", 1 if b == 1 else 0)]
    s += [] if first else [("out", 1)]
    if not projects:
        s += [("scores", 1), ("mask", 1), ("max", 0, 1), ("max", 1, 1)] if ahead and roots else []
        s += [("norm_turn", batch) for batch in norms]
    if rms and tiles:
        s += [("q_rms", half, 0 if tiles[0] == K else 1)]
    return s + [("transpose",)]


def norm_begin(batches, who):
    s = [("norm_stats", batches), ("norm_root", batches, who)]
    return s + ([("norm_write", batches[0], "dve")] if who == "dve" else [])


def lead_steps(rms):
    if rms:
        return norm_begin([3], "dve") + [
            ("tile", K, 0, 0), ("tile", V, 0, 0), ("tile", Q0, 0, 0), ("norm_turn", 3), ("k_rms", 0),
            ("tile", Q1, 0, 0), ("v_turn", 0), ("q_rms", 0, 0), ("tile", Q2, 0, 0), ("tile", Q3, 0, 0), ("q_rms", 0, 1),
            ("tile", K, 1, 0), ("q_rms_turn", 0), ("tile", Q0, 1, 0), ("k_norm", 0), ("k_rms", 1),
            ("tile", Q1, 1, 0), ("q_rms", 1, 0)]
    s = norm_begin([0, 1], "dve") + [("norm_turn", 0), ("norm_write", 1, "dve"), ("norm_turn", 1)]
    s += norm_begin([2, 3], "dve") + [("tile", K, 0, 0), ("norm_turn", 2), ("norm_write", 3, "dve")]
    s += [("tile", Q0, 0, 0), ("norm_turn", 3)] + [("tile", x, 0, 0) for x in (Q1, Q2, Q3, V)] + [("v_turn", 0)]
    return s + [("tile", x, 1, 0) for x in (K, Q0, Q1)]


def tail_steps():
    return [("pt_split",)] + norm_begin([2], "pool") + [("pv",), ("norm_write", 2, "act"), ("out", 0), ("out", 1),
                                                        ("norm_turn", 2)]


RING_STEPS = ("tile", "k_rms", "v_turn", "q_rms", "q_rms_turn", "k_norm", "out")
NORM_STEPS = ("norm_stats", "norm_root", "norm_write", "norm_turn")
SIDE = 2


class Tally:

    def __init__(self):
        self.turns, self.n = 0, 0

    def up(self, by=1):
        self.n += by

    def value(self):
        return self.turns + self.n


class Ring(Tally):

    def __init__(self):
        super().__init__()
        self.mains, self.last = 0, [0, 0, 0]

    def take(self, side=False):
        bank = SIDE if side else self.mains % 2
        before = self.last[bank]
        self.up()
        self.mains += not side
        self.last[bank] = self.n
        return bank, before


def turn_loop(eng, count, grows, body):
    with eng.Fori(0, count) as i:
        starts = [t.n for t, _ in grows]
        for t, by in grows:
            t.turns = i * by
        body(i)
    for (t, by), n in zip(grows, starts):
        assert t.n == n + by, (t.n - n, by)
        t.turns, t.n = 0, n + by * count
        if isinstance(t, Ring):
            t.last = [v + by * (count - 1) for v in t.last]


def build(nc, x_in, w_attn, w_dense, lora_a, lora_wr, lora_b, norm_w, codes, absmax, out):
    with ExitStack() as ctx:
        def sem(name):
            return ctx.enter_context(nc.semaphore(name))

        def sb(name, shape, dt=F32, scope=ctx):
            return scope.enter_context(nc.sbuf_tensor(name, shape, dt))

        def psum(name, shape):
            return ctx.enter_context(nc.psum_tensor(name, shape, F32))

        x = sb("x", [P, NT, D])
        xt_hi = sb("xt_hi", [P, DC, TOK], F32R)
        xt_lo = sb("xt_lo", [P, DC, TOK], F32R)
        ident = sb("ident", [P, P])
        xn = sb("xn", [P, 2, D])
        bn = sb("bn", [P, NT, 6])
        mv = sb("mv", [P, NT, 2])
        var_eps = sb("var_eps", [P, NT])
        rstd = sb("rstd", [P, NT])
        newton = sb("newton", [P, NT])
        shift = sb("shift", [P, NT])
        scores1 = psum("scores1", [P, HEADS, SEQ])
        scores0 = psum("scores0", [P, HEADS, P])
        turned = psum("turned", [P, 3, HEADS, P])
        ring = psum("ring", [P, 2, 512])

        s_x = [sem(f"s_x_loaded{t}") for t in range(NT)]
        s_ident = sem("s_ident")
        s_const = sem("s_const")
        s_norm_w = sem("s_norm_w")
        s_ring_full = sem("s_ring_full")
        s_ring_hi = sem("s_ring_hi")
        s_ring_free = sem("s_ring_free")
        s_xn = sem("s_xn")
        s_scores = sem("s_scores")
        s_max = sem("s_max")
        s_exp = sem("s_exp")
        s_prob = sem("s_prob")
        s_turned = sem("s_turned")
        s_pt_hi = sem("s_pt_hi")
        s_pt_lo = sem("s_pt_lo")
        s_pv = sem("s_pv")
        s_ot_hi = sem("s_ot_hi")
        s_ot_lo = sem("s_ot_lo")
        s_w_raw = [sem(f"s_w_raw{r}") for r in range(3)]
        s_wd_raw = [sem(f"s_wd_raw{r}") for r in range(2)]
        s_w = sem("s_w")
        s_wd = sem("s_wd")
        s_pool = sem("s_pool")
        s_dve = sem("s_dve")
        s_sq = sem("s_sq")
        s_sq_split = sem("s_sq_split")
        s_k_ready = sem("s_k_ready")
        s_roots = sem("s_roots")
        s_out = sem("s_out_stored")

        def mm3(o, l_hi, l_lo, r_hi, r_lo, start=True, stop=True):
            nc.tensor.matmul(o, l_lo, r_hi, start=start, stop=False)
            nc.tensor.matmul(o, l_hi, r_lo, start=False, stop=False)
            return nc.tensor.matmul(o, l_hi, r_hi, start=False, stop=stop)

        def as_f32(ap):
            return ap.bitcast(F32)

        pe_ring, act_ring, dve_ring, pool_ring = Ring(), Ring(), Ring(), Tally()
        ring_banks = [ring[:, 0, :], ring[:, 1, :], turned[:, 2, :, :].rearrange("p a b -> p (a b)")]
        act_hi, dve_hi, dve_chain, pool_chain = Tally(), Tally(), Tally(), Tally()
        act_sq, dve_sq, pool_sq, pe_sq = Tally(), Tally(), Tally(), Tally()
        pool_w, sp_w = Tally(), Tally()

        def hold(eng):
            eng.nop(nofuse=True)

        def dve_link(ins):
            ins.then_inc(s_dve, 1)
            dve_chain.up()
            nc.vector.wait_ge(s_dve, dve_chain.value())

        def pool_link(ins):
            ins.then_inc(s_pool, 1)
            pool_chain.up()
            nc.gpsimd.wait_ge(s_pool, pool_chain.value())

        def roots(eng, link, y, v, tmp):
            link(eng.tensor_scalar(y.bitcast(I32), v.bitcast(I32), -0.5, float(0x5F3759DF), ALU.mult, ALU.add))
            for _ in range(3):
                link(eng.tensor_tensor(tmp, y, y, ALU.mult))
                if eng is nc.vector:
                    link(eng.scalar_tensor_tensor(tmp, tmp, -0.5, v, ALU.mult, ALU.mult))
                    link(eng.scalar_tensor_tensor(y, tmp, 1.5, y, ALU.add, ALU.mult))
                else:
                    link(eng.tensor_tensor(tmp, tmp, v, ALU.mult))
                    link(eng.tensor_scalar(tmp, tmp, -0.5, 1.5, ALU.mult, ALU.add))
                    link(eng.tensor_tensor(y, y, tmp, ALU.mult))

        def pe_ring_bank(pe, side=False):
            bank, before = pe_ring.take(side)
            if not isinstance(pe_ring.turns, int) or before > 0:
                pe.wait_ge(s_ring_free, pe_ring.turns + before)
            return ring_banks[bank]

        def pe_ring_done(ins):
            ins.then_inc(s_ring_full, 1)

        def act_ring_tile(act, side=False):
            bank, _ = act_ring.take(side)
            act.wait_ge(s_ring_full, act_ring.value())
            return ring_banks[bank]

        def act_ring_hi(ins):
            ins.then_inc(s_ring_hi, 1)
            act_hi.up()

        def dve_ring_tile(dve, after_hi=False, side=False):
            bank, _ = dve_ring.take(side)
            if after_hi:
                dve_hi.up()
                dve.wait_ge(s_ring_hi, dve_hi.value())
            else:
                dve.wait_ge(s_ring_full, dve_ring.value())
            return ring_banks[bank]

        def dve_ring_free(ins):
            ins.then_inc(s_ring_free, 1)

        s_var = sem("s_var")
        s_shift = sem("s_shift")
        dve_normed, pe_normed, dve_vars, pool_vars, act_shifts = Tally(), Tally(), Tally(), Tally(), Tally()

        def dve_norm_stats(dve, batches):
            tiles = [t for b in batches for t in (2 * b, 2 * b + 1)]
            for t in tiles:
                if dve_normed.n < NT:
                    dve.wait_ge(s_x[t], 16)
                elif t == tiles[0]:
                    dve.wait_ge(s_ring_free, dve_ring.value())
                st = nc.vector.bn_stats(bn[:, t, :], x[:, t, :])
                dve_normed.up()
            dve_link(st)
            for t in tiles:
                st = nc.vector.bn_aggr(mv[:, t, :], bn[:, t, :])
            st.then_inc(s_var, 1)

        def norm_root(eng, link, batches):
            tiles = slice(2 * batches[0], 2 * batches[-1] + 2)
            link(eng.tensor_scalar(var_eps[:, tiles], mv[:, tiles, 1], LN_EPS, None, ALU.add))
            roots(eng, link, rstd[:, tiles], var_eps[:, tiles], newton[:, tiles])

        def dve_norm_write(b):
            for t in (2 * b, 2 * b + 1):
                nc.vector.tensor_scalar(xn[:, t % 2, :], x[:, t, :], mv[:, t, 0:1], rstd[:, t:t + 1],
                                  ALU.subtract, ALU.mult).then_inc(s_xn, 1)

        def dve_norm(dve, step):
            if step[0] == "norm_stats":
                dve_norm_stats(dve, step[1])
                dve_vars.up()
            elif step[0] == "norm_root" and step[2] == "dve":
                dve.wait_ge(s_var, dve_vars.value())
                norm_root(nc.vector, dve_link, step[1])
            elif step[0] == "norm_write" and step[2] == "dve":
                dve_norm_write(step[1])
            elif step[0] == "norm_turn":
                dve_norm_turn(dve, step[1])

        def pool_norm(pool, step):
            if step[0] == "norm_stats":
                pool_vars.up()
            elif step[0] == "norm_root" and step[2] == "pool":
                pool.wait_ge(s_var, pool_vars.value())
                norm_root(nc.gpsimd, pool_link, step[1])
                tiles = slice(2 * step[1][0], 2 * step[1][-1] + 2)
                pool_link(nc.gpsimd.tensor_tensor(shift[:, tiles], mv[:, tiles, 0], rstd[:, tiles], ALU.mult))
                nc.gpsimd.tensor_scalar(shift[:, tiles], shift[:, tiles], -1.0, 0.0, ALU.mult,
                                        ALU.add).then_inc(s_shift, 1)
            elif step[0] == "norm_turn":
                pool_ring.up(2)

        def pe_norm_turn(pe, b):
            for t in range(2 * b, 2 * b + 2):
                tile = pe_ring_bank(pe)
                pe_normed.up()
                pe.wait_ge(s_xn, pe_normed.value())
                for c in range(DC):
                    ins = nc.tensor.transpose(tile[:, c * P:(c + 1) * P], xn[:, t % 2, c * P:(c + 1) * P],
                                              ident[:, :])
                pe_ring_done(ins)
            xt_at[b] = pe_ring.n

        def act_norm(act, step):
            if step[0] == "norm_root" and step[2] == "pool":
                act_shifts.up()
            elif step[0] == "norm_write" and step[2] == "act":
                act.wait_ge(s_shift, act_shifts.value())
                act.wait_ge(s_ring_free, act_ring.value())
                for t in (2 * step[1], 2 * step[1] + 1):
                    nc.scalar.activation(xn[:, t % 2, :], x[:, t, :], ACT.Identity, bias=shift[:, t:t + 1],
                                         scale=rstd[:, t:t + 1]).then_inc(s_xn, 1)
            elif step[0] == "norm_turn":
                act_norm_turn(act, step[1])

        xt_at = [0] * BATCH

        def act_norm_turn(act, b):
            for t in range(2 * b, 2 * b + 2):
                tile = act_ring_tile(act)
                act_ring_hi(nc.scalar.copy(xt_hi[:, :, t * P:(t + 1) * P],
                                           tile.rearrange("p (c q) -> p c q", c=DC)))

        def dve_norm_turn(dve, b):
            for t in range(2 * b, 2 * b + 2):
                tile = dve_ring_tile(dve, after_hi=True)
                at = slice(t * P, (t + 1) * P)
                dve_ring_free(nc.vector.tensor_tensor(
                    xt_lo[:, :, at], tile.rearrange("p (c q) -> p c q", c=DC), as_f32(xt_hi[:, :, at]),
                    ALU.subtract))

        w_raw = sb("w_raw", [P, 3, DC * P])
        w_hi = sb("w_hi", [P, WT, DC, P], F32R)
        w_lo = sb("w_lo", [P, WT, DC, P], F32R)
        wd_raw = sb("wd_raw", [P, 2, D])
        wd_hi = sb("wd_hi", [P, HEADS, D], F32R)
        wd_lo = sb("wd_lo", [P, HEADS, D], F32R)
        tri = sb("tri", [P, P])
        pick = sb("pick", [P, 2 * P], F32R)
        rel = sb("rel", [P, SEQ + P])
        slopes = sb("slopes", [P, GROUPS * HEADS])
        norm_cols = sb("norm_cols", [P, 3])
        RING_TURN = [2 * WT + 2 + 2 * BATCH, 2 * WT + 2 + 2 * BATCH + 2 + 4 + 2 + 2]

        def split_steps(pool, dst_hi, dst_lo, src, sem_done):
            hold(nc.gpsimd)
            pool_link(nc.gpsimd.tensor_scalar(dst_hi, src, 1.0, 0.0, ALU.mult, ALU.add))
            nc.gpsimd.tensor_tensor(dst_lo, src, as_f32(dst_hi), ALU.subtract).then_inc(sem_done, 1)

        ROWS = HEADS + 1

        def attention(layer, scope):
            rms = layer == 1
            ring_turn = RING_TURN[layer]
            S0 = 32 * layer

            qt_hi = sb(f"qt_hi{layer}", [P, HEADS, TOK], F32R, scope)
            qt_lo = sb(f"qt_lo{layer}", [P, HEADS, TOK], F32R, scope)
            qt_f = sb(f"qt_f{layer}", [P, HEADS, BATCH, P], F32, scope)
            kt_hi = sb(f"kt_hi{layer}", [P, TOK], F32R, scope)
            kt_lo = sb(f"kt_lo{layer}", [P, TOK], F32R, scope)
            kt_f = sb(f"kt_f{layer}", [P, BATCH, P], F32, scope)
            v_hi = sb(f"v_hi{layer}", [P, NT, HD], F32R, scope)
            v_lo = sb(f"v_lo{layer}", [P, NT, HD], F32R, scope)
            p0 = sb(f"p0{layer}", [P, HEADS, P], F32, scope)
            p1 = sb(f"p1{layer}", [P, HEADS, SEQ], F32, scope)
            pt_hi = sb(f"pt_hi{layer}", [P, 3, HEADS, P], F32R, scope)
            pt_lo = sb(f"pt_lo{layer}", [P, 3, HEADS, P], F32R, scope)
            ot_hi = sb(f"ot_hi{layer}", [P, 2, HEADS, P], F32R, scope)
            ot_lo = sb(f"ot_lo{layer}", [P, 2, HEADS, P], F32R, scope)
            negmax = sb(f"negmax{layer}", [P, 2, HEADS], F32, scope)
            bias = sb(f"bias{layer}", [P, 2, HEADS], F32, scope)
            sums = sb(f"sums{layer}", [P, 2, HEADS], F32, scope)
            rsum = sb(f"rsum{layer}", [P, 2, HEADS], F32, scope)
            if rms:
                sq = sb("sq", [P, HALF], F32, scope)
                sq_hi = sb("sq_hi", [P, 2, HALF], F32R, scope)
                sq_lo = sb("sq_lo", [P, 2, HALF], F32R, scope)
                k_raw = sb("k_raw", [P, 2, HALF], F32, scope)
                sumsq = xn
                ms = sb("ms", [P, HALF // P, ROWS], F32, scope)
                ms_tmp = sb("ms_tmp", [P, HALF // P, ROWS], F32, scope)
                root = sb("root", [P, 2, HALF // P, ROWS], F32, scope)
                q_slope = sb("q_slope", [P, 2, HALF // P, HEADS], F32, scope)
            vt = sb(f"vt{layer}", [P, HALF], F32, scope)

            def q_slot(b, k):
                return slice(b * SEQ + k * P, b * SEQ + (k + 1) * P)

            pe_roots, dve_roots = Tally(), Tally()
            v_at = [0]

            def pe_steps(pe, steps, g, b):
                n = None if b is None else S0 + 4 * g + b
                pe_ring.last = [pe_ring.n] * 3
                for step in steps:
                    if step[0] == "tile":
                        _, X, half, ahead = step
                        tile = pe_ring_bank(pe)
                        if b is None and X == K:
                            pe.wait_ge(s_ring_free, xt_at[2 * half + 1])
                        if half == 0:
                            pe.wait_ge(s_w, WT * (GROUPS * layer + g + ahead) + X + 1)
                        cols = slice(half * HALF, (half + 1) * HALF)
                        for c in range(DC):
                            ins = mm3(tile, w_hi[:, X, c, :], w_lo[:, X, c, :], xt_hi[:, c, cols],
                                      xt_lo[:, c, cols], start=c == 0, stop=c == DC - 1)
                        pe_ring_done(ins)
                        if X == V:
                            v_at[0] = pe_ring.n
                    elif step[0] == "norm_turn":
                        pe_norm_turn(pe, step[1])
                    elif step[0] == "scores":
                        of, n_of = b + step[1], n + step[1]
                        if not isinstance(n_of, int) or n_of > S0:
                            pe.wait_ge(s_exp, 2 * n_of)
                        if of % 2 == 0 and rms:
                            pe.wait_ge(s_k_ready, 2 * g + of // 2 + 1)
                        for h in range(HEADS):
                            ins = nc.tensor.matmul(scores0[:, h, :], qt_f[:, h, of, :], kt_f[:, of, :],
                                                   start=True, stop=True)
                        keys = slice(of * SEQ, (of + 1) * SEQ)
                        for h in range(HEADS):
                            ins = mm3(scores1[:, h, :], qt_hi[:, h, q_slot(of, 1)], qt_lo[:, h, q_slot(of, 1)],
                                      kt_hi[:, keys], kt_lo[:, keys])
                        ins.then_inc(s_scores, 1)
                    elif step[0] == "pv":
                        pb = (b - 1) % 4
                        pe.wait_ge(s_pt_lo, 3 * n)
                        v0, v1 = 2 * pb, 2 * pb + 1
                        mm3(turned[:, 0, :, :], v_hi[:, v0, :], v_lo[:, v0, :], pt_hi[:, 0, :, :],
                            pt_lo[:, 0, :, :]).then_inc(s_pv, 1)
                        mm3(turned[:, 1, :, :], v_hi[:, v0, :], v_lo[:, v0, :], pt_hi[:, 1, :, :],
                            pt_lo[:, 1, :, :], stop=False)
                        mm3(turned[:, 1, :, :], v_hi[:, v1, :], v_lo[:, v1, :], pt_hi[:, 2, :, :],
                            pt_lo[:, 2, :, :], start=False).then_inc(s_pv, 1)
                    elif step[0] == "out":
                        k = step[1]
                        tile = pe_ring_bank(pe)
                        pe.wait_ge(s_ot_lo, 2 * (n - 1) + k + 1)
                        if k == 0 and b == 1:
                            pe.wait_ge(s_wd, HEADS * (GROUPS * layer + g + 1))
                        for h in range(HEADS):
                            ins = mm3(tile, ot_hi[:, k, h, :], ot_lo[:, k, h, :], wd_hi[:, h, :],
                                      wd_lo[:, h, :], start=h == 0, stop=h == HEADS - 1)
                        pe_ring_done(ins)
                    elif step[0] == "v_turn":
                        tile = pe_ring_bank(pe, side=True)
                        pe.wait_ge(s_ring_free, pe_ring.turns + v_at[0])
                        for q in range(HALF // P):
                            ins = nc.tensor.transpose(tile[:, q * P:(q + 1) * P], vt[:, q * P:(q + 1) * P],
                                                      ident[:, :])
                        pe_ring_done(ins)
                    elif step[0] == "k_rms":
                        tile = pe_ring_bank(pe, side=True)
                        pe.wait_ge(s_sq_split, pe_sq.value() + 1)
                        row = pick[:, P - HEADS:2 * P - HEADS]
                        nc.tensor.matmul(tile, row, sq_lo[:, step[1], :], start=True, stop=False)
                        pe_ring_done(nc.tensor.matmul(tile, row, sq_hi[:, step[1], :], start=False, stop=True))
                    elif step[0] == "q_rms":
                        _, half, pair = step
                        tile = pe_ring_bank(pe, side=True)
                        pe_sq.up(3 if pair == 0 else 2)
                        pe.wait_ge(s_sq_split, pe_sq.value())
                        for j in range(2):
                            h = 2 * pair + j
                            part = (half + 1 + h) % 2
                            row = pick[:, P - h:2 * P - h]
                            nc.tensor.matmul(tile, row, sq_lo[:, part, :], start=j == 0, stop=False)
                            ins = nc.tensor.matmul(tile, row, sq_hi[:, part, :], start=False, stop=j == 1)
                        pe_ring_done(ins)
                    elif step[0] == "q_rms_turn":
                        tile = pe_ring_bank(pe, side=True)
                        half = step[1]
                        if b is not None:
                            pe.wait_ge(s_pt_lo, 3 * n)
                        else:
                            pe.wait_ge(s_ring_free, pe_ring.value() - 1)
                        hold(nc.tensor)
                        for q in range(HALF // P):
                            ins = nc.tensor.transpose(tile[:, q * ROWS:(q + 1) * ROWS],
                                                      sumsq[0:ROWS, half, q * P:(q + 1) * P],
                                                      ident[0:ROWS, 0:ROWS])
                        pe_ring_done(ins)
                    elif step[0] == "k_norm":
                        tile = pe_ring_bank(pe, side=True)
                        pe_roots.up()
                        pe.wait_ge(s_roots, pe_roots.value())
                        for q in range(HALF // P):
                            ins = nc.tensor.matmul(tile[:, q * P:(q + 1) * P],
                                                   root[:, step[1], q, HEADS:ROWS].to_broadcast([P, P]),
                                                   ident[:, :], start=True, stop=True)
                        pe_ring_done(ins)
                    elif step[0] == "transpose":
                        pe.wait_ge(s_prob, 2 * n + 1)
                        for h in range(HEADS):
                            ins = nc.tensor.transpose(turned[:, 0, h, :], p0[:, h, :], ident[:, :])
                        ins.then_inc(s_turned, 1)
                        pe.wait_ge(s_prob, 2 * n + 2)
                        for k in range(2):
                            if k == 1:
                                pe.wait_ge(s_ring_free, pe_ring.turns + pe_ring.last[SIDE])
                            for h in range(HEADS):
                                ins = nc.tensor.transpose(turned[:, 1 + k, h, :],
                                                          p1[:, h, k * P:(k + 1) * P], ident[:, :])
                            ins.then_inc(s_turned, 1)

            def act_steps(act, steps, g, b):
                n = None if b is None else S0 + 4 * g + b
                for step in steps:
                    if step[0] == "pt_split":
                        for j in range(3):
                            act.wait_ge(s_turned, 3 * (n - 1) + j + 1)
                            nc.scalar.copy(pt_hi[:, j, :, :], turned[:, j, :, :]).then_inc(s_pt_hi, 1)
                    elif step[0] in NORM_STEPS:
                        act_norm(act, step)
                    elif step[0] == "exp":
                        k = step[1]
                        sc, pr = ((scores0, p0), (scores1, p1))[k]
                        act.wait_ge(s_max, 2 * n + k + 1)
                        for h in range(HEADS):
                            scale = root[:, b // 2, 2 * (b % 2) + k, h:h + 1] if rms else SCALE
                            ins = nc.scalar.activation(pr[:, h, :], sc[:, h, :], ACT.Exp, bias=bias[:, k, h:h + 1],
                                                       scale=scale, accum_out=sums[:, k, h:h + 1])
                        ins.then_inc(s_exp, 1)
                    elif step[0] == "pv":
                        for k in range(2):
                            act.wait_ge(s_pv, 2 * (n - 1) + k + 1)
                            nc.scalar.copy(ot_hi[:, k, :, :], turned[:, k, :, :]).then_inc(s_ot_hi, 1)
                    elif step[0] == "tile":
                        _, X, half, ahead = step
                        tile = act_ring_tile(act)
                        tile_b = tile.rearrange("p (b s) -> p b s", b=2)
                        cols = slice(half * HALF, (half + 1) * HALF)
                        if X == V:
                            continue
                        if rms:
                            if not isinstance(act_sq.value(), int) or act_sq.value() > 0:
                                act.wait_ge(s_sq_split, act_sq.value())
                            nc.scalar.activation(sq[:, :], tile, ACT.Square).then_inc(s_sq, 1)
                            act_sq.up()
                        if X == K:
                            if rms:
                                continue
                            nc.scalar.copy(kt_f[:, 2 * half:2 * half + 2, :], tile_b[:, :, 0:P])
                            act_ring_hi(nc.scalar.copy(kt_hi[:, cols], tile))
                        else:
                            h = X - Q0
                            nc.scalar.copy(qt_f[:, h, 2 * half:2 * half + 2, :], tile_b[:, :, 0:P])
                            act_ring_hi(nc.scalar.copy(qt_hi[:, h, cols], tile))
                    elif step[0] == "v_turn":
                        tile = act_ring_tile(act, side=True)
                        act_ring_hi(nc.scalar.copy(v_hi[:, 4 * step[1]:4 * step[1] + 4, :],
                                                   tile.rearrange("p (t d) -> p t d", d=HD)))
                    elif step[0] in ("k_rms", "q_rms", "q_rms_turn", "k_norm", "out"):
                        act_ring.take(side=step[0] != "out")

            def dve_steps(dve, steps, g, b):
                n = None if b is None else S0 + 4 * g + b
                for step in steps:
                    if step[0] == "pt_split":
                        for j in range(3):
                            dve.wait_ge(s_pt_hi, 3 * (n - 1) + j + 1)
                            nc.vector.tensor_tensor(pt_lo[:, j, :, :], turned[:, j, :, :],
                                                    as_f32(pt_hi[:, j, :, :]), ALU.subtract).then_inc(s_pt_lo, 1)
                    elif step[0] in NORM_STEPS:
                        dve_norm(dve, step)
                    elif step[0] == "mask":
                        of = b + step[1]
                        dve.wait_ge(s_scores, n + step[1] + 1)
                        if rms:
                            half, t = of // 2, 2 * (of % 2)
                            for h in range(HEADS):
                                nc.vector.scalar_tensor_tensor(
                                    scores0[:, h, :], rel[:, 0:P], q_slope[:, half, t, h:h + 1],
                                    scores0[:, h, :], ALU.mult, ALU.add)
                            for h in range(HEADS):
                                ins = nc.vector.scalar_tensor_tensor(
                                    scores1[:, h, :], rel[:, P:P + SEQ], q_slope[:, half, t + 1, h:h + 1],
                                    scores1[:, h, :], ALU.mult, ALU.add)
                        else:
                            see = tri[:, :].unsqueeze(1).to_broadcast([P, HEADS, P])
                            nc.vector.tensor_tensor(scores0[:, :, :], scores0[:, :, :], see, ALU.add)
                            ins = nc.vector.tensor_tensor(scores1[:, :, P:SEQ], scores1[:, :, P:SEQ], see, ALU.add)
                        dve_link(ins)
                    elif step[0] == "max":
                        k, of = step[1], b + step[2]
                        sc = (scores0, scores1)[k]
                        dve_link(nc.vector.tensor_reduce(negmax[:, k, :], sc[:, :, :], AX.X, ALU.max, negate=True))
                        if rms:
                            ins = nc.vector.tensor_tensor(bias[:, k, :], negmax[:, k, :],
                                                          root[:, of // 2, 2 * (of % 2) + k, 0:HEADS], ALU.mult)
                        else:
                            ins = nc.vector.tensor_scalar(bias[:, k, :], negmax[:, k, :], SCALE, None, ALU.mult)
                        ins.then_inc(s_max, 1)
                    elif step[0] == "normalise":
                        k = step[1]
                        pr, width = ((p0, P), (p1, SEQ))[k]
                        dve.wait_ge(s_exp, 2 * n + k + 1)
                        dve_link(nc.vector.reciprocal(rsum[:, k, :], sums[:, k, :]))
                        nc.vector.tensor_tensor(pr[:, :, :], pr[:, :, :],
                                                rsum[:, k, :].unsqueeze(2).to_broadcast([P, HEADS, width]),
                                                ALU.mult).then_inc(s_prob, 1)
                    elif step[0] == "pv":
                        for k in range(2):
                            dve.wait_ge(s_ot_hi, 2 * (n - 1) + k + 1)
                            nc.vector.tensor_tensor(ot_lo[:, k, :, :], turned[:, k, :, :],
                                                    as_f32(ot_hi[:, k, :, :]), ALU.subtract).then_inc(s_ot_lo, 1)
                    elif step[0] == "out":
                        tile = dve_ring_tile(dve)
                        t = 2 * ((b - 1) % 4) + step[1]
                        dve_ring_free(nc.vector.tensor_tensor(x[:, t, :], x[:, t, :], tile, ALU.add))
                    elif step[0] == "tile":
                        _, X, half, ahead = step
                        cols = slice(half * HALF, (half + 1) * HALF)
                        if X == V:
                            tile = dve_ring_tile(dve)
                            dve_ring_free(nc.vector.tensor_copy(vt[:, :], tile))
                        elif X == K and rms:
                            tile = dve_ring_tile(dve)
                            dve_sq.up()
                            dve.wait_ge(s_sq, dve_sq.value())
                            dve_ring_free(nc.vector.tensor_scalar(k_raw[:, half, :], tile, norm_cols[:, 2:3], None,
                                                                  ALU.mult))
                        else:
                            if rms:
                                dve_sq.up()
                            tile = dve_ring_tile(dve, after_hi=True)
                            hi, lo = (kt_hi[:, cols], kt_lo[:, cols]) if X == K else \
                                (qt_hi[:, X - Q0, cols], qt_lo[:, X - Q0, cols])
                            dve_ring_free(nc.vector.tensor_tensor(lo, tile, as_f32(hi), ALU.subtract))
                    elif step[0] == "v_turn":
                        tile = dve_ring_tile(dve, after_hi=True, side=True)
                        at = slice(4 * step[1], 4 * step[1] + 4)
                        dve_ring_free(nc.vector.tensor_tensor(
                            v_lo[:, at, :], tile.rearrange("p (t d) -> p t d", d=HD), as_f32(v_hi[:, at, :]),
                            ALU.subtract))
                    elif step[0] == "k_rms":
                        tile = dve_ring_tile(dve, side=True)
                        dve_ring_free(nc.vector.tensor_copy(sumsq[0:ROWS, step[1], :], tile[0:ROWS, :]))
                    elif step[0] == "q_rms":
                        tile = dve_ring_tile(dve, side=True)
                        rows = sumsq[0:ROWS, step[1], :]
                        dve_ring_free(nc.vector.tensor_tensor(rows, rows, tile[0:ROWS, :], ALU.add))
                    elif step[0] == "q_rms_turn":
                        tile, half = dve_ring_tile(dve, side=True), step[1]
                        dve_ring_free(nc.vector.tensor_scalar(
                            ms[:, :, :], tile[:, 0:HALF // P * ROWS].rearrange("p (t h) -> p t h", h=ROWS),
                            1.0 / HD, RMS_EPS, ALU.mult, ALU.add))
                        dve.wait_ge(s_ring_free, dve_ring.value())
                        roots(nc.vector, dve_link, root[:, half, :, :], ms[:, :, :], ms_tmp[:, :, :])
                        dve_link(nc.vector.reciprocal(ms[:, :, :], root[:, half, :, :]))
                        group = 0 if b is None else g if half == 1 else g + 1
                        of_group = slopes[:, bass.ds(HEADS * group, HEADS)] if not isinstance(group, int) else \
                            slopes[:, HEADS * group:HEADS * group + HEADS]
                        dve_roots.up()
                        nc.vector.tensor_tensor(q_slope[:, half, :, :], ms[:, :, 0:HEADS],
                                                of_group.unsqueeze(1).to_broadcast([P, HALF // P, HEADS]),
                                                ALU.mult).then_inc(s_roots, 1)
                        dve.wait_ge(s_roots, dve_roots.value())
                    elif step[0] == "k_norm":
                        tile = dve_ring_tile(dve, side=True)
                        keys = k_raw[:, step[1], :]
                        dve_ring_free(nc.vector.tensor_tensor(keys, keys, tile, ALU.mult))

            squares_used = [0]

            def pool_steps(pool, steps, g, b, refill=True):
                if b is not None:
                    squares_used[0] = pool_ring.n
                for step in steps:
                    if step[0] in RING_STEPS:
                        pool_ring.up()
                    elif step[0] in NORM_STEPS:
                        pool_norm(pool, step)
                    if step[0] in ("k_rms", "q_rms"):
                        squares_used[0] = pool_ring.n
                    if step[0] == "tile":
                        _, X, half, ahead = step
                        if rms and X != V:
                            pool_sq.up()
                            part = half if X == K else (half + 1 + X - Q0) % 2
                            pool.wait_ge(s_sq, pool_sq.value())
                            if squares_used[0]:
                                pool.wait_ge(s_ring_full, pool_ring.turns + squares_used[0])
                            split_steps(pool, sq_hi[:, part, :], sq_lo[:, part, :], sq[:, :], s_sq_split)
                        if half == 1 and refill:
                            pool.wait_ge(s_ring_full, pool_ring.value())
                            pool_split_w(pool, X)
                    elif step[0] == "k_norm":
                        cols = slice(step[1] * HALF, (step[1] + 1) * HALF)
                        keys = k_raw[:, step[1], :]
                        pool.wait_ge(s_ring_free, pool_ring.value())
                        hold(nc.gpsimd)
                        nc.gpsimd.tensor_scalar(kt_f[:, 2 * step[1]:2 * step[1] + 2, :],
                                                keys.rearrange("p (b s) -> p b s", b=2)[:, :, 0:P],
                                                1.0, 0.0, ALU.mult, ALU.add)
                        split_steps(pool, kt_hi[:, cols], kt_lo[:, cols], keys, s_k_ready)
                    elif step == ("out", 1) and b == 0 and g is not GROUPS:
                        pool.wait_ge(s_ring_full, pool_ring.value())
                        pool_split_wd(pool)

            def sp_steps(sp, steps, g, b, refill=True):
                for step in steps:
                    if step[0] == "tile" and step[2] == 1 and refill:
                        sp_load_w(sp, step[1], GROUPS * layer + g + step[3] + 1)
                    elif step == ("out", 1) and b == 0 and g is not GROUPS:
                        sp_load_wd(sp, GROUPS * layer + g)

            def walk(eng, do, grows, pool_like=False):
                do(eng, lead_steps(rms), 0, None)
                do(eng, slot_steps(0, rms, True, first=True), 0, 0)
                last = GROUPS - 1

                def turn(g, **more):
                    for b in (1, 2, 3):
                        do(eng, slot_steps(b, rms, True), g, b, **more)
                    do(eng, slot_steps(0, rms, True), g + 1, 0, **more)

                if pool_like and layer == 1:
                    turn_loop(eng, last - 1, grows, turn)
                    turn(last - 1, refill=False)
                else:
                    turn_loop(eng, last, grows, turn)
                if do is pe_steps:
                    last_slots[layer] = pe_ring.n
                for b in (1, 2, 3):
                    do(eng, slot_steps(b, rms, False), last, b)
                do(eng, tail_steps(), GROUPS, 0)

            hi_turn = 2 * (WT - 1 - rms) + 2

            def pe(eng):
                walk(eng, pe_steps, [(pe_ring, ring_turn), (pe_sq, 10 * rms), (pe_roots, 2 * rms)])

            def act(eng):
                walk(eng, act_steps, [(act_ring, ring_turn), (act_hi, hi_turn),
                                      (act_sq, 10 * rms)])

            def dve(eng):
                walk(eng, dve_steps, [(dve_ring, ring_turn), (dve_hi, hi_turn),
                                      (dve_chain, 4 * (3 + 2) + 22 * rms),
                                      (dve_sq, 10 * rms), (dve_roots, 2 * rms)])

            def pool(eng):
                if layer == 0:
                    for X in range(WT):
                        pool_split_w(eng, X)
                else:
                    eng.wait_ge(s_ring_full, attention_starts[1])
                pool_split_wd(eng)
                walk(eng, pool_steps, [(pool_ring, ring_turn), (pool_chain, WT + HEADS + 12 * rms),
                                       (pool_sq, 10 * rms), (pool_w, 2), (pool_wd, 2)], True)

            def sp(eng):
                if layer == 0:
                    for X in range(WT):
                        sp_load_w(eng, X, 0)
                sp_load_wd(eng, GROUPS * layer)
                walk(eng, sp_steps, [(sp_w, WT), (sp_wd, HEADS)], True)

            return pe, act, dve, pool, sp

        pool_wd, sp_wd = Tally(), Tally()

        def pool_split_w(pool, X):
            if X % 3 == 0:
                pool_w.up()
            pool.wait_ge(s_w_raw[X % 3], 16 * pool_w.value())
            split_steps(pool, w_hi[:, X, :, :], w_lo[:, X, :, :],
                        w_raw[:, X % 3, :].rearrange("p (c d) -> p c d", c=DC), s_w)

        def pool_split_wd(pool):
            for h in range(HEADS):
                if h % 2 == 0:
                    pool_wd.up()
                pool.wait_ge(s_wd_raw[h % 2], 16 * pool_wd.value())
                split_steps(pool, wd_hi[:, h, :], wd_lo[:, h, :], wd_raw[:, h % 2, :], s_wd)

        def sp_load_w(sp, X, group):
            if not (isinstance(sp_w.turns, int) and sp_w.n < 3):
                sp.wait_ge(s_w, sp_w.value() - 2)
            sp_w.up()
            sp.dma_start(w_raw[:, X % 3, :], w_attn[group, X, :, :]).then_inc(s_w_raw[X % 3], 16)

        def sp_load_wd(sp, group):
            for h in range(HEADS):
                if not (isinstance(sp_wd.turns, int) and sp_wd.n < 2):
                    sp.wait_ge(s_wd, sp_wd.value() - 1)
                sp_wd.up()
                sp.dma_start(wd_raw[:, h % 2, :], w_dense[group, h, :, :]).then_inc(s_wd_raw[h % 2], 16)

        s_lora_raw = [sem(f"s_lora_raw{i}") for i in range(2)]
        s_split_hi = sem("s_split_hi")
        s_split = sem("s_split")
        s_spread = sem("s_spread")
        s_turned_scores = sem("s_turned_scores")
        s_top = sem("s_top")
        s_gate_exp = sem("s_gate_exp")
        s_gates = sem("s_gates")
        s_gates_turned = sem("s_gates_turned")
        s_gates_hi = sem("s_gates_hi")
        s_gates_lo = sem("s_gates_lo")
        s_ranks = sem("s_ranks")
        s_ranks_out = sem("s_ranks_out")
        s_spread_gates = sem("s_spread_gates")
        s_gated = sem("s_gated")
        s_gated_hi = sem("s_gated_hi")
        s_gated_lo = sem("s_gated_lo")

        AW = EXPERTS + ER
        UNITS = ER // 256

        def expert_steps():
            head = lambda b: [("scores", b), ("turn_scores", b)]
            ranks = lambda b: [("ranks", b, u) for u in range(UNITS)]
            gated = lambda b: [("turn_gates", b)] + [("gated", b, u) for u in range(UNITS)]
            s = [("split_a", 0)] + head(0) + [("split_a", p) for p in range(1, UNITS + 1)] + [("router", 0)]
            s += norm_begin([3], "pool") + ranks(0)[0:2] + [("norm_write", 3, "act")] + ranks(0)[2:4] + head(1)
            s += [("norm_turn", 3)]
            s += gated(0) + [("router", 1)] + [("split_b", p) for p in range(UNITS)] + ranks(1) + [("out", 0)]
            s += head(2) + gated(1) + [("router", 2)] + norm_begin([0], "pool") + ranks(2)
            s += [("norm_write", 0, "act"), ("out", 1), ("norm_turn", 0)] + head(3) + gated(2)
            s += [("router", 3)] + norm_begin([1], "pool") + ranks(3)
            s += [("norm_write", 1, "act"), ("out", 2), ("norm_turn", 1)] + gated(3) + norm_begin([2], "pool")
            s += [("norm_write", 2, "act"), ("out", 3), ("norm_turn", 2)]
            return s

        def experts(scope):
            a_hi = sb("a_hi", [P, DC, AW], F32R, scope)
            a_lo = sb("a_lo", [P, DC, AW], F32R, scope)
            b_hi = sb("b_hi", [P, EC, D], F32R, scope)
            b_lo = sb("b_lo", [P, EC, D], F32R, scope)
            ranks = sb("ranks", [P, EC, SEQ], F32, scope)
            spread = sb("spread", [EXPERTS, ER], F32R, scope)
            gates_hi = sb("gates_hi", [EXPERTS, SEQ], F32R, scope)
            gates_lo = sb("gates_lo", [EXPERTS, SEQ], F32R, scope)
            scores_t = sb("scores_t", [EXPERTS, SEQ], F32, scope)
            score = sb("score", [P, 2, EXPERTS], F32, scope)
            rest = sb("rest", [P, 2, 2, EXPERTS], F32, scope)
            top = sb("top", [P, 2, 2, 8], F32, scope)
            top_neg = sb("top_neg", [P, 2], F32, scope)
            gate = sb("gate", [P, 2, EXPERTS], F32, scope)
            gsum = sb("gsum", [P, 2], F32, scope)
            grec = sb("grec", [P, 2], F32, scope)
            sb("behind_attention", [P, 256], F32, scope)
            a_raw = sb("a_raw", [P, DC, AW], F32, scope)
            b_raw = a_raw[:, :, :].rearrange("p c e -> p (c e)")[:, 0:EC * D].rearrange("p (c d) -> p c d", d=D)
            gated_hi, gated_lo = (w[:, :, :].rearrange("p h d -> p (h d)").rearrange("p (c q) -> p c q", q=SEQ)
                                  for w in (wd_hi, wd_lo))
            rank_banks = [scores1[:, 0:2, :], scores1[:, 2:4, :]]
            gate_banks = [turned[:, k, :, :].rearrange("p a b -> p (a b)").rearrange("p (c q) -> p c q", q=SEQ)
                          for k in (1, 2)]

            def piece(step):
                p = step[1]
                if step[0] == "split_b":
                    at = slice(2 * p, 2 * p + 2)
                    return b_raw[:, at, :], b_hi[:, at, :], b_lo[:, at, :], s_lora_raw[1], UNITS + 1 + p + 1
                at = slice(EXPERTS + 256 * (p - 1), EXPERTS + 256 * p) if p else slice(0, EXPERTS)
                return a_raw[:, :, at], a_hi[:, :, at], a_lo[:, :, at], s_lora_raw[0], p + 1

            def sp(eng):
                eng.wait_ge(s_ring_full, last_slots[0])
                eng.dma_start(a_raw[:, :, 0:EXPERTS], lora_wr).then_inc(s_lora_raw[0], 16)
                eng.dma_start(a_raw[:, :, EXPERTS:AW], lora_a).then_inc(s_lora_raw[0], 16)
                eng.wait_ge(s_split, UNITS + 1)
                eng.dma_start(b_raw, lora_b).then_inc(s_lora_raw[1], 16)

            def pe(eng):
                scores_at = 0
                for step in expert_steps():
                    b = step[1]
                    if step[0] == "scores":
                        tokens = slice(b * SEQ, (b + 1) * SEQ)
                        tile = pe_ring_bank(eng)
                        if b == 0:
                            eng.wait_ge(s_split, 1)
                        eng.wait_ge(s_ring_free, xt_at[b])
                        for c in range(DC):
                            ins = mm3(tile[0:EXPERTS, 0:SEQ], a_hi[:, c, 0:EXPERTS], a_lo[:, c, 0:EXPERTS],
                                      xt_hi[:, c, tokens], xt_lo[:, c, tokens], start=c == 0, stop=c == DC - 1)
                        pe_ring_done(ins)
                        scores_at = pe_ring.n
                    elif step[0] == "turn_scores":
                        eng.wait_ge(s_ring_free, scores_at)
                        if b:
                            eng.wait_ge(s_top, b)
                        for t in range(2):
                            ins = nc.tensor.transpose(turned[:, 0, t, 0:EXPERTS], scores_t[:, t * P:(t + 1) * P],
                                                      ident[0:EXPERTS, 0:EXPERTS])
                        ins.then_inc(s_turned_scores, 1)
                    elif step[0] == "ranks":
                        u = step[2]
                        n = UNITS * b + u
                        tokens = slice(b * SEQ, (b + 1) * SEQ)
                        if n < UNITS:
                            eng.wait_ge(s_split, u + 2)
                        if n >= 2:
                            eng.wait_ge(s_ranks_out, n - 1)
                        for k in range(2):
                            at = EXPERTS + (2 * u + k) * P
                            for c in range(DC):
                                ins = mm3(rank_banks[u % 2][:, k, :], a_hi[:, c, at:at + P], a_lo[:, c, at:at + P],
                                          xt_hi[:, c, tokens], xt_lo[:, c, tokens], start=c == 0,
                                          stop=c == DC - 1)
                        ins.then_inc(s_ranks, 1)
                    elif step[0] == "turn_gates":
                        eng.wait_ge(s_gates, b + 1)
                        if b:
                            eng.wait_ge(s_gates_lo, b)
                        for t in range(2):
                            ins = nc.tensor.transpose(scores0[0:EXPERTS, t, :], gate[:, t, :], ident[:, :])
                        ins.then_inc(s_gates_turned, 1)
                    elif step[0] == "gated":
                        u = step[2]
                        n = UNITS * b + u
                        if n == 0:
                            eng.wait_ge(s_spread, 1)
                        eng.wait_ge(s_gates_lo, b + 1)
                        if n >= 2:
                            eng.wait_ge(s_gated, n - 1)
                        for k in range(2):
                            cols = slice((2 * u + k) * P, (2 * u + k + 1) * P)
                            nc.tensor.matmul(gate_banks[u % 2][:, k, :], spread[:, cols], gates_lo[:, :],
                                             start=True, stop=False)
                            ins = nc.tensor.matmul(gate_banks[u % 2][:, k, :], spread[:, cols], gates_hi[:, :],
                                                   start=False, stop=True)
                        ins.then_inc(s_spread_gates, 1)
                    elif step[0] == "out":
                        if b == 0:
                            eng.wait_ge(s_split, 2 * UNITS + 1)
                        eng.wait_ge(s_gated_lo, UNITS * (b + 1))
                        for t in range(2):
                            tile = pe_ring_bank(eng)
                            at = slice(t * P, (t + 1) * P)
                            for c in range(EC):
                                ins = mm3(tile, gated_hi[:, c, at], gated_lo[:, c, at], b_hi[:, c, :],
                                          b_lo[:, c, :], start=c == 0, stop=c == EC - 1)
                            pe_ring_done(ins)
                    elif step[0] == "norm_turn":
                        pe_norm_turn(eng, b)

            def act(eng):
                out_at = 0
                for step in expert_steps():
                    b = step[1]
                    if step[0] in ("split_a", "split_b"):
                        raw, hi, _, landed, count = piece(step)
                        if count == 1:
                            eng.wait_ge(s_ring_free, attention_tiles[0])
                        eng.wait_ge(landed, 32 if landed is s_lora_raw[0] else 16)
                        nc.scalar.copy(hi, raw).then_inc(s_split_hi, 1)
                    elif step[0] == "scores":
                        act_ring.take()
                    elif step[0] == "router":
                        eng.wait_ge(s_top, b + 1)
                        if b:
                            eng.wait_ge(s_gates_turned, b)
                        for t in range(2):
                            ins = nc.scalar.activation(gate[:, t, :], score[:, t, :], ACT.Exp,
                                                       bias=top_neg[:, t:t + 1])
                        ins.then_inc(s_gate_exp, 1)
                    elif step[0] == "ranks":
                        n = UNITS * b + step[2]
                        eng.wait_ge(s_ranks, n + 1)
                        if n == UNITS // 2:
                            eng.wait_ge(s_spread, 1)
                        if b:
                            eng.wait_ge(s_gated_lo, n - UNITS + 1)
                        nc.scalar.copy(ranks[:, 2 * step[2]:2 * step[2] + 2, :],
                                       rank_banks[step[2] % 2]).then_inc(s_ranks_out, 1)
                    elif step[0] == "turn_gates":
                        eng.wait_ge(s_gates_turned, b + 1)
                        if b:
                            eng.wait_ge(s_spread_gates, UNITS * b)
                        nc.scalar.copy(gates_hi[:, :].rearrange("p (t q) -> p t q", q=P),
                                       scores0[0:EXPERTS, 0:2, :]).then_inc(s_gates_hi, 1)
                    elif step[0] == "gated":
                        n = UNITS * b + step[2]
                        eng.wait_ge(s_gated, n + 1)
                        if b and step[2] == 0:
                            eng.wait_ge(s_ring_full, out_at)
                        at = slice(2 * step[2], 2 * step[2] + 2)
                        nc.scalar.copy(gated_hi[:, at, :], ranks[:, at, :]).then_inc(s_gated_hi, 1)
                    elif step[0] == "out":
                        act_ring.take()
                        act_ring.take()
                        out_at = act_ring.n
                    elif step[0] in NORM_STEPS:
                        act_norm(eng, step)

            def pool(eng):
                eng.wait_ge(s_ring_free, attention_tiles[0])
                ones = ranks[0:EXPERTS, EC // 2:EC, :].rearrange("p c d -> p (c d)")
                pool_link(nc.gpsimd.memset(ones, 1.0))
                pool_link(nc.gpsimd.affine_select(out=ones, in_=ones, compare_op=ALU.is_ge, fill=0.0, base=0,
                                                  pattern=[[1, ER]], channel_multiplier=-RANK))
                pool_link(nc.gpsimd.affine_select(out=ones, in_=ones, compare_op=ALU.is_ge, fill=0.0,
                                                  base=RANK - 1, pattern=[[-1, ER]], channel_multiplier=RANK))
                nc.gpsimd.tensor_scalar(spread[:, :], ones, 1.0, 0.0, ALU.mult, ALU.add).then_inc(s_spread, 1)
                for step in expert_steps():
                    if step[0] == "gated":
                        eng.wait_ge(s_gated_hi, UNITS * step[1] + step[2] + 1)
                        at = slice(2 * step[2], 2 * step[2] + 2)
                        nc.gpsimd.tensor_tensor(gated_lo[:, at, :], ranks[:, at, :], as_f32(gated_hi[:, at, :]),
                                                ALU.subtract).then_inc(s_gated_lo, 1)
                    elif step[0] == "scores":
                        pool_ring.up()
                    elif step[0] == "out":
                        pool_ring.up(2)
                    elif step[0] in NORM_STEPS:
                        pool_norm(eng, step)

            def dve(eng):
                for step in expert_steps():
                    b = step[1]
                    if step[0] in ("split_a", "split_b"):
                        raw, hi, lo, _, count = piece(step)
                        eng.wait_ge(s_split_hi, count)
                        nc.vector.tensor_tensor(lo, raw, as_f32(hi), ALU.subtract).then_inc(s_split, 1)
                    elif step[0] == "scores":
                        tile = dve_ring_tile(eng)
                        dve_ring_free(nc.vector.tensor_copy(scores_t[:, :], tile[0:EXPERTS, 0:SEQ]))
                    elif step[0] == "router":
                        router(eng, b)
                    elif step[0] == "turn_gates":
                        eng.wait_ge(s_gates_hi, b + 1)
                        nc.vector.tensor_tensor(gates_lo[:, :].rearrange("p (t q) -> p t q", q=P),
                                                scores0[0:EXPERTS, 0:2, :],
                                                as_f32(gates_hi[:, :]).rearrange("p (t q) -> p t q", q=P),
                                                ALU.subtract).then_inc(s_gates_lo, 1)
                    elif step[0] == "gated":
                        n = UNITS * b + step[2]
                        eng.wait_ge(s_ranks_out, n + 1)
                        eng.wait_ge(s_spread_gates, n + 1)
                        at = slice(2 * step[2], 2 * step[2] + 2)
                        nc.vector.tensor_tensor(ranks[:, at, :], ranks[:, at, :], gate_banks[step[2] % 2],
                                                ALU.mult).then_inc(s_gated, 1)
                    elif step[0] == "out":
                        for t in (2 * b, 2 * b + 1):
                            tile = dve_ring_tile(eng)
                            dve_ring_free(nc.vector.tensor_tensor(x[:, t, :], x[:, t, :], tile, ALU.add))
                    elif step[0] in NORM_STEPS:
                        dve_norm(eng, step)

            def router(eng, b):
                eng.wait_ge(s_turned_scores, b + 1)
                dve_link(nc.vector.tensor_copy(score[:, :, :], turned[:, 0, 0:2, 0:EXPERTS]))
                for t in range(2):
                    ins = nc.vector.max(top[:, t, 0, :], score[:, t, :])
                dve_link(ins)
                nc.vector.tensor_scalar(top_neg[:, :], top[:, :, 0, 0], -1.0, None, ALU.mult).then_inc(s_top, 1)
                for k in range(2):
                    for t in range(2):
                        ins = nc.vector.match_replace(rest[:, t, k, :], top[:, t, k, :],
                                                      rest[:, t, 0, :] if k else score[:, t, :], TAKEN)
                    dve_link(ins)
                    if k == 0:
                        for t in range(2):
                            ins = nc.vector.max(top[:, t, 1, :], rest[:, t, 0, :])
                        dve_link(ins)
                dve_link(nc.vector.tensor_scalar(rest[:, :, 0, :], rest[:, :, 1, :], TAKEN, None, ALU.is_equal))
                eng.wait_ge(s_gate_exp, b + 1)
                dve_link(nc.vector.tensor_tensor(gate[:, :, :], gate[:, :, :], rest[:, :, 0, :], ALU.mult))
                dve_link(nc.vector.tensor_reduce(gsum[:, :], gate[:, :, :], AX.X, ALU.add))
                dve_link(nc.vector.reciprocal(grec[:, :], gsum[:, :]))
                dve_link(nc.vector.tensor_scalar(grec[:, :], grec[:, :], LORA_SCALE, None, ALU.mult))
                nc.vector.tensor_tensor(gate[:, :, :], gate[:, :, :],
                                        grec[:, :].unsqueeze(2).to_broadcast([P, 2, EXPERTS]),
                                        ALU.mult).then_inc(s_gates, 1)

            return pe, act, dve, pool, sp

        TILES = 6
        RAWS = 3
        LV_ACT = 6
        s_code = [sem(f"s_codes{i}") for i in range(RAWS)]
        s_minus7 = sem("s_minus7")
        s_bits = sem("s_bits")
        s_lv_act = sem("s_levels_act")
        s_lv_pool = sem("s_levels_pool")
        s_selected = sem("s_selected")
        s_deq = sem("s_dequantised")
        s_wq_hi = sem("s_wq_hi")
        s_wq = sem("s_wq")
        s_gu = sem("s_gate_up")
        s_silu = sem("s_silu")
        s_h = sem("s_h")
        s_h_hi = sem("s_h_hi")
        s_h_lo = sem("s_h_lo")
        s_dn = sem("s_dn")
        s_added = sem("s_added")
        s_dn_out = sem("s_down_out")
        s_added_odd = sem("s_added_odd")

        def nf4(scope):
            bits = sb("bits", [P, 2, 4, D], I32, scope)
            lv = sb("lv", [P, 2, 8, D], F32, scope)
            deq = sb("deq", [P, TILES, D], F32, scope)
            wq_hi = w_hi[:, :, :, :].rearrange("p t c d -> p t (c d)")
            wq_lo = w_lo[:, :, :, :].rearrange("p t c d -> p t (c d)")
            sg = sb("sg", [P, 2, HALF], F32, scope)
            hf = sb("hf", [P, 2, HALF], F32, scope)
            h_hi = sb("h_hi", [P, 2, TOK], F32R, scope)
            h_lo = sb("h_lo", [P, 2, TOK], F32R, scope)
            minus7 = sb("minus7", [P, 1], F32, scope)
            sb("up_to_the_squares", [P, 31], F32, scope)
            raw = sb("code_raw", [P, RAWS, D], I32, scope)
            am = sb("absmax_rows", [P, RAWS, D], F32, scope)
            steps_of = nf4_steps()
            gu = [(ring[:, 0, :], ring[:, 1, :]),
                  tuple(turned[:, k, :, :].rearrange("p a b -> p (a b)") for k in range(2))]
            dn = [scores1[:, 0:2, :].rearrange("p a b -> p (a b)"), scores1[:, 2:4, :].rearrange("p a b -> p (a b)"),
                  scores0[:, :, :].rearrange("p a b -> p (a b)"), turned[:, 2, :, :].rearrange("p a b -> p (a b)")]
            LAST = MT // 2 - 1

            def plan(i):
                more = not (isinstance(i, int) and i == LAST)

                def unit(u, *his):
                    s = [("unit", u)] + ([("deq", u)] if more or u == 0 else []) + [("silu", u), ("h", u)]
                    return s + [("hi",) + hi for hi in his] + [("h_hi", u), ("h_lo", u)]
                s = unit(0, (5, 0)) + [("lo", 4, 0)] + unit(1) + [("lo", 5, 0)]
                if not more:
                    return s + unit(2) + unit(3) + [("down", 0), ("add", 0), ("down", 1), ("add", 1)]
                s += unit(2, (0, 1)) + [("lo", 0, 1)] + unit(3, (1, 1)) + [("lo", 1, 1)]
                s += [("down", 0), ("deq", 4), ("add", 0), ("hi", 2, 1), ("lo", 2, 1)]
                return s + [("down", 1), ("deq", 5), ("add", 1), ("hi", 3, 1), ("hi", 4, 1), ("lo", 3, 1)]

            lead = norm_begin([3], "pool") + [("deq", 0), ("norm_write", 3, "act"), ("deq", 1), ("norm_turn", 3)]
            lead += [("hi", 0, 1), ("lo", 0, 1)]
            for k in range(2, TILES):
                lead += [("deq", k), ("hi", k - 1, 1)] + ([("lo", k - 1, 1)] if k < TILES - 1 else [])

            def walk(eng, do):
                do(eng, lead, -1)
                do(eng, plan(0), 0)
                with eng.Fori(1, LAST) as i:
                    do(eng, plan(i), i)
                do(eng, plan(LAST), LAST)

            def above(eng, s, v, low=1):
                if not isinstance(v, int) or v >= low:
                    eng.wait_ge(s, v)

            def exists(i, k):
                return not (isinstance(i, int) and i == LAST)

            def sp(eng):
                def load(eng, steps, i):
                    for step in steps:
                        if step[0] == "deq" and exists(i, step[1]):
                            k = step[1]
                            j = TILES * (i + 1) + k
                            m = 2 * (i + 1) + (k // 2 if k < 4 else k - 4)
                            kind = k % 2 if k < 4 else 2
                            above(eng, s_deq, j - RAWS + 1)
                            eng.dma_start(raw[:, k % RAWS, :], codes[m, kind, :, :]).then_inc(s_code[k % RAWS], 16)
                            for side in range(2):
                                eng.dma_start(am[64 * side:64 * side + 64, k % RAWS, :],
                                              absmax[m, kind, side, :].partition_broadcast(64)
                                              ).then_inc(s_code[k % RAWS], 16)
                eng.wait_ge(s_k_ready, 2 * GROUPS)
                walk(eng, load)
                for t in range(NT):
                    eng.wait_ge((s_added, s_added_odd)[t % 2], NT // 2 * LAST + t // 2 + 1)
                    eng.dma_start(out[t * P:(t + 1) * P, :], x[:, t, :]).then_inc(s_out, 16)
                eng.wait_ge(s_out, 16 * NT)

            def act(eng):
                def do(eng, steps, i):
                    for step in steps:
                        if step[0] == "silu":
                            u = 4 * i + step[1]
                            g_bank = gu[step[1] % 2][0]
                            eng.wait_ge(s_gu, 2 * u + 1)
                            above(eng, s_h, u - 1)
                            nc.scalar.activation(sg[:, step[1] % 2, :], g_bank, ACT.Silu).then_inc(s_silu, 1)
                        elif step[0] == "h_hi":
                            u = 4 * i + step[1]
                            eng.wait_ge(s_h, u + 1)
                            mm, half = step[1] % 2, step[1] // 2
                            nc.scalar.copy(h_hi[:, mm, half * HALF:(half + 1) * HALF],
                                           hf[:, step[1] % 2, :]).then_inc(s_h_hi, 1)
                        elif step[0] == "deq" and exists(i, step[1]):
                            k = step[1]
                            j = TILES * (i + 1) + k
                            eng.wait_ge(s_bits, j + 1)
                            above(eng, s_deq, j - 1)
                            for q in range(LV_ACT):
                                low, dist = steps_of[q]
                                nc.scalar.activation(lv[:, k % 2, q, :], bits[:, k % 2, 0, :], ACT.Copy,
                                                           bias=low, scale=dist)
                            nc.scalar.activation(bits[:, k % 2, 3, :], raw[:, k % RAWS, :], ACT.Relu,
                                                 bias=minus7[:, :]).then_inc(s_lv_act, 1)
                        elif step[0] in NORM_STEPS:
                            act_norm(eng, step)
                        elif step[0] == "hi":
                            k, j = step[1], TILES * (i + step[2]) + step[1]
                            eng.wait_ge(s_deq, j + 1)
                            slot_used(eng, i, k, step[2])
                            nc.scalar.copy(wq_hi[:, k, :], deq[:, k, :]).then_inc(s_wq_hi, 1)
                        elif step[0] == "add":
                            for t in (4 * step[1] + 1, 4 * step[1] + 3):
                                eng.wait_ge(s_dn, NT * i + t + 1)
                                above(eng, s_added_odd, NT // 2 * i + t // 2 - 1)
                                nc.scalar.copy(xn[:, t // 2 % 2, :], dn[t % 4]).then_inc(s_dn_out, 1)
                eng.wait_ge(s_minus7, 1)
                walk(eng, do)

            def slot_used(eng, i, k, ahead):
                if k in (0, 1):
                    above(eng, s_gu, 2 * (4 * i + 2) + 2)
                elif k in (2, 3):
                    above(eng, s_gu, 2 * (4 * i + 3) + 2)
                else:
                    above(eng, s_dn, NT * (i + ahead))

            def pool(eng):
                eng.wait_ge(s_ring_free, attention_tiles[1])
                nc.gpsimd.memset(minus7[:, :], -7.0).then_inc(s_minus7, 1)

                def do(eng, steps, i):
                    for step in steps:
                        if step[0] in NORM_STEPS:
                            pool_norm(eng, step)
                        elif step[0] == "h_lo":
                            u = 4 * i + step[1]
                            mm, half = step[1] % 2, step[1] // 2
                            cols = slice(half * HALF, (half + 1) * HALF)
                            eng.wait_ge(s_h_hi, u + 1)
                            nc.gpsimd.tensor_tensor(h_lo[:, mm, cols], hf[:, step[1] % 2, :],
                                                    as_f32(h_hi[:, mm, cols]), ALU.subtract).then_inc(s_h_lo, 1)
                        elif step[0] == "deq":
                            k = step[1]
                            j = TILES * (i + 1) + k
                            if exists(i, k):
                                eng.wait_ge(s_bits, j + 1)
                                above(eng, s_deq, j - 1)
                                hold(nc.gpsimd)
                                for q in range(LV_ACT, 8):
                                    low, dist = steps_of[q]
                                    ins = nc.gpsimd.tensor_scalar(lv[:, k % 2, q, :], bits[:, k % 2, 0, :], dist,
                                                                  low, ALU.mult, ALU.add)
                                ins.then_inc(s_lv_pool, 1)
                            if not (isinstance(j, int) and j == 0):
                                eng.wait_ge(s_selected, j)
                                above(eng, s_wq, j - TILES)
                                nc.gpsimd.tensor_tensor(deq[:, (k - 1) % TILES, :], lv[:, (k - 1) % 2, 0, :],
                                                        am[:, (k - 1) % RAWS, :], ALU.mult).then_inc(s_deq, 1)
                        elif step[0] == "lo":
                            k, j = step[1], TILES * (i + step[2]) + step[1]
                            eng.wait_ge(s_wq_hi, j + 1)
                            nc.gpsimd.tensor_tensor(wq_lo[:, k, :], deq[:, k, :], as_f32(wq_hi[:, k, :]),
                                                    ALU.subtract).then_inc(s_wq, 1)
                        elif step[0] == "add":
                            for t in (4 * step[1] + 1, 4 * step[1] + 3):
                                eng.wait_ge(s_dn_out, NT // 2 * i + t // 2 + 1)
                                nc.gpsimd.tensor_tensor(x[:, t, :], x[:, t, :], xn[:, t // 2 % 2, :],
                                                        ALU.add).then_inc(s_added_odd, 1)
                walk(eng, do)

            def dve(eng):
                chain = dve_chain

                def do(eng, steps, i):
                    for step in steps:
                        if step[0] in NORM_STEPS:
                            dve_norm(eng, step)
                        elif step[0] == "h":
                            u = 4 * i + step[1]
                            eng.wait_ge(s_silu, u + 1)
                            eng.wait_ge(s_gu, 2 * u + 2)
                            above(eng, s_h_lo, u - 1)
                            nc.vector.tensor_tensor(hf[:, step[1] % 2, :], sg[:, step[1] % 2, :],
                                                    gu[step[1] % 2][1], ALU.mult).then_inc(s_h, 1)
                        elif step[0] == "deq":
                            k = step[1]
                            j = TILES * (i + 1) + k
                            def bit(b):
                                if exists(i, k):
                                    return nc.vector.tensor_scalar(bits[:, k % 2, b, :], raw[:, k % RAWS, :],
                                                                   1 << b, None, ALU.bitwise_and)
                            if exists(i, k):
                                eng.wait_ge(s_code[k % RAWS], 48 * (2 * (i + 1) + k // RAWS + 1))
                                bit(0).then_inc(s_bits, 1)
                            if isinstance(j, int) and j == 0:
                                bit(1)
                                dve_link(bit(2))
                            else:
                                select(eng, j - 1, k - 1, bit)
                        elif step[0] == "add":
                            for t in (4 * step[1], 4 * step[1] + 2):
                                eng.wait_ge(s_dn, NT * i + t + 1)
                                nc.vector.tensor_tensor(x[:, t, :], x[:, t, :], dn[t % 4], ALU.add).then_inc(s_added, 1)

                def select(eng, j, k, bit):
                    par = k % 2
                    above(eng, s_selected, j)
                    eng.wait_ge(s_lv_act, j + 1)
                    eng.wait_ge(s_lv_pool, j + 1)
                    hold(nc.vector)
                    for b, (into, other) in ((1, (lv[:, par, 0::2, :], lv[:, par, 1::2, :])),
                                             (2, (lv[:, par, 0::4, :], lv[:, par, 2::4, :])),
                                             (3, (lv[:, par, 0:1, :], lv[:, par, 4:5, :]))):
                        ins = nc.vector.copy_predicated(
                            into, bits[:, par, b, :].unsqueeze(1).to_broadcast([P, 8 >> b, D]), other)
                        if b < 3:
                            ins.then_inc(s_dve, 1)
                            chain.up()
                            bit(b)
                            eng.wait_ge(s_dve, chain.value())
                            hold(nc.vector)
                    ins.then_inc(s_selected, 1)

                do(eng, lead, -1)
                do(eng, plan(0), 0)
                turn_loop(eng, LAST - 1, [(dve_chain, 2 * TILES)], lambda i: do(eng, plan(i + 1), i + 1))
                do(eng, plan(LAST), LAST)

            def pe(eng):
                pe_norm_turn(eng, 3)
                eng.wait_ge(s_ring_free, pe_ring.value())

                def do(eng, steps, i):
                    for step in steps:
                        if step[0] == "unit":
                            k = step[1]
                            u, mm, half = 4 * i + k, k % 2, k // 2
                            cols = slice(half * HALF, (half + 1) * HALF)
                            above(eng, s_h, u - 1)
                            for kind in range(2):
                                w = 2 * mm + kind
                                if half == 0:
                                    eng.wait_ge(s_wq, TILES * i + w + 1)
                                for c in range(DC):
                                    at = slice(c * P, (c + 1) * P)
                                    ins = mm3(gu[k % 2][kind], wq_hi[:, w, at], wq_lo[:, w, at], xt_hi[:, c, cols],
                                              xt_lo[:, c, cols], start=c == 0, stop=c == DC - 1)
                                ins.then_inc(s_gu, 1)
                        elif step[0] == "down":
                            eng.wait_ge(s_h_lo, 4 * i + 2 * step[1] + 2)
                            if step[1] == 0:
                                eng.wait_ge(s_wq, TILES * i + TILES)
                            for t in range(4 * step[1], 4 * step[1] + 4):
                                above(eng, (s_added, s_dn_out)[t % 2], NT // 2 * i + t // 2 - 1)
                                for mm in range(2):
                                    at = slice(t * P, (t + 1) * P)
                                    ins = mm3(dn[t % 4], h_hi[:, mm, at], h_lo[:, mm, at], wq_hi[:, 4 + mm, :],
                                              wq_lo[:, 4 + mm, :], start=mm == 0, stop=mm == 1)
                                ins.then_inc(s_dn, 1)
                do(eng, plan(0), 0)
                with eng.Fori(1, LAST) as i:
                    do(eng, plan(i), i)
                do(eng, plan(LAST), LAST)

            return pe, act, dve, pool, sp

        attention_tiles = [0, 0]
        attention_starts = [0, 0]
        last_slots = [0, 0]
        a_scope, b_scope, c_scope, d_scope = ExitStack(), ExitStack(), ExitStack(), ExitStack()
        with a_scope:
            pe_a, act_a, dve_a, pool_a, sp_a = attention(0, a_scope)
        with b_scope:
            pe_b, act_b, dve_b, pool_b, sp_b = experts(b_scope)
        with c_scope:
            pe_c, act_c, dve_c, pool_c, sp_c = attention(1, c_scope)
        with d_scope:
            pe_d, act_d, dve_d, pool_d, sp_d = nf4(d_scope)

        block = ctx.enter_context(nc.Block())

        @block.tensor
        def _(pe):
            pe.wait_ge(s_ident, 2)
            pe_a(pe)
            attention_tiles[0] = pe_ring.n
            pe_b(pe)
            attention_starts[1] = pe_ring.n
            pe.wait_ge(s_const, 1)
            pe_c(pe)
            attention_tiles[1] = pe_ring.n
            pe_d(pe)

        @block.scalar
        def _(act):
            act_a(act)
            act_b(act)
            act_c(act)
            act_d(act)

        @block.vector
        def _(dve):
            dve.wait_ge(s_ident, 2)
            dve_a(dve)
            dve_b(dve)
            dve.wait_ge(s_norm_w, 32)
            dve_link(nc.vector.tensor_scalar(norm_cols[:, 2:3], norm_cols[:, 0:1], norm_cols[:, 1:2], SCALE,
                                             ALU.mult, ALU.mult))
            dve.wait_ge(s_const, 2)
            dve_c(dve)
            dve_d(dve)

        @block.gpsimd
        def _(pool):
            pool_link(nc.gpsimd.memset(ident[:, :], 0.0))
            pool_link(nc.gpsimd.memset(tri[:, :], 0.0))
            nc.gpsimd.affine_select(out=ident[:, :], in_=ident[:, :], compare_op=ALU.not_equal, fill=1.0,
                                    base=0, pattern=[[-1, P]], channel_multiplier=1).then_inc(s_ident, 1)
            nc.gpsimd.affine_select(out=tri[:, :], in_=tri[:, :], compare_op=ALU.is_ge, fill=MASKED,
                                    base=0, pattern=[[-1, P]], channel_multiplier=1).then_inc(s_ident, 1)
            pool_a(pool)
            pool_link(nc.gpsimd.memset(rel[:, 0:2 * P], 0.0))
            pool_link(nc.gpsimd.memset(rel[:, P:P + 1], 1.0))
            nc.gpsimd.tensor_scalar(pick[:, :], rel[:, 0:2 * P], 1.0, 0.0, ALU.mult, ALU.add).then_inc(s_const, 1)
            for i, slope in enumerate(alibi_slopes()):
                nc.gpsimd.memset(slopes[:, i:i + 1], slope)
            pool.wait_ge(s_const, 1)
            for base, cols in ((0, slice(0, P)), (-P, slice(P, P + SEQ))):
                part = rel[:, cols]
                width = cols.stop - cols.start
                pool_link(nc.gpsimd.iota(part, pattern=[[1, width]], base=base, channel_multiplier=-1,
                                         allow_small_or_imprecise_dtypes=True))
                last = nc.gpsimd.affine_select(out=part, in_=part, compare_op=ALU.is_ge, fill=MASKED,
                                               base=-base, pattern=[[-1, width]], channel_multiplier=1)
                if base == 0:
                    pool_link(last)
            last.then_inc(s_const, 1)
            pool_b(pool)
            pool_c(pool)
            pool_d(pool)

        @block.sync
        def _(sp):
            for t in range(NT):
                sp.dma_start(x[:, t, :], x_in[t * P:(t + 1) * P, :]).then_inc(s_x[t], 16)
            for i in range(2):
                sp.dma_start(norm_cols[:, i:i + 1], norm_w[i, :].rearrange("(p a) -> p a", a=1)).then_inc(s_norm_w, 16)
            sp_a(sp)
            sp_b(sp)
            sp_c(sp)
            sp_d(sp)


def kernel(L0_attn_q, L0_attn_w_qkv, L0_attn_w_dense, L0_ffn_A, L0_ffn_B, L0_ffn_Wr, L1_attn_Wq, L1_attn_Wk,
           L1_attn_Wv, L1_attn_Wo, L1_attn_q_norm_w, L1_attn_k_norm_w, L1_ffn_gate_q, L1_ffn_gate_absmax,
           L1_ffn_up_q, L1_ffn_up_absmax, L1_ffn_down_q, L1_ffn_down_absmax):
    import concourse.bacc as bacc
    from concourse.bass_utils import run_bass_kernel_spmd

    def attn_tiles(wq, wk, wv):
        q = np.asarray(wq).reshape(GROUPS, HEADS, HD, DC, P)
        k = np.asarray(wk).reshape(GROUPS, 1, HD, DC, P)
        v = np.asarray(wv).reshape(GROUPS, 1, HD, DC, P)
        tiles = np.concatenate([k, q, v], axis=1)
        return tiles.transpose(0, 1, 4, 3, 2).reshape(GROUPS, WT, P, DC * HD)

    def by_chunk(w):
        return np.asarray(w).T.reshape(DC, P, -1).transpose(1, 0, 2)

    def hidden_in(q):
        return np.asarray(q).reshape(MT, P, DC, P).transpose(0, 3, 2, 1).reshape(MT, P, D)

    def hidden_in_absmax(a):
        return np.asarray(a).reshape(MT, P, DC, 2).transpose(0, 3, 2, 1).reshape(MT, 2, D)

    qkv, nq, nk = np.asarray(L0_attn_w_qkv), GROUPS * HEADS * HD, GROUPS * HD
    arrays = {
        "x_in": np.asarray(L0_attn_q).reshape(TOK, D),
        "w_attn": np.concatenate([attn_tiles(qkv[:nq], qkv[nq:nq + nk], qkv[nq + nk:]),
                                  attn_tiles(L1_attn_Wq, L1_attn_Wk, L1_attn_Wv)]),
        "w_dense": np.concatenate([np.asarray(w).T.reshape(GROUPS, HEADS, HD, D)
                                   for w in (L0_attn_w_dense, L1_attn_Wo)]),
        "lora_a": by_chunk(np.asarray(L0_ffn_A).reshape(ER, D)),
        "lora_wr": by_chunk(L0_ffn_Wr),
        "lora_b": np.asarray(L0_ffn_B).transpose(0, 2, 1).reshape(EC, P, D).transpose(1, 0, 2),
        "norm_w": np.stack([np.asarray(L1_attn_q_norm_w), np.asarray(L1_attn_k_norm_w)]),
        "codes": np.stack([hidden_in(L1_ffn_gate_q), hidden_in(L1_ffn_up_q),
                           np.asarray(L1_ffn_down_q).T.reshape(MT, P, D)], axis=1),
        "absmax": np.stack([hidden_in_absmax(L1_ffn_gate_absmax), hidden_in_absmax(L1_ffn_up_absmax),
                            np.asarray(L1_ffn_down_absmax).reshape(D, MT, 2).transpose(1, 2, 0)], axis=1),
    }
    nc = bacc.Bacc("TRN2", target_bir_lowering=False, num_devices=1)
    arrays = {f"{n}_dram": np.ascontiguousarray(a) for n, a in arrays.items()}
    args = {n[:-5]: nc.dram_tensor(n, a.shape, mybir.dt.from_np(a.dtype), kind="ExternalInput").ap()
            for n, a in arrays.items()}
    out = nc.dram_tensor("out_dram", (TOK, D), F32, kind="ExternalOutput").ap()
    build(nc, out=out, **args)
    r = run_bass_kernel_spmd(nc, [arrays], core_ids=[0])
    return r.results[0]["out_dram"].reshape(BATCH, SEQ, D)
```
